# Optimizing a Trainium2 kernel written in Bass

```python
import numpy as np
import jax
import jax.numpy as jnp

def _softmax(x, axis=-1):
    return jax.nn.softmax(x, axis=axis)

def _gelu(x):
    return jax.nn.gelu(x, approximate=True)

def _silu(x):
    return jax.nn.silu(x)

def _sigmoid(x):
    return jax.nn.sigmoid(x)

def _layernorm(x, axis=-1, eps=1e-05):
    m = jnp.mean(x, axis=axis, keepdims=True)
    v = jnp.var(x, axis=axis, keepdims=True)
    return (x - m) / jnp.sqrt(v + eps)

def _scatter_add(tgt, idx, src, axis=0):
    return tgt.at[idx].add(src)

def _segment_sum(src, seg, n):
    return jax.ops.segment_sum(src, seg, n)
kernel_name = 'mk_xattn_ffn_d4_seqx_r8_d50112'

def setup_inputs(seed: int=0):
    np.random.seed(seed)
    _w = jnp.asarray

    def _rec_inputs():
        import jax
        import jax.numpy as jnp
        _rk = jax.random.key(seed)
        x = -0.0002928 + 1 * jax.random.normal(jax.random.fold_in(_rk, 1), (2, 512, 128), jnp.float32)
        _lenS = 512 - jax.random.randint(jax.random.fold_in(_rk, 7), (2,), 0, max(1, 512 // 4) + 1, jnp.int32)
        _lenS2 = 77 - jax.random.randint(jax.random.fold_in(_rk, 8), (2,), 0, max(1, 77 // 4) + 1, jnp.int32)
        _ctx_1024P = jax.random.normal(jax.random.fold_in(_rk, 11), (2, 16, 128), jnp.float32)
        _ctx_1024c = jax.random.dirichlet(jax.random.fold_in(_rk, 511), 0.3 * jnp.ones((16,), jnp.float32), (2, 77))
        _ctx_1024t = jnp.einsum('bsk,bkd->bsd', _ctx_1024c, _ctx_1024P)
        _ctx_1024t = _ctx_1024t * jax.lax.rsqrt(jnp.mean(jnp.square(_ctx_1024t)) + 1e-12) * 0.953939
        ctx_1024 = 4.13588e-05 + 0.999923 * (_ctx_1024t + 0.3 * jax.random.normal(jax.random.fold_in(_rk, 611), (2, 77, 128), jnp.float32))
        _validS = jnp.arange(512)[None, :] < _lenS[:, None]
        _validS2 = jnp.arange(77)[None, :] < _lenS2[:, None]
        _causal = jnp.tril(jnp.ones((512, 512), dtype=bool))
        mask_BxS2_ik0 = jnp.where(jnp.broadcast_to(_validS2[:, :], (2, 77)), 0, 1).astype(jnp.int32)
        return (x, ctx_1024, mask_BxS2_ik0)
    x, ctx_1024, mask_BxS2_ik0 = _rec_inputs()

    def _L0_xattn_setup():
        import jax, jax.numpy as jnp
        import numpy as np
        HEADS = 16
        DIM_Q = 128
        DIM_KV = 128
        INNER = 128
        key = jax.random.key(seed)
        k1, k2, k3, k4, k5, k6, k7 = jax.random.split(key, 7)
        B, Lq, Lkv = (2, 256, 512)
        H = jax.random.normal(k1, (B, Lq, DIM_Q), dtype=jnp.float32)
        T = jax.random.normal(k2, (B, Lkv, DIM_KV), dtype=jnp.float32)
        mask = jax.random.randint(k3, (B, Lkv), 0, 2, dtype=jnp.int32)
        s = 0.02
        Wq = jax.random.normal(k4, (DIM_Q, INNER), dtype=jnp.float32) * s
        Wk = jax.random.normal(k5, (DIM_KV, INNER), dtype=jnp.float32) * s
        Wv = jax.random.normal(k6, (DIM_KV, INNER), dtype=jnp.float32) * s
        Wo = jax.random.normal(k7, (INNER, DIM_Q), dtype=jnp.float32) * s
        return {'H': H, 'T': T, 'mask': mask, 'Wq': Wq, 'Wk': Wk, 'Wv': Wv, 'Wo': Wo}
    _L0_xattn_all = _L0_xattn_setup()
    _L0_xattn_in = {k: v for k, v in _L0_xattn_all.items() if k in ('Wq', 'Wk', 'Wv', 'Wo')}
    del _L0_xattn_all

    def _L0_ffn_setup():
        import math
        import jax, jax.numpy as jnp
        import numpy as np
        B, S, D, H, E, F = (2, 128, 128, 16, 16, 512)
        HEAD = D // H
        MOE_TOKEN_DROPOUT = 0.2
        EPS = 1e-05

        def layer_norm(x, w, b):
            mu = x.mean(-1, keepdims=True)
            var = ((x - mu) ** 2).mean(-1, keepdims=True)
            return (x - mu) * jax.lax.rsqrt(var + EPS) * w + b
        key = jax.random.key(seed)
        ks = jax.random.split(key, 16)
        w = lambda k, shape: jax.random.normal(k, shape, jnp.float32) * 0.02
        return {'hidden_states': jax.random.normal(ks[0], (B, S, D), jnp.float32), 'ln1_w': jnp.ones((D,), jnp.float32), 'ln1_b': jnp.zeros((D,), jnp.float32), 'q_w': w(ks[1], (D, D)), 'q_b': jnp.zeros((D,), jnp.float32), 'k_w': w(ks[2], (D, D)), 'k_b': jnp.zeros((D,), jnp.float32), 'v_w': w(ks[3], (D, D)), 'v_b': jnp.zeros((D,), jnp.float32), 'o_w': w(ks[4], (D, D)), 'o_b': jnp.zeros((D,), jnp.float32), 'ln2_w': jnp.ones((D,), jnp.float32), 'ln2_b': jnp.zeros((D,), jnp.float32), 'router_w': w(ks[5], (D, E)), 'fc1_w': w(ks[6], (E, D, F)), 'fc1_b': jnp.zeros((E, F), jnp.float32), 'fc2_w': w(ks[7], (E, F, D)), 'fc2_b': jnp.zeros((E, D), jnp.float32)}
    _L0_ffn_all = _L0_ffn_setup()
    _L0_ffn_in = {k: v for k, v in _L0_ffn_all.items() if k in ('ln1_w', 'ln1_b', 'q_w', 'q_b', 'k_w', 'k_b', 'v_w', 'v_b', 'o_w', 'o_b', 'ln2_w', 'ln2_b', 'router_w', 'fc1_w', 'fc1_b', 'fc2_w', 'fc2_b')}
    del _L0_ffn_all

    def _L1_xattn_setup():
        import jax, jax.numpy as jnp
        import numpy as np
        DIM = 128
        NUM_HEADS = 8
        HEAD_DIM = 64
        INNER = NUM_HEADS * HEAD_DIM
        key = jax.random.key(seed)
        ks = jax.random.split(key, 7)
        B, N, M = (8, 64, 512)
        x = jax.random.normal(ks[0], (B, N, DIM), dtype=jnp.float32)
        context = jax.random.normal(ks[1], (B, M, DIM), dtype=jnp.float32)
        s_in = 1.0 / np.sqrt(DIM)
        s_inner = 1.0 / np.sqrt(INNER)
        Wq = jax.random.normal(ks[2], (DIM, INNER), dtype=jnp.float32) * s_in
        Wk = jax.random.normal(ks[3], (DIM, INNER), dtype=jnp.float32) * s_in
        Wv = jax.random.normal(ks[4], (DIM, INNER), dtype=jnp.float32) * s_in
        Wo = jax.random.normal(ks[5], (INNER, DIM), dtype=jnp.float32) * s_inner
        bo = jax.random.normal(ks[6], (DIM,), dtype=jnp.float32) * 0.01
        return {'x': x, 'context': context, 'Wq': Wq, 'Wk': Wk, 'Wv': Wv, 'Wo': Wo, 'bo': bo}
    _L1_xattn_all = _L1_xattn_setup()
    _L1_xattn_in = {k: v for k, v in _L1_xattn_all.items() if k in ('Wq', 'Wk', 'Wv', 'Wo', 'bo')}
    del _L1_xattn_all

    def _L1_ffn_setup():
        import jax, jax.numpy as jnp
        import numpy as np
        D = 128
        H = 4
        DF = 512
        E = 8
        EPS = 1e-05

        def _layer_norm(x, g, b):
            mu = jnp.mean(x, axis=-1, keepdims=True)
            var = jnp.mean(jnp.square(x - mu), axis=-1, keepdims=True)
            return (x - mu) * jax.lax.rsqrt(var + EPS) * g + b

        def _mha(x, Wqkv, bqkv, Wo, bo):
            S, B, _ = x.shape
            hd = D // H
            qkv = x @ Wqkv.T + bqkv
            q, k, v = jnp.split(qkv, 3, axis=-1)
            to_heads = lambda t: t.reshape(S, B, H, hd).transpose(1, 2, 0, 3)
            q, k, v = (to_heads(q), to_heads(k), to_heads(v))
            scores = jnp.einsum('bhqd,bhkd->bhqk', q, k) * (1.0 / np.sqrt(hd))
            att = jax.nn.softmax(scores, axis=-1)
            o = jnp.einsum('bhqk,bhkd->bhqd', att, v)
            o = o.transpose(2, 0, 1, 3).reshape(S, B, D)
            return o @ Wo.T + bo

        def _moe(x, Wg, W1, b1, W2, b2):
            S, B, _ = x.shape
            xf = x.reshape(S * B, D)
            logits = xf @ Wg.T
            idx = jnp.argmax(logits, axis=-1)
            out = jnp.zeros_like(xf)
            for e in range(E):
                m = (idx == e)[:, None].astype(xf.dtype)
                h = jax.nn.relu(xf @ W1[e] + b1[e])
                out = out + m * (h @ W2[e] + b2[e])
            return out.reshape(S, B, D)
        key = jax.random.key(seed)
        ks = jax.random.split(key, 16)
        S, B = (64, 8)
        s = lambda k, shape, fan: jax.random.normal(k, shape, jnp.float32) * (1.0 / np.sqrt(fan))
        return {'x': jax.random.normal(ks[0], (S, B, D), jnp.float32), 'Wqkv': s(ks[1], (3 * D, D), D), 'bqkv': jnp.zeros((3 * D,), jnp.float32), 'Wo': s(ks[2], (D, D), D), 'bo': jnp.zeros((D,), jnp.float32), 'g1': jnp.ones((D,), jnp.float32), 'be1': jnp.zeros((D,), jnp.float32), 'g2': jnp.ones((D,), jnp.float32), 'be2': jnp.zeros((D,), jnp.float32), 'Wg': s(ks[3], (E, D), D), 'W1': s(ks[4], (E, D, DF), D), 'b1': jnp.zeros((E, DF), jnp.float32), 'W2': s(ks[5], (E, DF, D), DF), 'b2': jnp.zeros((E, D), jnp.float32)}
    _L1_ffn_all = _L1_ffn_setup()
    _L1_ffn_in = {k: v for k, v in _L1_ffn_all.items() if k in ('Wqkv', 'bqkv', 'Wo', 'bo', 'g1', 'be1', 'g2', 'be2', 'Wg', 'W1', 'b1', 'W2', 'b2')}
    del _L1_ffn_all

    def _L2_xattn_setup():
        import jax, jax.numpy as jnp
        import numpy as np
        N_HEADS = 16
        KQ_DIM = 64
        EMB_DIM = 128
        CTX_DIM = 128
        EPS = 1e-05

        def _layernorm(x, w, b):
            mu = jnp.mean(x, axis=-1, keepdims=True)
            var = jnp.mean(jnp.square(x - mu), axis=-1, keepdims=True)
            return (x - mu) * jax.lax.rsqrt(var + EPS) * w + b
        key = jax.random.key(seed)
        ks = jax.random.split(key, 10)
        B, SQ, SK = (2, 256, 256)
        inner = N_HEADS * KQ_DIM
        s_e = 1.0 / np.sqrt(EMB_DIM)
        s_c = 1.0 / np.sqrt(CTX_DIM)
        s_i = 1.0 / np.sqrt(inner)
        return {'emb': jax.random.normal(ks[0], (B, SQ, EMB_DIM), jnp.float32), 'context': jax.random.normal(ks[1], (B, SK, CTX_DIM), jnp.float32), 'Wq': jax.random.uniform(ks[2], (inner, EMB_DIM), jnp.float32, -s_e, s_e), 'Wk': jax.random.uniform(ks[3], (inner, CTX_DIM), jnp.float32, -s_c, s_c), 'Wv': jax.random.uniform(ks[4], (inner, CTX_DIM), jnp.float32, -s_c, s_c), 'Wu': jax.random.uniform(ks[5], (EMB_DIM, inner), jnp.float32, -s_i, s_i), 'bu': jax.random.uniform(ks[6], (EMB_DIM,), jnp.float32, -s_i, s_i), 'qn_w': jnp.ones((KQ_DIM,), jnp.float32), 'qn_b': jnp.zeros((KQ_DIM,), jnp.float32), 'kn_w': jnp.ones((KQ_DIM,), jnp.float32), 'kn_b': jnp.zeros((KQ_DIM,), jnp.float32)}
    _L2_xattn_all = _L2_xattn_setup()
    _L2_xattn_in = {k: v for k, v in _L2_xattn_all.items() if k in ('Wq', 'Wk', 'Wv', 'Wu', 'bu', 'qn_w', 'qn_b', 'kn_w', 'kn_b')}
    del _L2_xattn_all

    def _L2_ffn_setup():
        import jax, jax.numpy as jnp
        import numpy as np
        D_MODEL = 128
        N_HEADS = 16
        D_HEAD = D_MODEL // N_HEADS
        N_EXPERTS = 8
        TOP_K = 2
        D_FF = 256
        EPS = 1e-06

        def rmsnorm(x, w):
            return x * jax.lax.rsqrt(jnp.mean(x * x, axis=-1, keepdims=True) + EPS) * w

        def swiglu(x, w_gate, w_up, w_down):
            return jax.nn.silu(x @ w_gate) * (x @ w_up) @ w_down
        key = jax.random.key(seed)
        ks = jax.random.split(key, 16)
        s = 0.02
        B, S = (2, 256)
        return {'X': jax.random.normal(ks[0], (B, S, D_MODEL), dtype=jnp.float32), 'norm1_w': jnp.ones((D_MODEL,), jnp.float32), 'norm2_w': jnp.ones((D_MODEL,), jnp.float32), 'wq': jax.random.normal(ks[1], (D_MODEL, D_MODEL), jnp.float32) * s, 'wk': jax.random.normal(ks[2], (D_MODEL, D_MODEL), jnp.float32) * s, 'wv': jax.random.normal(ks[3], (D_MODEL, D_MODEL), jnp.float32) * s, 'wo': jax.random.normal(ks[4], (D_MODEL, D_MODEL), jnp.float32) * s, 'router_w': jax.random.normal(ks[5], (D_MODEL, N_EXPERTS), jnp.float32) * s, 'sh_gate': jax.random.normal(ks[6], (D_MODEL, D_FF), jnp.float32) * s, 'sh_up': jax.random.normal(ks[7], (D_MODEL, D_FF), jnp.float32) * s, 'sh_down': jax.random.normal(ks[8], (D_FF, D_MODEL), jnp.float32) * s, 'e_gate': jax.random.normal(ks[9], (N_EXPERTS, D_MODEL, D_FF), jnp.float32) * s, 'e_up': jax.random.normal(ks[10], (N_EXPERTS, D_MODEL, D_FF), jnp.float32) * s, 'e_down': jax.random.normal(ks[11], (N_EXPERTS, D_FF, D_MODEL), jnp.float32) * s}
    _L2_ffn_all = _L2_ffn_setup()
    _L2_ffn_in = {k: v for k, v in _L2_ffn_all.items() if k in ('norm1_w', 'norm2_w', 'wq', 'wk', 'wv', 'wo', 'router_w', 'sh_gate', 'sh_up', 'sh_down', 'e_gate', 'e_up', 'e_down')}
    del _L2_ffn_all

    def _L3_xattn_setup():
        import jax, jax.numpy as jnp
        import numpy as np
        HEADS = 16
        DIM_HEAD = 64
        QUERY_DIM = 128
        CONTEXT_DIM = 128
        INNER = HEADS * DIM_HEAD
        key = jax.random.key(seed)
        k1, k2, k3, k4, k5, k6, k7 = jax.random.split(key, 7)
        B, N, M = (4, 256, 256)
        s = 0.02
        return {'x': jax.random.normal(k1, (B, N, QUERY_DIM), jnp.float32), 'context': jax.random.normal(k2, (B, M, CONTEXT_DIM), jnp.float32), 'Wq': jax.random.normal(k3, (INNER, QUERY_DIM), jnp.float32) * s, 'Wk': jax.random.normal(k4, (INNER, CONTEXT_DIM), jnp.float32) * s, 'Wv': jax.random.normal(k5, (INNER, CONTEXT_DIM), jnp.float32) * s, 'Wo': jax.random.normal(k6, (QUERY_DIM, INNER), jnp.float32) * s, 'bo': jax.random.normal(k7, (QUERY_DIM,), jnp.float32) * s}
    _L3_xattn_all = _L3_xattn_setup()
    _L3_xattn_in = {k: v for k, v in _L3_xattn_all.items() if k in ('Wq', 'Wk', 'Wv', 'Wo', 'bo')}
    del _L3_xattn_all

    def _L3_ffn_setup():
        import jax, jax.numpy as jnp
        import numpy as np
        B, S, D, H, E = (4, 256, 128, 512, 8)
        EPS = 1e-12

        def _wn(v, g):
            n = jnp.sqrt(jnp.sum(v * v, axis=-1, keepdims=True))
            return v / jnp.maximum(n, EPS) * g[:, None]
        key = jax.random.key(seed)
        ks = jax.random.split(key, 8)
        return {'x': jax.random.normal(ks[0], (B, S, D), dtype=jnp.float32), 'gate_v': jax.random.normal(ks[1], (E, D), dtype=jnp.float32), 'gate_g': jnp.ones((E,), dtype=jnp.float32), 'gate_b': jnp.zeros((E,), dtype=jnp.float32), 'w1_v': jax.random.normal(ks[2], (E, H, D), dtype=jnp.float32), 'w1_g': jnp.ones((E, H), dtype=jnp.float32), 'b1': jnp.zeros((E, H), dtype=jnp.float32), 'w2_v': jax.random.normal(ks[3], (E, D, H), dtype=jnp.float32), 'w2_g': jnp.ones((E, D), dtype=jnp.float32), 'b2': jnp.zeros((E, D), dtype=jnp.float32)}
    _L3_ffn_all = _L3_ffn_setup()
    _L3_ffn_in = {k: v for k, v in _L3_ffn_all.items() if k in ('gate_v', 'gate_g', 'gate_b', 'w1_v', 'w1_g', 'b1', 'w2_v', 'w2_g', 'b2')}
    del _L3_ffn_all
    return {'x': x, 'ctx_1024': ctx_1024, 'mask_BxS2_ik0': mask_BxS2_ik0, 'L0_xattn_Wq': _L0_xattn_in['Wq'], 'L0_xattn_Wk': _L0_xattn_in['Wk'], 'L0_xattn_Wv': _L0_xattn_in['Wv'], 'L0_xattn_Wo': _L0_xattn_in['Wo'], 'L0_ffn_ln1_w': _L0_ffn_in['ln1_w'], 'L0_ffn_ln1_b': _L0_ffn_in['ln1_b'], 'L0_ffn_q_w': _L0_ffn_in['q_w'], 'L0_ffn_q_b': _L0_ffn_in['q_b'], 'L0_ffn_k_w': _L0_ffn_in['k_w'], 'L0_ffn_k_b': _L0_ffn_in['k_b'], 'L0_ffn_v_w': _L0_ffn_in['v_w'], 'L0_ffn_v_b': _L0_ffn_in['v_b'], 'L0_ffn_o_w': _L0_ffn_in['o_w'], 'L0_ffn_o_b': _L0_ffn_in['o_b'], 'L0_ffn_ln2_w': _L0_ffn_in['ln2_w'], 'L0_ffn_ln2_b': _L0_ffn_in['ln2_b'], 'L0_ffn_router_w': _L0_ffn_in['router_w'], 'L0_ffn_fc1_w': _L0_ffn_in['fc1_w'], 'L0_ffn_fc1_b': _L0_ffn_in['fc1_b'], 'L0_ffn_fc2_w': _L0_ffn_in['fc2_w'], 'L0_ffn_fc2_b': _L0_ffn_in['fc2_b'], 'L1_xattn_Wq': _L1_xattn_in['Wq'], 'L1_xattn_Wk': _L1_xattn_in['Wk'], 'L1_xattn_Wv': _L1_xattn_in['Wv'], 'L1_xattn_Wo': _L1_xattn_in['Wo'], 'L1_xattn_bo': _L1_xattn_in['bo'], 'L1_ffn_Wqkv': _L1_ffn_in['Wqkv'], 'L1_ffn_bqkv': _L1_ffn_in['bqkv'], 'L1_ffn_Wo': _L1_ffn_in['Wo'], 'L1_ffn_bo': _L1_ffn_in['bo'], 'L1_ffn_g1': _L1_ffn_in['g1'], 'L1_ffn_be1': _L1_ffn_in['be1'], 'L1_ffn_g2': _L1_ffn_in['g2'], 'L1_ffn_be2': _L1_ffn_in['be2'], 'L1_ffn_Wg': _L1_ffn_in['Wg'], 'L1_ffn_W1': _L1_ffn_in['W1'], 'L1_ffn_b1': _L1_ffn_in['b1'], 'L1_ffn_W2': _L1_ffn_in['W2'], 'L1_ffn_b2': _L1_ffn_in['b2'], 'L2_xattn_Wq': _L2_xattn_in['Wq'], 'L2_xattn_Wk': _L2_xattn_in['Wk'], 'L2_xattn_Wv': _L2_xattn_in['Wv'], 'L2_xattn_Wu': _L2_xattn_in['Wu'], 'L2_xattn_bu': _L2_xattn_in['bu'], 'L2_xattn_qn_w': _L2_xattn_in['qn_w'], 'L2_xattn_qn_b': _L2_xattn_in['qn_b'], 'L2_xattn_kn_w': _L2_xattn_in['kn_w'], 'L2_xattn_kn_b': _L2_xattn_in['kn_b'], 'L2_ffn_norm1_w': _L2_ffn_in['norm1_w'], 'L2_ffn_norm2_w': _L2_ffn_in['norm2_w'], 'L2_ffn_wq': _L2_ffn_in['wq'], 'L2_ffn_wk': _L2_ffn_in['wk'], 'L2_ffn_wv': _L2_ffn_in['wv'], 'L2_ffn_wo': _L2_ffn_in['wo'], 'L2_ffn_router_w': _L2_ffn_in['router_w'], 'L2_ffn_sh_gate': _L2_ffn_in['sh_gate'], 'L2_ffn_sh_up': _L2_ffn_in['sh_up'], 'L2_ffn_sh_down': _L2_ffn_in['sh_down'], 'L2_ffn_e_gate': _L2_ffn_in['e_gate'], 'L2_ffn_e_up': _L2_ffn_in['e_up'], 'L2_ffn_e_down': _L2_ffn_in['e_down'], 'L3_xattn_Wq': _L3_xattn_in['Wq'], 'L3_xattn_Wk': _L3_xattn_in['Wk'], 'L3_xattn_Wv': _L3_xattn_in['Wv'], 'L3_xattn_Wo': _L3_xattn_in['Wo'], 'L3_xattn_bo': _L3_xattn_in['bo'], 'L3_ffn_gate_v': _L3_ffn_in['gate_v'], 'L3_ffn_gate_g': _L3_ffn_in['gate_g'], 'L3_ffn_gate_b': _L3_ffn_in['gate_b'], 'L3_ffn_w1_v': _L3_ffn_in['w1_v'], 'L3_ffn_w1_g': _L3_ffn_in['w1_g'], 'L3_ffn_b1': _L3_ffn_in['b1'], 'L3_ffn_w2_v': _L3_ffn_in['w2_v'], 'L3_ffn_w2_g': _L3_ffn_in['w2_g'], 'L3_ffn_b2': _L3_ffn_in['b2']}

def reference(x, ctx_1024, mask_BxS2_ik0, L0_xattn_Wq, L0_xattn_Wk, L0_xattn_Wv, L0_xattn_Wo, L0_ffn_ln1_w, L0_ffn_ln1_b, L0_ffn_q_w, L0_ffn_q_b, L0_ffn_k_w, L0_ffn_k_b, L0_ffn_v_w, L0_ffn_v_b, L0_ffn_o_w, L0_ffn_o_b, L0_ffn_ln2_w, L0_ffn_ln2_b, L0_ffn_router_w, L0_ffn_fc1_w, L0_ffn_fc1_b, L0_ffn_fc2_w, L0_ffn_fc2_b, L1_xattn_Wq, L1_xattn_Wk, L1_xattn_Wv, L1_xattn_Wo, L1_xattn_bo, L1_ffn_Wqkv, L1_ffn_bqkv, L1_ffn_Wo, L1_ffn_bo, L1_ffn_g1, L1_ffn_be1, L1_ffn_g2, L1_ffn_be2, L1_ffn_Wg, L1_ffn_W1, L1_ffn_b1, L1_ffn_W2, L1_ffn_b2, L2_xattn_Wq, L2_xattn_Wk, L2_xattn_Wv, L2_xattn_Wu, L2_xattn_bu, L2_xattn_qn_w, L2_xattn_qn_b, L2_xattn_kn_w, L2_xattn_kn_b, L2_ffn_norm1_w, L2_ffn_norm2_w, L2_ffn_wq, L2_ffn_wk, L2_ffn_wv, L2_ffn_wo, L2_ffn_router_w, L2_ffn_sh_gate, L2_ffn_sh_up, L2_ffn_sh_down, L2_ffn_e_gate, L2_ffn_e_up, L2_ffn_e_down, L3_xattn_Wq, L3_xattn_Wk, L3_xattn_Wv, L3_xattn_Wo, L3_xattn_bo, L3_ffn_gate_v, L3_ffn_gate_g, L3_ffn_gate_b, L3_ffn_w1_v, L3_ffn_w1_g, L3_ffn_b1, L3_ffn_w2_v, L3_ffn_w2_g, L3_ffn_b2):
    import jax
    import jax.numpy as jnp

    def _L0_xattn_ref(H, T, mask, Wq, Wk, Wv, Wo):
        import jax, jax.numpy as jnp
        import numpy as np
        HEADS = 16
        DIM_Q = 128
        DIM_KV = 128
        INNER = 128
        B, Lq, _ = H.shape
        Lkv = T.shape[1]
        dph = INNER // HEADS

        def shape(x, L):
            return x.reshape(B, L, HEADS, dph).transpose(0, 2, 1, 3)
        q = shape(H @ Wq, Lq) * dph ** (-0.5)
        k = shape(T @ Wk, Lkv)
        v = shape(T @ Wv, Lkv)
        scores = jnp.einsum('bhqd,bhkd->bhqk', q, k)
        ext = (1.0 - mask.astype(scores.dtype))[:, None, None, :] * jnp.finfo(scores.dtype).min
        scores = scores + ext
        attn = jax.nn.softmax(scores.astype(jnp.float32), axis=-1).astype(scores.dtype)
        out = jnp.einsum('bhqk,bhkd->bhqd', attn, v)
        out = out.transpose(0, 2, 1, 3).reshape(B, Lq, INNER)
        return out @ Wo

    def _L0_ffn_ref(hidden_states, ln1_w, ln1_b, q_w, q_b, k_w, k_b, v_w, v_b, o_w, o_b, ln2_w, ln2_b, router_w, fc1_w, fc1_b, fc2_w, fc2_b):
        import math
        import jax, jax.numpy as jnp
        import numpy as np
        B, S, D, H, E, F = (2, 128, 128, 16, 16, 512)
        HEAD = D // H
        MOE_TOKEN_DROPOUT = 0.2
        EPS = 1e-05

        def layer_norm(x, w, b):
            mu = x.mean(-1, keepdims=True)
            var = ((x - mu) ** 2).mean(-1, keepdims=True)
            return (x - mu) * jax.lax.rsqrt(var + EPS) * w + b
        b, s, _ = hidden_states.shape
        T = b * s
        neg = jnp.finfo(jnp.float32).min
        resid = hidden_states
        x = layer_norm(hidden_states, ln1_w, ln1_b)
        q = (x @ q_w + q_b) / math.sqrt(HEAD)
        k = x @ k_w + k_b
        v = x @ v_w + v_b
        split = lambda t: t.reshape(b, s, H, HEAD).transpose(0, 2, 1, 3)
        q, k, v = (split(q), split(k), split(v))
        scores = jnp.einsum('bhqd,bhkd->bhqk', q, k)
        causal = jnp.tril(jnp.ones((s, s), bool))
        scores = jnp.where(causal, scores, neg)
        attn = jax.nn.softmax(scores, axis=-1)
        ctx = jnp.einsum('bhqk,bhkd->bhqd', attn, v)
        ctx = ctx.transpose(0, 2, 1, 3).reshape(b, s, D)
        hidden = resid + (ctx @ o_w + o_b)
        resid = hidden
        xt = layer_norm(hidden, ln2_w, ln2_b).reshape(T, D)
        logits = xt @ router_w
        probs = jax.nn.softmax(logits, axis=-1)
        top1 = jnp.argmax(probs, axis=-1)
        m1 = jax.nn.one_hot(top1, E, dtype=jnp.float32)
        logits_no1 = jnp.where(m1 > 0, -jnp.inf, logits)
        top2 = jnp.argmax(logits_no1, axis=-1)
        m2 = jax.nn.one_hot(top2, E, dtype=jnp.float32)
        loc1 = jnp.cumsum(m1, axis=0) - 1.0
        loc2 = jnp.cumsum(m2, axis=0) - 1.0 + m1.sum(axis=0, keepdims=True)
        C = 2 * math.ceil(T / E)
        m1 = m1 * (loc1 < C)
        m2 = m2 * (loc2 < C)
        g1 = (probs * m1).sum(-1)
        g2 = (probs * m2).sum(-1)
        denom = jnp.maximum(g1 + g2, jnp.finfo(jnp.float32).eps)
        g1, g2 = (g1 / denom, g2 / denom)
        slot1 = (loc1 * m1).sum(-1).astype(jnp.int32)
        slot2 = (loc2 * m2).sum(-1).astype(jnp.int32)
        d1 = m1[:, :, None] * jax.nn.one_hot(slot1, C, dtype=jnp.float32)[:, None, :]
        d2 = m2[:, :, None] * jax.nn.one_hot(slot2, C, dtype=jnp.float32)[:, None, :]
        dispatch = d1 + d2
        combine = g1[:, None, None] * d1 + g2[:, None, None] * d2
        xin = jnp.einsum('tec,td->ecd', dispatch, xt)
        h = jnp.einsum('ecd,edf->ecf', xin, fc1_w) + fc1_b[:, None, :]
        h = jax.nn.gelu(h, approximate=False)
        eout = jnp.einsum('ecf,efd->ecd', h, fc2_w) + fc2_b[:, None, :]
        eout = eout * (1.0 - MOE_TOKEN_DROPOUT)
        moe_out = jnp.einsum('tec,ecd->td', combine, eout).reshape(b, s, D)
        return resid + moe_out

    def _L1_xattn_ref(x, context, Wq, Wk, Wv, Wo, bo):
        import jax, jax.numpy as jnp
        import numpy as np
        DIM = 128
        NUM_HEADS = 8
        HEAD_DIM = 64
        INNER = NUM_HEADS * HEAD_DIM
        B, N, _ = x.shape
        M = context.shape[1]
        scale = HEAD_DIM ** (-0.5)
        q = (x @ Wq).reshape(B, N, NUM_HEADS, HEAD_DIM).transpose(0, 2, 1, 3)
        k = (context @ Wk).reshape(B, M, NUM_HEADS, HEAD_DIM).transpose(0, 2, 1, 3)
        v = (context @ Wv).reshape(B, M, NUM_HEADS, HEAD_DIM).transpose(0, 2, 1, 3)
        attn = jax.nn.softmax(jnp.einsum('bhnd,bhmd->bhnm', q, k) * scale, axis=-1)
        out = jnp.einsum('bhnm,bhmd->bhnd', attn, v)
        out = out.transpose(0, 2, 1, 3).reshape(B, N, INNER)
        return out @ Wo + bo

    def _L1_ffn_ref(x, Wqkv, bqkv, Wo, bo, g1, be1, g2, be2, Wg, W1, b1, W2, b2):
        import jax, jax.numpy as jnp
        import numpy as np
        D = 128
        H = 4
        DF = 512
        E = 8
        EPS = 1e-05

        def _layer_norm(x, g, b):
            mu = jnp.mean(x, axis=-1, keepdims=True)
            var = jnp.mean(jnp.square(x - mu), axis=-1, keepdims=True)
            return (x - mu) * jax.lax.rsqrt(var + EPS) * g + b

        def _mha(x, Wqkv, bqkv, Wo, bo):
            S, B, _ = x.shape
            hd = D // H
            qkv = x @ Wqkv.T + bqkv
            q, k, v = jnp.split(qkv, 3, axis=-1)
            to_heads = lambda t: t.reshape(S, B, H, hd).transpose(1, 2, 0, 3)
            q, k, v = (to_heads(q), to_heads(k), to_heads(v))
            scores = jnp.einsum('bhqd,bhkd->bhqk', q, k) * (1.0 / np.sqrt(hd))
            att = jax.nn.softmax(scores, axis=-1)
            o = jnp.einsum('bhqk,bhkd->bhqd', att, v)
            o = o.transpose(2, 0, 1, 3).reshape(S, B, D)
            return o @ Wo.T + bo

        def _moe(x, Wg, W1, b1, W2, b2):
            S, B, _ = x.shape
            xf = x.reshape(S * B, D)
            logits = xf @ Wg.T
            idx = jnp.argmax(logits, axis=-1)
            out = jnp.zeros_like(xf)
            for e in range(E):
                m = (idx == e)[:, None].astype(xf.dtype)
                h = jax.nn.relu(xf @ W1[e] + b1[e])
                out = out + m * (h @ W2[e] + b2[e])
            return out.reshape(S, B, D)
        y = _layer_norm(x + _mha(x, Wqkv, bqkv, Wo, bo), g1, be1)
        z = _layer_norm(y + _moe(y, Wg, W1, b1, W2, b2), g2, be2)
        return z

    def _L2_xattn_ref(emb, context, Wq, Wk, Wv, Wu, bu, qn_w, qn_b, kn_w, kn_b):
        import jax, jax.numpy as jnp
        import numpy as np
        N_HEADS = 16
        KQ_DIM = 64
        EMB_DIM = 128
        CTX_DIM = 128
        EPS = 1e-05

        def _layernorm(x, w, b):
            mu = jnp.mean(x, axis=-1, keepdims=True)
            var = jnp.mean(jnp.square(x - mu), axis=-1, keepdims=True)
            return (x - mu) * jax.lax.rsqrt(var + EPS) * w + b
        B, SQ, _ = emb.shape
        SK = context.shape[1]
        q = (emb @ Wq.T).reshape(B, SQ, N_HEADS, KQ_DIM).transpose(0, 2, 1, 3)
        k = (context @ Wk.T).reshape(B, SK, N_HEADS, KQ_DIM).transpose(0, 2, 1, 3)
        v = (context @ Wv.T).reshape(B, SK, N_HEADS, KQ_DIM).transpose(0, 2, 1, 3)
        q = _layernorm(q, qn_w, qn_b)
        k = _layernorm(k, kn_w, kn_b)
        scale = 1.0 / jnp.sqrt(jnp.asarray(KQ_DIM, emb.dtype))
        attn = jnp.einsum('bhqd,bhkd->bhqk', q, k) * scale
        attn = jax.nn.softmax(attn, axis=-1)
        out = jnp.einsum('bhqk,bhkd->bhqd', attn, v)
        out = out.transpose(0, 2, 1, 3).reshape(B, SQ, N_HEADS * KQ_DIM)
        return out @ Wu.T + bu

    def _L2_ffn_ref(X, norm1_w, norm2_w, wq, wk, wv, wo, router_w, sh_gate, sh_up, sh_down, e_gate, e_up, e_down):
        import jax, jax.numpy as jnp
        import numpy as np
        D_MODEL = 128
        N_HEADS = 16
        D_HEAD = D_MODEL // N_HEADS
        N_EXPERTS = 8
        TOP_K = 2
        D_FF = 256
        EPS = 1e-06

        def rmsnorm(x, w):
            return x * jax.lax.rsqrt(jnp.mean(x * x, axis=-1, keepdims=True) + EPS) * w

        def swiglu(x, w_gate, w_up, w_down):
            return jax.nn.silu(x @ w_gate) * (x @ w_up) @ w_down
        B, S, d = X.shape
        scale = 1.0 / jnp.sqrt(jnp.asarray(D_HEAD, X.dtype))
        h = rmsnorm(X, norm1_w)
        q = (h @ wq).reshape(B, S, N_HEADS, D_HEAD)
        k = (h @ wk).reshape(B, S, N_HEADS, D_HEAD)
        v = (h @ wv).reshape(B, S, N_HEADS, D_HEAD)
        scores = jnp.einsum('bshd,bthd->bhst', q, k) * scale
        attn = jax.nn.softmax(scores, axis=-1)
        ctx = jnp.einsum('bhst,bthd->bshd', attn, v).reshape(B, S, d)
        X = X + ctx @ wo
        h2 = rmsnorm(X, norm2_w).reshape(B * S, d)
        logits = h2 @ router_w
        probs = jax.nn.softmax(logits, axis=-1)
        topw, topi = jax.lax.top_k(probs, TOP_K)
        topw = jax.nn.softmax(topw, axis=-1)
        combine = jnp.sum(jax.nn.one_hot(topi, N_EXPERTS, dtype=h2.dtype) * topw[..., None], axis=1)
        shared = swiglu(h2, sh_gate, sh_up, sh_down)
        gate = jnp.einsum('td,edf->etf', h2, e_gate)
        up = jnp.einsum('td,edf->etf', h2, e_up)
        eout = jnp.einsum('etf,efd->etd', jax.nn.silu(gate) * up, e_down)
        spec = jnp.einsum('etd,te->td', eout, combine)
        moe_out = (shared + spec).reshape(B, S, d)
        return X + moe_out

    def _L3_xattn_ref(x, context, Wq, Wk, Wv, Wo, bo):
        import jax, jax.numpy as jnp
        import numpy as np
        HEADS = 16
        DIM_HEAD = 64
        QUERY_DIM = 128
        CONTEXT_DIM = 128
        INNER = HEADS * DIM_HEAD
        B, N, _ = x.shape
        M = context.shape[1]
        scale = DIM_HEAD ** (-0.5)
        q = jnp.einsum('bnd,ed->bne', x, Wq)
        k = jnp.einsum('bmd,ed->bme', context, Wk)
        v = jnp.einsum('bmd,ed->bme', context, Wv)
        q = q.reshape(B, N, HEADS, DIM_HEAD).transpose(0, 2, 1, 3)
        k = k.reshape(B, M, HEADS, DIM_HEAD).transpose(0, 2, 1, 3)
        v = v.reshape(B, M, HEADS, DIM_HEAD).transpose(0, 2, 1, 3)
        sim = jnp.einsum('bhid,bhjd->bhij', q, k) * scale
        attn = jax.nn.softmax(sim, axis=-1)
        out = jnp.einsum('bhij,bhjd->bhid', attn, v)
        out = out.transpose(0, 2, 1, 3).reshape(B, N, INNER)
        return jnp.einsum('bne,oe->bno', out, Wo) + bo

    def _L3_ffn_ref(x, gate_v, gate_g, gate_b, w1_v, w1_g, b1, w2_v, w2_g, b2):
        import jax, jax.numpy as jnp
        import numpy as np
        B, S, D, H, E = (4, 256, 128, 512, 8)
        EPS = 1e-12

        def _wn(v, g):
            n = jnp.sqrt(jnp.sum(v * v, axis=-1, keepdims=True))
            return v / jnp.maximum(n, EPS) * g[:, None]
        b, s, d = x.shape
        xf = x.reshape(-1, d)
        gw = _wn(gate_v, gate_g)
        gates = jax.nn.softmax(xf @ gw.T + gate_b, axis=-1)
        top_k = min(2, E)
        _, top_idx = jax.lax.top_k(gates, top_k)
        out = jnp.zeros_like(xf)
        for i in range(E):
            mask = jnp.any(top_idx == i, axis=1).astype(xf.dtype)[:, None]
            xm = xf * mask
            W1 = _wn(w1_v[i], w1_g[i])
            h = xm @ W1.T + b1[i]
            h = h * jax.nn.sigmoid(h)
            W2 = _wn(w2_v[i], w2_g[i])
            out = out + mask * (h @ W2.T + b2[i])
        return out.reshape(b, s, d)
    x = x + _L0_xattn_ref(_layernorm(x, axis=-1), ctx_1024, mask_BxS2_ik0, L0_xattn_Wq, L0_xattn_Wk, L0_xattn_Wv, L0_xattn_Wo)
    x = x + _L0_ffn_ref(_layernorm(x, axis=-1), L0_ffn_ln1_w, L0_ffn_ln1_b, L0_ffn_q_w, L0_ffn_q_b, L0_ffn_k_w, L0_ffn_k_b, L0_ffn_v_w, L0_ffn_v_b, L0_ffn_o_w, L0_ffn_o_b, L0_ffn_ln2_w, L0_ffn_ln2_b, L0_ffn_router_w, L0_ffn_fc1_w, L0_ffn_fc1_b, L0_ffn_fc2_w, L0_ffn_fc2_b)
    x = x + _L1_xattn_ref(_layernorm(x, axis=-1), ctx_1024, L1_xattn_Wq, L1_xattn_Wk, L1_xattn_Wv, L1_xattn_Wo, L1_xattn_bo)
    x = x + _L1_ffn_ref(_layernorm(x, axis=-1), L1_ffn_Wqkv, L1_ffn_bqkv, L1_ffn_Wo, L1_ffn_bo, L1_ffn_g1, L1_ffn_be1, L1_ffn_g2, L1_ffn_be2, L1_ffn_Wg, L1_ffn_W1, L1_ffn_b1, L1_ffn_W2, L1_ffn_b2)
    x = x + _L2_xattn_ref(_layernorm(x, axis=-1), ctx_1024, L2_xattn_Wq, L2_xattn_Wk, L2_xattn_Wv, L2_xattn_Wu, L2_xattn_bu, L2_xattn_qn_w, L2_xattn_qn_b, L2_xattn_kn_w, L2_xattn_kn_b)
    x = x + _L2_ffn_ref(_layernorm(x, axis=-1), L2_ffn_norm1_w, L2_ffn_norm2_w, L2_ffn_wq, L2_ffn_wk, L2_ffn_wv, L2_ffn_wo, L2_ffn_router_w, L2_ffn_sh_gate, L2_ffn_sh_up, L2_ffn_sh_down, L2_ffn_e_gate, L2_ffn_e_up, L2_ffn_e_down)
    x = x + _L3_xattn_ref(_layernorm(x, axis=-1), ctx_1024, L3_xattn_Wq, L3_xattn_Wk, L3_xattn_Wv, L3_xattn_Wo, L3_xattn_bo)
    x = x + _L3_ffn_ref(_layernorm(x, axis=-1), L3_ffn_gate_v, L3_ffn_gate_g, L3_ffn_gate_b, L3_ffn_w1_v, L3_ffn_w1_g, L3_ffn_b1, L3_ffn_w2_v, L3_ffn_w2_g, L3_ffn_b2)
    return x

_drawn_inputs = setup_inputs


def setup_inputs(seed=0):
    import zlib

    import numpy as np

    out = dict(_drawn_inputs(seed))
    spreads = {'L0_ffn_ln1_w': (1.0, 0.6),
     'L0_ffn_ln1_b': (0.0, 0.358),
     'L0_ffn_q_b': (0.0, 0.8),
     'L0_ffn_k_b': (0.0, 2.0),
     'L0_ffn_v_b': (0.0, 0.1),
     'L0_ffn_o_b': (0.0, 0.1),
     'L0_ffn_ln2_w': (1.0, 0.2),
     'L0_ffn_ln2_b': (0.0, 0.1),
     'L0_ffn_fc1_b': (0.0, 0.1),
     'L0_ffn_fc2_b': (0.0, 0.1),
     'L1_ffn_bqkv': (0.0, 0.1),
     'L1_ffn_bo': (0.0, 0.1),
     'L1_ffn_g1': (1.0, 0.2),
     'L1_ffn_be1': (0.0, 0.1),
     'L1_ffn_g2': (1.0, 0.2),
     'L1_ffn_be2': (0.0, 0.1),
     'L1_ffn_b1': (0.0, 0.1),
     'L1_ffn_b2': (0.0, 0.1),
     'L2_xattn_qn_w': (1.0, 0.6),
     'L2_xattn_qn_b': (0.0, 0.8),
     'L2_xattn_kn_w': (1.0, 0.6),
     'L2_xattn_kn_b': (0.0, 2.0),
     'L2_ffn_norm1_w': (1.0, 0.6),
     'L2_ffn_norm2_w': (1.0, 0.6),
     'L3_ffn_gate_g': (1.0, 0.2),
     'L3_ffn_gate_b': (0.0, 0.1),
     'L3_ffn_w1_g': (1.0, 0.6),
     'L3_ffn_b1': (0.0, 0.988),
     'L3_ffn_w2_g': (1.0, 0.6),
     'L3_ffn_b2': (0.0, 0.625)}
    factors = {'L0_xattn_Wq': 5.936,
     'L0_xattn_Wk': 4.501,
     'L0_ffn_q_w': 8.0,
     'L0_ffn_k_w': 7.553,
     'L0_ffn_v_w': 2.676,
     'L2_ffn_wq': 8.0,
     'L2_ffn_wk': 8.0,
     'L2_ffn_wv': 4.569,
     'L2_ffn_wo': 4.639,
     'L2_ffn_router_w': 8.0,
     'L2_ffn_sh_gate': 8.0,
     'L2_ffn_sh_up': 8.0,
     'L2_ffn_sh_down': 6.012,
     'L2_ffn_e_gate': 8.0,
     'L2_ffn_e_up': 8.0,
     'L2_ffn_e_down': 8.0,
     'L3_xattn_Wq': 36.741,
     'L3_xattn_Wk': 34.988,
     'L3_xattn_Wv': 3.942,
     'L3_xattn_Wo': 3.644,
     'L3_xattn_bo': 8.0}
    for name, (base, spread) in spreads.items():
        noise = np.random.default_rng([zlib.crc32(name.encode()), seed]).standard_normal(out[name].shape)
        drawn = base * np.exp(spread * noise) if base else spread * noise
        out[name] = jnp.asarray(drawn.astype(out[name].dtype))
    for name, factor in factors.items():
        out[name] = (out[name] * factor).astype(out[name].dtype)
    return out
```

```python
from contextlib import ExitStack

import numpy as np

import concourse.bass as bass
from concourse import mybir

ALU = mybir.AluOpType
ACT = mybir.ActivationFunctionType
F32 = mybir.dt.float32
BF16 = mybir.dt.bfloat16
I32 = mybir.dt.int32
AX_X = mybir.AxisListType.X

P = 128
B = 2
S = 512
TB = S // P
NT = B * TB
KV = 77
BANK = 512
EPS_LN = 1e-5
ARENA = 23808
FMIN = float(np.finfo(np.float32).min)
STAGES = 8
NMOE = 4

XATTN = [
    dict(G=1, H=16, dh=8, mask=True, qk_norm=False, bias=False),
    dict(G=4, H=8, dh=64, mask=False, qk_norm=False, bias=True),
    dict(G=8, H=16, dh=64, mask=False, qk_norm=True, bias=True),
    dict(G=8, H=16, dh=64, mask=False, qk_norm=False, bias=True),
]
MOE = [
    dict(E=16, C=4, act=ACT.Gelu, W=1028),
    dict(E=8, C=4, act=ACT.Relu, W=1028),
    dict(E=8, C=2, act=ACT.Silu, W=768),
    dict(E=8, C=4, act=ACT.Silu, W=1028),
]
XSTEPS = [10, 10, 16, 10]
CAPACITY = 2 * -(-B * S // 16)
E0 = 16
SLOTS = E0 * CAPACITY
DROPPED = 2 * SLOTS
assert CAPACITY == P
HS, DS = 16, 8


def constants():
    p = np.arange(P)
    f = np.float32
    return {
        "ident": np.eye(P, dtype=f),
        "headmask": (p[:, None] // DS == np.arange(HS)).astype(f),
        "halfmask": (p[:, None] // 64 == np.arange(2)).astype(f),
        "later": np.triu(np.ones((P, P), f), 1) * f(-1e30),
        "before": np.triu(np.ones((P, P), f)),
        "firstness": np.broadcast_to(16.0 - np.arange(16, dtype=f), (P, 16)),
        "neghalf": np.full((P, 16), -0.5, f),
        "ones": np.ones((P, P), f),
        "queue": np.broadcast_to(np.arange(E0, dtype=f) * CAPACITY - 1, (P, E0)),
    }


def layout(inp):
    col = lambda v: v.reshape(-1, 1)
    row = lambda v: np.broadcast_to(v.reshape(1, -1), (P, v.size))
    blocks = dict(constants())
    blocks["ctxT"] = inp["ctx_1024"].transpose(2, 0, 1).reshape(P, B * KV)
    for l in range(4):
        n = f"L{l}_xattn_"
        out = inp[n + ("Wu" if l == 2 else "Wo")]
        if l >= 2:
            wq, wk, wv, out = inp[n + "Wq"].T, inp[n + "Wk"].T, inp[n + "Wv"].T, out.T
        else:
            wq, wk, wv = inp[n + "Wq"], inp[n + "Wk"], inp[n + "Wv"]
        G = XATTN[l]["G"]
        blocks[f"x{l}_wk"], blocks[f"x{l}_wv"], blocks[f"x{l}_wq"] = wk, wv, wq
        blocks[f"x{l}_wo"] = out.reshape(G, P, P).transpose(1, 0, 2).reshape(P, G * P)
        if l:
            blocks[f"x{l}_bo"] = row(inp[n + ("bu" if l == 2 else "bo")])
        if l == 2:
            for k in ("qn_w", "qn_b", "kn_w", "kn_b"):
                blocks[k] = col(np.concatenate([inp[n + k]] * 2))
        m = f"L{l}_ffn_"
        if l == 0:
            for k in ("q_w", "k_w", "v_w", "o_w"):
                blocks["s0_" + k] = inp[m + k]
            for k in ("q_b", "k_b", "ln1_w", "ln1_b", "ln2_w", "ln2_b"):
                blocks["s0_" + k] = col(inp[m + k])
            blocks["s0_v_b"], blocks["s0_o_b"] = row(inp[m + "v_b"]), row(inp[m + "o_b"])
            blocks["m0_router"] = inp[m + "router_w"]
            blocks["m0_b2"] = inp[m + "fc2_b"]
        if l == 1:
            blocks["h_wqkv"] = inp[m + "Wqkv"].T
            blocks["h_wo"] = inp[m + "Wo"].T
            for k in ("bqkv", "bo", "g1", "be1", "g2", "be2"):
                blocks["h_" + k] = row(inp[m + k])
            blocks["m1_router"] = inp[m + "Wg"].T
            blocks["m1_b2"] = inp[m + "b2"]
        if l == 2:
            for k in ("wq", "wk", "wv", "wo"):
                blocks["s2_" + k[1] + "_w"] = inp[m + k]
            blocks["s2_norm1"], blocks["s2_norm2"] = col(inp[m + "norm1_w"]), col(inp[m + "norm2_w"])
            blocks["m2_router"] = inp[m + "router_w"]
        if l == 3:
            blocks["m3_gate_v"] = inp[m + "gate_v"]
            blocks["m3_gate_g"] = col(inp[m + "gate_g"])
            blocks["m3_gate_b"] = row(inp[m + "gate_b"])
            blocks["m3_g1"] = inp[m + "w1_g"].reshape(8, 4, P).transpose(2, 0, 1).reshape(P, 32)
            blocks["m3_g2"] = inp[m + "w2_g"].T
            blocks["m3_b2"] = inp[m + "b2"]
    return blocks


def expert_layout(inp):
    up = lambda w: w
    down = lambda w: w.reshape(w.shape[0], -1, P, P).transpose(0, 2, 1, 3).reshape(w.shape[0], P, -1)
    bias = lambda v: v.reshape(v.shape[0], 4, P).transpose(0, 2, 1)
    out = []
    out.append(np.concatenate([up(inp["L0_ffn_fc1_w"]), down(inp["L0_ffn_fc2_w"]), bias(inp["L0_ffn_fc1_b"])], 2))
    out.append(np.concatenate([up(inp["L1_ffn_W1"]), down(inp["L1_ffn_W2"]), bias(inp["L1_ffn_b1"])], 2))
    m = "L2_ffn_"
    routed = np.concatenate([inp[m + "e_gate"], inp[m + "e_up"], down(inp[m + "e_down"])], 2)
    shared = np.concatenate([inp[m + "sh_gate"][None], inp[m + "sh_up"][None], down(inp[m + "sh_down"][None])], 2)
    out.append(np.concatenate([routed, shared]))
    m = "L3_ffn_"
    out.append(np.concatenate([inp[m + "w1_v"].transpose(0, 2, 1), down(inp[m + "w2_v"].transpose(0, 2, 1)), bias(inp[m + "b1"])], 2))
    return out



def cuts(at):
    return [at[n][0] + at[n][2] for n in ("x0_wo", "m0_b2", "m1_b2", "m2_router", "m3_b2")]


def program(nc, x, mask, packed, experts, out, queued, answers, at):
    ctx = ExitStack()
    with ctx:
        def sb(name, shape, dt=F32):
            return ctx.enter_context(nc.sbuf_tensor(name, shape, dt))

        def sem(name):
            return ctx.enter_context(nc.semaphore(name))

        def sems(names):
            return [sem(n) for n in names.split()]

        ends = cuts(at)
        held = sb("held", [P, ends[-1]])

        def w(name, lo=0, hi=None):
            a, r, c = at[name]
            return held[0:r, a + lo:a + (c if hi is None else hi)]

        def w_at(name, lo, n=1):
            return held[0:at[name][1], bass.ds(lo + at[name][0], n)]

        x_res = sb("x_res", [P, NT * P])
        r_res = sb("r_res", [P, NT * P])
        xT_all = sb("xT_all", [P, NT * P])
        kbd = sb("kbd", [P, B * 16 * KV])
        vx = sb("vx", [KV, B * 16 * 65])
        wexp = sb("wexp", [P, 2, 1028])
        gates = sb("gates", [P, NT, 16])
        gatesT = sb("gatesT", [16, NT * P])
        logits = sb("logits", [P, NT * 16])
        mask_i = sb("mask_i", [P, B, 4 * KV], I32)
        stats = sb("stats", [P, B, 6])
        mv = sb("mv", [P, B, 2])
        var = sb("var", [P, B, 16])
        rstd = sb("rstd", [P, B, 16])
        small = sb("small", [P, B, 64])
        chain = sb("chain", [P, 8 * P])
        arena = sb("arena", [P, ARENA])
        pool_pad = sb("pool_pad", [P, 8])
        n_sum = sb("n_sum", [P, 40])
        slot_i = sb("slot_i", [P, 32], I32)
        s1_now = sb("s1_now", [P, 2, 4])
        ident_bf = sb("ident_bf", [P, P], BF16)
        later_bf = sb("later_bf", [P, P], BF16)
        psum = ctx.enter_context(nc.psum_tensor("psum", [P, 8 * BANK], F32))

        def bank(n, lo, hi, rows=P):
            return psum[0:rows, n * BANK + lo:n * BANK + hi]

        def take(sizes):
            views, a = {}, 0
            for name, n in sizes.items():
                views[name] = arena[:, a:a + n]
                a += n
            assert a <= ARENA, a
            return views

        def two(v):
            return v.rearrange("p (j n) -> p j n", j=2)

        xn, xT, cc, yb = (two(chain[:, n * 256:n * 256 + 256]) for n in range(4))
        A = take(dict(qn=2048, qT=2048, E=2 * 1232, PT=4096, O=2048, OT=2048, ext=8 * KV, kn=2048, kaff=8 * 154))
        qn, qT, E, PT, O, OT, ext, kn = (two(A[k]) for k in ("qn", "qT", "E", "PT", "O", "OT", "ext", "kn"))
        kaff = A["kaff"]
        U = take(dict(k=2 * HS * S, P=4 * BANK, PT=4 * BANK, qa=NT * P, ka=NT * P, va=NT * HS * (DS + 1), qcur=P))
        kself, pself, ptself, q_all, k_all, v_all, qcur = (U[n] for n in ("k", "P", "PT", "qa", "ka", "va", "qcur"))
        ctx_all = xT_all[:, :]
        H = take(dict(qkv=2 * 384, prod=512, sc=64))
        qkv, prod = two(H["qkv"]), H["prod"]
        M = take(dict(h=2 * 2048, s=2048, w2n=1024, s2=8 * P, diag=8 * P, gv=P, gwT=8, ga=P, gb=P, gc=P,
                      m12=256, pre=256, tot=16, mk=256))
        sq = qn
        s1_all, s2_col = n_sum[:, 0:32], n_sum[:, 32:40]
        hT, sg, w2n = two(M["h"]), two(M["s"]), two(M["w2n"])

        D = take(dict(skip=10624, w=2 * 1028, xin=4 * P, xe=2 * P, h=2 * 512, y=4 * P, back=16 * P, loc=256, slot=64))
        W0 = [wexp[:, 0, :], wexp[:, 1, :], D["w"][:, 0:1028], D["w"][:, 1028:2056]]

        in_x, in_mask, stored, const_ok = sems("in_x in_mask stored const_ok")
        in_held = [sem(f"in_held{n}") for n in range(5)]
        dve_step, act_step, pool_step = sems("dve_step act_step pool_step")
        x_stat, x_rstd, x_xn, x_xTp, x_xT = sems("x_stat x_rstd x_xn x_xTp x_xT")
        kv_ps, kn_ok, kT_ps, k_ok, v_ok = sems("kv_ps kn_ok kT_ps k_ok v_ok")
        kc_ok, ksq_ok, kvar_ok, krstd_ok = sems("kc_ok ksq_ok kvar_ok krstd_ok")
        q_ps, qc_ok, qsq_ok, qvar_ok, qrstd_ok, qn_ok, qnT_ps, qT_ok = sems(
            "q_ps qc_ok qsq_ok qvar_ok qrstd_ok qn_ok qnT_ps qT_ok")
        sc_ps, e_ok, p_ok, pT_ps, pT_act, pT_dve = sems("sc_ps e_ok p_ok pT_ps pT_act pT_dve")
        o_ps, o_ok, oT_ps, oT_ok, y_ps, x_done = sems("o_ps o_ok oT_ps oT_ok y_ps x_done")
        a_stat, a_rstd, h0_ok, b_stat, b_rstd, b_xn, s_xTp, s_xT, qkv_ps, qkv_ok = sems(
            "a_stat a_rstd h0_ok b_stat b_rstd b_xn s_xTp s_xT qkv_ps qkv_ok")
        kself0, kself1, qcur_ok, us_ps, um_ok, up_ok, upT_ps, upT_act, upT_dve, uo_ps, ctx_ok, inv_ok = sems(
            "kself0 kself1 qcur_ok us_ps um_ok up_ok upT_ps upT_act upT_dve uo_ps ctx_ok inv_ok")
        t_cc, t_ccT, t_ccS, t_y, r_ok = sems("t_cc t_ccT t_ccS t_y r_ok")
        m_stat, m_rstd, m_xn, m_xTp, m_xT, m_copy, lg_ps, lg_ok = sems(
            "m_stat m_rstd m_xn m_xTp m_xT m_copy lg_ps lg_ok")
        g_sub, g_exp, g_m, g_loc, gate_ok, gT_ps, gT_ok, b2_ps, b2_ok = sems(
            "g_sub g_exp g_m g_loc gate_ok gT_ps gT_ok b2_ps b2_ok")
        w_in = [sem(f"w_in{n}") for n in range(2)]
        h_ps, h_ok, sg_ok, h2_ok, ye_ps, acc_ok, w2n_ok = sems("h_ps h_ok sg_ok h2_ok ye_ps acc_ok w2n_ok")
        n_sq, n_ps, n_max, n_pow, n_ok, n_gv, n_gvT, n_diag, n_row, n_s2 = sems(
            "n_sq n_ps n_max n_pow n_ok n_gv n_gvT n_diag n_row n_s2")
        w0_in = [sem(f"w0_in{n}") for n in range(4)]
        d_in = [sem(f"d_in{n}") for n in range(4)]
        d_stored = [sem(f"d_stored{n}") for n in range(4)]
        d_back = [sem(f"d_back{n}") for n in range(4)]
        zeros_set, zeros_out, slots_ok, scattered = sems("zeros_set zeros_out slots_ok scattered")
        d_T, d_xe, d_H, d_h, d_O, d_y, d_done = sems("d_T d_xe d_H d_h d_O d_y d_done")
        f_stat, f_rstd, f_done = sems("f_stat f_rstd f_done")
        t1_e, t1_p, t1_av = sems("t1_e t1_p t1_av")

        block = ctx.enter_context(nc.Block())

        def tile(i, j):
            return bass.ds(i * P + j * S, P)

        class Steps:
            def __init__(self, eng, semaphore):
                self.eng, self.sem, self.base, self.n, self.i, self.per = eng, semaphore, 0, 0, None, 0

            def loop(self, i, per):
                self.base, self.n, self.i, self.per = self.base + self.n, 0, i, per

            def end(self, trips):
                assert self.n == self.per, (self.n, self.per)
                self.base, self.n, self.i = self.base + trips * self.per, 0, None

            def then(self, instruction):
                self.n += 1
                instruction.then_inc(self.sem, 1)
                at = self.base + self.n
                self.eng.wait_ge(self.sem, at if self.i is None else self.i * self.per + at)

        def count(base, i, j):
            return i * 2 + (base + j + 1)

        UNITS = NT * HS
        LEAD = 4
        KB = [2 * n for n in np.cumsum([0, 0, 8, 9, 8]).tolist()]
        HB = [0, 0, 64, 64, 128]
        HPB = [4 * n for n in KB]
        WB = [[0, 0], [0, 0], [4, 4], [9, 8]]

        def block_done(eng, n):
            if n == 0:
                eng.wait_ge(in_x, 16)
            elif n % 2:
                eng.wait_ge(x_done, NT * (n // 2 + 1))
            elif n == 2:
                eng.wait_ge(d_done, 1)
            elif n == 4:
                eng.wait_ge(f_done, NT)
            else:
                eng.wait_ge(acc_ok, 2 + KB[n // 2])

        def held_in(eng, n):
            eng.wait_ge(in_held[n], 16)

        def q_tiles(eng, u):
            if u == 0:
                for qt in range(TB):
                    with eng.Fori(0, B) as b:
                        yield b + qt * B, b, qt, (qt + 1) * P
            else:
                with eng.Fori(0, B) as b:
                    with eng.Fori(0, TB) as qt:
                        yield b * TB + qt, b, qt, S

        def load_count(l, e, side):
            before = 16 * (WB[l][side] + (4 if l == 3 else 0) + 1) - 8 * side
            return e * 8 + before

        def run_queues(eng, *lagged):
            def steps(e, k, i):
                for do, ahead in lagged:
                    if isinstance(e, int) and not 0 <= e + ahead < E0:
                        continue
                    do(e + ahead, (k + ahead) % 4, i + (k + ahead) // 4)

            for e in range(-max(ahead for _, ahead in lagged), 0):
                steps(e, e, 0)
            with eng.Fori(0, E0 // 4 - 1) as i:
                for k in range(4):
                    steps(i * 4 + k, k, i)
            for k in range(4):
                steps(E0 - 4 + k, k, E0 // 4 - 1)

        def expert_order(eng, l, first, second):
            n = MOE[l]["E"] + (l == 2)

            def pair(e0, more):
                for side in range(2):
                    e = e0 + side
                    first(e, side, 1)
                    second(e, side, 0)
                    if side == 0 or more:
                        first(e + 1, 1 - side, 0)
                    second(e, side, 1)

            first(0, 0, 0)
            trips = n // 2 if n % 2 else n // 2 - 1
            with eng.Fori(0, trips) as i:
                pair(i * 2, True)
            if n % 2:
                first(n - 1, 0, 1)
                second(n - 1, 0, 0)
                second(n - 1, 0, 1)
            else:
                pair(n - 2, False)

        @block.sync
        def _(sp):
            first = 0
            for n, end in enumerate(ends):
                sp.dma_start(held[:, first:end], packed[:, first:end]).then_inc(in_held[n], 16)
                first = end
                if n == 0:
                    sp.dma_start(x_res[:, :].rearrange("p (t d) -> p t d", d=P),
                                 x.rearrange("(t p) d -> p t d", p=P)).then_inc(in_x, 16)
                    sp.dma_start(mask_i[:, :, :], mask).then_inc(in_mask, 16)

            def load(l, e, side):
                W = MOE[l]["W"]
                src = experts[l].rearrange("e p n -> p e n")[:, bass.ds(e, 1), :]
                sp.dma_start(wexp[:, side:side + 1, 0:W], src).then_inc(w_in[side], 16)

            sp.wait_ge(zeros_set, 1)
            for n in range(SLOTS // 1024):
                sp.dma_start(queued[n * 1024:(n + 1) * 1024, :].rearrange("(p t) d -> p (t d)", p=P),
                             xT_all[:, :]).then_inc(zeros_out, 16)

            def load0(e, side):
                src = experts[0].rearrange("e p n -> p e n")[:, bass.ds(e, 1), :]
                sp.dma_start(W0[side].unsqueeze(1), src).then_inc(w0_in[side], 16)

            def load_queue(e, side):
                src = queued.rearrange("(e p) d -> p e d", p=P)[:, bass.ds(e, 1), :]
                sp.dma_start(D["xin"][:, side * P:(side + 1) * P].unsqueeze(1), src).then_inc(d_in[side], 16)

            def store_answer(e, side):
                sp.wait_ge(d_y, e + 3)
                dst = answers.rearrange("(e p) d -> p e d", p=P)[:, bass.ds(e, 1), :]
                sp.dma_start(dst, D["y"][:, side * P:(side + 1) * P].unsqueeze(1)).then_inc(d_stored[side], 16)

            def load_ahead(e, side):
                sp.wait_ge(d_O, e + 1)
                load0(e + 4, side)
                load_queue(e + 4, side)

            for side in range(4):
                if side == 2:
                    sp.wait_ge(ctx_ok, 1 + NT)
                load0(side, side)
            sp.wait_ge(scattered, 16 * 16)
            for side in range(4):
                load_queue(side, side)
            with sp.Fori(0, E0 // 4 - 1) as i:
                for k in range(4):
                    load_ahead(i * 4 + k, k)
                    store_answer(i * 4 + k, k)
            for k in range(4):
                store_answer(E0 - 4 + k, k)

            for l in range(1, NMOE):
                n = MOE[l]["E"] + (l == 2)
                if l == 3:
                    for side in range(2):
                        sp.wait_ge(ye_ps, 2 + KB[l])
                        load(l, side, side)
                    with sp.Fori(0, 3) as i:
                        for side in range(2):
                            sp.wait_ge(n_sq, i * 2 + (side + 1))
                            load(l, i * 2 + (side + 2), side)
                    sp.wait_ge(n_sq, 8)
                else:
                    sp.wait_ge(ye_ps, 2 + KB[l])
                for side in range(2):
                    load(l, side, side)
                with sp.Fori(0, (n - 2) // 2) as i:
                    for side in range(2):
                        sp.wait_ge(ye_ps, i * 4 + (2 + KB[l] + 2 * side + 2))
                        load(l, i * 2 + (side + 2), side)
                if n % 2:
                    sp.wait_ge(ye_ps, 2 + KB[l] + 2 * (n - 2))
                    load(l, n - 1, 0)
            block_done(sp, STAGES)
            sp.dma_start(out.rearrange("(t p) d -> p t d", p=P),
                         x_res[:, :].rearrange("p (t d) -> p t d", d=P)).then_inc(stored, 16)
            sp.wait_ge(stored, 16)

        @block.gpsimd
        def _(pool):
            step = Steps(pool, pool_step)
            half = w("neghalf")

            def carry(n):
                pool.tensor_tensor(pool_pad[:, n:n + 1], half[:, 0:1], half[:, 0:1], ALU.mult)

            def rsqrt(dst, src, ready, at, done):
                pool.wait_ge(ready, at)
                n = src.shape[-1]
                pool.tensor_tensor(dst, src, half[0:src.shape[0], 0:n], ALU.pow).then_inc(done, 1)

            held_in(pool, 0)

            def xattn(l):
                if l == 2:
                    for b in range(B):
                        rsqrt(rstd[0:KV, b, :], var[0:KV, b, :], kvar_ok, b + 1, krstd_ok)
                with pool.Fori(0, TB) as i:
                    for j in range(B):
                        rsqrt(rstd[:, j, 0:1], var[:, j, 0:1], x_stat, count(8 * l, i, j), x_rstd)
                    if l == 2:
                        for j in range(B):
                            rsqrt(rstd[:, j, :], var[:, j, :], qvar_ok, count(0, i, j), qrstd_ok)

            def selfattn(u):
                with pool.Fori(0, TB) as i:
                    for j in range(B):
                        rsqrt(rstd[:, j, 0:1], var[:, j, 0:1], a_stat, count(16 * u, i, j), a_rstd)
                    for j in range(B):
                        rsqrt(rstd[:, j, 0:1], var[:, j, 0:1], b_stat, count(8 * u, i, j), b_rstd)
                pool.wait_ge(qkv_ok, NT * (u + 1))
                for h in range(HS):
                    last = pool.tensor_scalar(kself[:, (HS + h) * S:(HS + h + 1) * S], k_all[:, S:2 * S],
                                              w("headmask", h, h + 1), None, ALU.mult)
                last.then_inc(kself1, 1)
                for o, b, qt, _ in q_tiles(pool, u):
                    pool.wait_ge(us_ps, o * HS + (LEAD + u * UNITS))
                    carry(4)
                    pool.tensor_copy(qcur, q_all[:, bass.ds(b * S + qt * P, P)]).then_inc(qcur_ok, 1)

            def moe_input(l):
                with pool.Fori(0, TB) as i:
                    if l in (0, 2):
                        for j in range(B):
                            pool.wait_ge(ctx_ok, 1 + NT * (l // 2 + 1))
                            carry(j)
                            pool.tensor_copy(cc[:, j, :], ctx_all[:, tile(i, j)]).then_inc(t_cc, 1)
                    for j in range(B):
                        rsqrt(rstd[:, j, 0:1], var[:, j, 0:1], m_stat, count(8 * l, i, j), m_rstd)
                    for j in range(B):
                        pool.wait_ge(m_xn if l == 0 else m_xT, count(8 * l, i, j))
                        carry(2 + j)
                        pool.tensor_copy(xT_all[:, tile(i, j)], (xn if l == 0 else xT)[:, j, :]).then_inc(m_copy, 1)

            def queues():
                pool.wait_ge(slots_ok, 1)
                pool.wait_ge(zeros_out, 16 * (SLOTS // 1024))
                pool.wait_ge(m_copy, NT)
                for k in range(2):
                    for t in range(NT):
                        pool.indirect_dma_start(
                            queued, bass.IndirectOffsetOnAxis(ap=slot_i[:, k * NT + t:k * NT + t + 1], axis=0),
                            xT_all[:, t * P:(t + 1) * P], None, bounds_check=SLOTS - 1, oob_is_err=False)\
                            .then_inc(scattered, 16)
                for side in range(4):
                    pool.wait_ge(d_stored[side], 16 * (1 + E0 // 4))
                for n in range(2 * NT):
                    pool.indirect_dma_start(
                        D["back"][:, n * P:(n + 1) * P], None, answers,
                        bass.IndirectOffsetOnAxis(ap=slot_i[:, 2 * NT + n:2 * NT + n + 1], axis=0))\
                        .then_inc(d_back[n // 4], 16)

            def norms3():
                held_in(pool, 4)
                pool.wait_ge(n_max, 8 + 1)
                gv = small[0:8, 0, 33:34]
                step.then(pool.tensor_tensor(gv, gv, half[0:8, 0:1], ALU.pow))
                pool.tensor_tensor(gv, gv, w("m3_gate_g"), ALU.mult).then_inc(n_pow, 1)
                step.then(pool.tensor_tensor(n_sum[:, :], n_sum[:, :], half[:, 0:1].broadcast_to([P, 40]), ALU.pow))
                pool.tensor_tensor(s1_all, s1_all, w("m3_g1"), ALU.mult)
                pool.tensor_tensor(s2_col, s2_col, w("m3_g2"), ALU.mult).then_inc(n_ok, 1)
                pool.wait_ge(n_ok, 1)

            def experts3():
                pool.wait_ge(n_s2, 2)
                with pool.Fori(0, 4) as i:
                    for side in range(2):
                        pool.wait_ge(w_in[side], i * 16 + 16 * (WB[3][side] + 4 + 1))
                        carry(5 + side)
                        pool.tensor_copy(s1_now[:, side, :], s1_all[:, bass.ds(i * 8 + side * 4, 4)])
                        pool.tensor_tensor(w2n[:, side, :].rearrange("p (c d) -> p c d", d=P),
                                           wexp[:, side, 512:1024].rearrange("p (c d) -> p c d", d=P),
                                           M["s2"][:, bass.ds(i * 256 + side * P, P)].unsqueeze(1).broadcast_to([P, 4, P]),
                                           ALU.mult).then_inc(w2n_ok, 1)

            for l in range(4):
                if STAGES > 2 * l:
                    xattn(l)
                if STAGES > 2 * l + 1:
                    if l == 1:
                        with pool.Fori(0, TB) as i:
                            for j in range(B):
                                rsqrt(rstd[:, j, 0:1], var[:, j, 0:1], a_stat, count(8, i, j), a_rstd)
                            for j in range(B):
                                rsqrt(rstd[:, j, 0:1], var[:, j, 0:1], m_stat, count(8, i, j), m_rstd)
                            for j in range(B):
                                pool.wait_ge(m_xT, count(8, i, j))
                                carry(2 + j)
                                pool.tensor_copy(xT_all[:, tile(i, j)], xT[:, j, :]).then_inc(m_copy, 1)
                        with pool.Fori(0, TB) as i:
                            for j in range(B):
                                rsqrt(rstd[:, j, 0:1], var[:, j, 0:1], f_stat, count(0, i, j), f_rstd)
                    elif l == 3:
                        norms3()
                        moe_input(l)
                        experts3()
                    else:
                        selfattn(l // 2)
                        moe_input(l)
                        if l == 0:
                            queues()

        @block.scalar
        def _(act):
            step = Steps(act, act_step)
            act.sem_inc(up_ok, LEAD)
            act.sem_inc(upT_act, LEAD)
            act.sem_inc(h_ok, 4)
            act.sem_inc(d_h, 2)
            act.sem_inc(sg_ok, 2)

            def copy_tile(ready, at, dst, src, done, func=ACT.Copy, **kw):
                act.wait_ge(ready, at)
                act.activation(dst, src, func, **kw).then_inc(done, 1)

            def xattn(l):
                c = XATTN[l]
                G, NH, dh = c["G"], c["H"], c["dh"]
                nb = NH // 4
                held_in(act, [0, 2, 3, 4][l])
                if l == 2:
                    for b in range(B):
                        act.wait_ge(kc_ok, b + 1)
                        act.activation(O[0:KV, b, :], kn[0:KV, b, :], ACT.Square).then_inc(ksq_ok, 1)
                act.wait_ge(kv_ps, l + 1)
                V = vx[:, 0:B * NH * (dh + 1)].rearrange("p (b h d) -> p b h d", b=B, d=dh + 1)
                for b in range(B):
                    first = 4 + 2 * b
                    last = act.activation(V[:, b, :, 0:dh],
                                          psum[0:KV, first * BANK:first * BANK + NH * dh].rearrange("p (h d) -> p h d", d=dh),
                                          ACT.Copy)
                last.then_inc(v_ok, 1)
                with act.Fori(0, TB) as i:
                    for j in range(B):
                        copy_tile(x_xTp, count(8 * l, i, j), xT[:, j, :], bank(4 * j, 0, P), x_xT)
                    if l == 2:
                        for j in range(B):
                            act.wait_ge(qc_ok, count(0, i, j))
                            act.activation(O[:, j, :], qn[:, j, :], ACT.Square).then_inc(qsq_ok, 1)
                        for j in range(B):
                            copy_tile(qnT_ps, count(0, i, j), qT[:, j, :], psum[:, (4 * j + 2) * BANK:(4 * j + 4) * BANK],
                                      qT_ok, ACT.Identity, scale=w("qn_w"), bias=w("qn_b"))
                    else:
                        for j in range(B):
                            copy_tile(q_ps, count(8 * l, i, j), qT[:, j, 0:G * P],
                                      psum[:, 4 * j * BANK:4 * j * BANK + G * P], qT_ok)
                    for j in range(B):
                        act.wait_ge(e_ok, count(8 * l, i, j))
                        act.activation(E[:, j, 0:NH * KV], E[:, j, 0:NH * KV], ACT.Exp,
                                       scale=1.0 if c["mask"] else dh ** -0.5).then_inc(p_ok, 1)
                    for j in range(B):
                        copy_tile(pT_ps, count(8 * l, i, j), PT[0:KV, j, 0:nb // 2 * BANK],
                                  psum[0:KV, 4 * j * BANK:(4 * j + nb // 2) * BANK], pT_act)
                    for j in range(B):
                        copy_tile(oT_ps, count(8 * l, i, j), OT[:, j, 0:G * P],
                                  psum[:, 4 * j * BANK:4 * j * BANK + G * P], oT_ok)
                    if l == 3:
                        for side in range(2):
                            act.wait_ge(w_in[side], i * 16 + 16 * (WB[3][side] + 1))
                            act.wait_ge(n_ps, i * 2 + (side + 1))
                            act.activation(sq[:, side, :], wexp[:, side, 0:1024], ACT.Square).then_inc(n_sq, 1)

            def selfattn(u):
                held_in(act, [1, 3][u])
                with act.Fori(0, TB) as i:
                    for j in range(B):
                        act.wait_ge(s_xTp, count(16 * u, i, j))
                        if u == 0:
                            act.activation(xT[:, j, :], bank(4 * j, 0, P), ACT.Identity,
                                           scale=w("s0_ln1_w"), bias=w("s0_ln1_b")).then_inc(s_xT, 1)
                        else:
                            act.activation(xT[:, j, :], bank(4 * j, 0, P), ACT.Copy,
                                           scale=w("s2_norm1")).then_inc(s_xT, 1)
                for o, b, qt, W in q_tiles(act, u):
                    base = u * UNITS
                    for h in range(HS + 1):
                        if h < HS:
                            act.wait_ge(um_ok, o * HS + (base + h + 1))
                            act.wait_ge(upT_ps, o * HS + (LEAD + base + h - 3))
                            act.activation(pself[:, (h % 4) * BANK:(h % 4) * BANK + W], bank(h % 4, 0, W), ACT.Exp,
                                           bias=small[:, 0, h:h + 1]).then_inc(up_ok, 1)
                        g = h - 1
                        if g >= 0 and g % 2 == 0:
                            act.wait_ge(upT_ps, o * HS + (LEAD + base + g + 1))
                            act.wait_ge(uo_ps, o * HS + (LEAD + base + g - 3))
                            act.activation(ptself[:, (g % 4) * BANK:(g % 4) * BANK + W], bank(4 + g % 2, 0, W),
                                           ACT.Copy).then_inc(upT_act, 1)

            def moe_input(l):
                held_in(act, [1, 2, 3, 4][l])
                with act.Fori(0, TB) as i:
                    if l in (0, 2):
                        for j in range(B):
                            copy_tile(t_ccT, count(8 * l, i, j), yb[:, j, :], bank(4 * j, 0, P), t_ccS)
                    for j in range(B):
                        act.wait_ge(m_xTp, count(8 * l, i, j))
                        src = bank(4 * j, 0, P)
                        if l == 0:
                            ins = act.activation(xT[:, j, :], src, ACT.Identity, scale=w("s0_ln2_w"), bias=w("s0_ln2_b"))
                        elif l == 2:
                            ins = act.activation(xT[:, j, :], src, ACT.Copy, scale=w("s2_norm2"))
                        else:
                            ins = act.activation(xT[:, j, :], src, ACT.Copy)
                        ins.then_inc(m_xT, 1)

            def two_token():
                held_in(act, 2)
                with act.Fori(0, TB) as i:
                    for j in range(B):
                        copy_tile(s_xTp, count(8, i, j), xT[:, j, :], bank(4 * j, 0, P), s_xT)
                    act.wait_ge(t1_e, i + 1)
                    act.activation(H["sc"][:, 0:16], H["sc"][:, 0:16], ACT.Exp, scale=32 ** -0.5).then_inc(t1_p, 1)
                    for j in range(B):
                        copy_tile(t_ccT, count(8, i, j), xT[:, j, :], bank(4 * j, 0, P), t_ccS)
                    for j in range(B):
                        copy_tile(m_xTp, count(8, i, j), xT[:, j, :], bank(4 * j, 0, P), m_xT)

            def gating(l):
                E_ = MOE[l]["E"]
                if l in (0, 2):
                    act.wait_ge(g_sub, [1, 0, 2][l])
                    act.activation(M["gc"][:, 0:NT * E_], M["gc"][:, 0:NT * E_], ACT.Exp).then_inc(g_exp, 1)
                if l == 2:
                    act.wait_ge(g_sub, 3)
                    act.activation(M["gc"][:, 0:NT * E_], M["gc"][:, 0:NT * E_], ACT.Exp).then_inc(g_exp, 1)
                if l != 2:
                    act.wait_ge(gT_ps, [1, 2, 0, 3][l])
                    act.activation(gatesT[0:E_, :], psum[0:E_, 0:2 * BANK], ACT.Copy).then_inc(gT_ok, 1)

            def experts(l):
                m = MOE[l]
                n, func = m["E"], m["act"]

                def hidden(e, side, b):
                    if l == 2:
                        for c in range(2):
                            act.wait_ge(h_ps, e * 8 + (HPB[l] + 4 * b + c + 1))
                            act.wait_ge(h2_ok, e * 4 + (2 * b + c + 1))
                            act.activation(sg[:, b, c * BANK:(c + 1) * BANK], bank(c, 0, BANK), func).then_inc(sg_ok, 1)
                        return
                    for c in range(4):
                        act.wait_ge(h_ps, e * 8 + (HPB[l] + 4 * b + c + 1))
                        if c == 0:
                            act.wait_ge(ye_ps, e * 2 + (2 + KB[l] + b - 1))
                        kw = dict(bias=wexp[:, side, 1024 + c:1025 + c])
                        if l == 3:
                            if c == 0:
                                act.wait_ge(w2n_ok, e + 1)
                            kw["scale"] = s1_now[:, side, c:c + 1]
                        act.activation(hT[:, b, c * BANK:(c + 1) * BANK], bank(c, 0, BANK), func, **kw).then_inc(h_ok, 1)

                act.preload_act_table(func)
                with act.Fori(0, n // 2) as i:
                    for side in range(2):
                        for b in range(B):
                            hidden(i * 2 + side, side, b)
                if l == 2:
                    for b in range(B):
                        hidden(n, 0, b)
                act.preload_act_table(ACT.Exp)

            def norms3():
                held_in(act, 4)
                block_done(act, 7)
                act.activation(M["gv"][0:8, :], w("m3_gate_v"), ACT.Square, accum_out=small[0:8, 0, 32:33]).then_inc(n_gv, 1)
                act.wait_ge(n_gvT, 1)
                act.activation(M["gwT"], bank(7, 0, 8), ACT.Copy).then_inc(n_gv, 1)

            def norm_rows3():
                for n in range(2):
                    act.wait_ge(n_row, n + 1)
                    act.activation(M["s2"][:, n * BANK:(n + 1) * BANK], bank(4 + n, 0, BANK), ACT.Copy).then_inc(n_s2, 1)

            def experts0():
                def activate(e, side, i):
                    act.wait_ge(d_H, e + 1)
                    act.wait_ge(w0_in[side], i * 16 + 16)
                    for c in range(4):
                        last = act.activation(D["h"][:, side % 2 * BANK + c * P:side % 2 * BANK + (c + 1) * P],
                                              bank(2 + side % 2, c * P, (c + 1) * P), ACT.Gelu,
                                              bias=W0[side][:, 1024 + c:1025 + c])
                    last.then_inc(d_h, 1)

                act.preload_act_table(ACT.Gelu)
                run_queues(act, (activate, 0))
                act.preload_act_table(ACT.Exp)

            act.preload_act_table(ACT.Exp)
            for l in range(4):
                if STAGES > 2 * l:
                    xattn(l)
                if STAGES > 2 * l + 1:
                    if l == 1:
                        two_token()
                    elif l == 3:
                        norms3()
                        moe_input(l)
                        norm_rows3()
                    else:
                        selfattn(l // 2)
                        moe_input(l)
                    gating(l)
                    experts(l) if l else experts0()

        @block.vector
        def _(dve):
            step = Steps(dve, dve_step)
            dve.sem_inc(upT_dve, LEAD)
            dve.sem_inc(h2_ok, 4)
            dve.sem_inc(acc_ok, 2)
            dve.sem_inc(ctx_ok, 1)
            dve.sem_inc(d_xe, 2)
            dve.sem_inc(d_y, 2)
            for side in range(4):
                dve.sem_inc(d_stored[side], 16)
            dve.memset(xT_all[:, :], 0.0).then_inc(zeros_set, 1)
            held_in(dve, 0)
            dve.tensor_copy(ident_bf[:, :], w("ident"))
            dve.tensor_copy(later_bf[:, :], w("later")).then_inc(const_ok, 1)
            dve.wait_ge(in_mask, 16)
            step.then(dve.tensor_copy(A["ext"], mask_i[:, :, :].rearrange("p b n -> p (b n)")))
            step.then(dve.tensor_scalar(A["ext"], A["ext"], 1.0, -FMIN, ALU.subtract, ALU.mult))

            def carry(j):
                dve.memset(small[:, j, 63:64], 0.0)

            def moments(j, src, done, rms=False, eps=EPS_LN):
                carry(j)
                step.then(dve.bn_stats(stats[:, j, :], src))
                carry(j)
                step.then(dve.bn_aggr(mv[:, j, :], stats[:, j, :]))
                v = mv[:, j, 1:2]
                if rms:
                    v = var[:, j, 1:2]
                    step.then(dve.scalar_tensor_tensor(v, mv[:, j, 0:1], mv[:, j, 0:1], mv[:, j, 1:2], ALU.mult, ALU.add))
                dve.tensor_scalar(var[:, j, 0:1], v, eps, None, ALU.add).then_inc(done, 1)

            def scaled(j, dst, src, rms=False):
                if rms:
                    return dve.tensor_scalar(dst, src, rstd[:, j, 0:1], None, ALU.mult)
                return dve.tensor_scalar(dst, src, mv[:, j, 0:1], rstd[:, j, 0:1], ALU.subtract, ALU.mult)

            def heads_centre(rows, j, dst, src, sm, done):
                step.then(dve.tensor_reduce(sm[0:rows, j, 0:16], src, AX_X, ALU.add))
                step.then(dve.tensor_scalar(sm[0:rows, j, 16:32], sm[0:rows, j, 0:16], 1.0 / 64, None, ALU.mult))
                dve.tensor_tensor(dst, src, sm[0:rows, j, 16:32].unsqueeze(2).broadcast_to([rows, 16, 64]),
                                  ALU.subtract).then_inc(done, 1)

            def heads_var(rows, j, squares, sm, done):
                step.then(dve.tensor_reduce(sm[0:rows, j, 32:48], squares, AX_X, ALU.add))
                dve.tensor_scalar(var[0:rows, j, :], sm[0:rows, j, 32:48], 1.0 / 64, EPS_LN, ALU.mult, ALU.add)\
                   .then_inc(done, 1)

            def by_head(v):
                return v.rearrange("p (h d) -> p h d", d=64)

            def xattn(l):
                c = XATTN[l]
                G, NH, dh = c["G"], c["H"], c["dh"]
                nb = NH // 4
                block_done(dve, 2 * l)
                held_in(dve, [0, 2, 3, 4][l])
                K = kbd[:, 0:B * NH * KV].rearrange("p (b h k) -> p b h k", b=B, k=KV)
                if c["qk_norm"]:
                    dve.wait_ge(kv_ps, l + 1)
                    for b in range(B):
                        heads_centre(KV, b, by_head(kn[0:KV, b, :]),
                                     by_head(psum[0:KV, 2 * b * BANK:(2 * b + 2) * BANK]), small, kc_ok)
                    for b in range(B):
                        dve.wait_ge(ksq_ok, b + 1)
                        heads_var(KV, b, by_head(O[0:KV, b, :]), small, kvar_ok)
                    for b in range(B):
                        dve.wait_ge(krstd_ok, b + 1)
                        dve.tensor_tensor(by_head(kn[0:KV, b, :]), by_head(kn[0:KV, b, :]),
                                          rstd[0:KV, b, :].unsqueeze(2).broadcast_to([KV, 16, 64]), ALU.mult)\
                           .then_inc(kn_ok, 1)
                    dve.wait_ge(kT_ps, 1)
                    for n in range(3):
                        cols = min(3, G - 3 * n) * 2 * KV
                        last = dve.tensor_scalar(kaff[:, n * 462:n * 462 + cols], bank(n, 0, cols),
                                                 w("kn_w"), w("kn_b"), ALU.mult, ALU.add)
                    step.then(last)
                else:
                    dve.wait_ge(kv_ps, l + 1)
                for h in range(NH):
                    g = h * dh // P
                    src = kaff[:, g * 154:g * 154 + 154] if c["qk_norm"] else bank(g // 3, g % 3 * 154, g % 3 * 154 + 154)
                    own = w("headmask", h, h + 1) if dh == DS else w("halfmask", h % 2, h % 2 + 1)
                    dve.tensor_scalar(K[:, :, h, :], src.rearrange("p (b k) -> p b k", b=B), own, None, ALU.mult)
                V = vx[:, 0:B * NH * (dh + 1)].rearrange("p (n d) -> p n d", d=dh + 1)
                dve.memset(V[:, :, dh:dh + 1], 1.0).then_inc(k_ok, 1)

                with dve.Fori(0, TB) as i:
                    step.loop(i, XSTEPS[l])
                    for j in range(B):
                        moments(j, x_res[:, tile(i, j)], x_stat)
                    for j in range(B):
                        dve.wait_ge(x_rstd, count(8 * l, i, j))
                        scaled(j, xn[:, j, :], x_res[:, tile(i, j)]).then_inc(x_xn, 1)
                    if c["qk_norm"]:
                        for j in range(B):
                            dve.wait_ge(q_ps, count(8 * l, i, j))
                            heads_centre(P, j, by_head(qn[:, j, :]), by_head(psum[:, 4 * j * BANK:(4 * j + 2) * BANK]),
                                         small, qc_ok)
                        for j in range(B):
                            dve.wait_ge(qsq_ok, count(0, i, j))
                            heads_var(P, j, by_head(O[:, j, :]), small, qvar_ok)
                        for j in range(B):
                            dve.wait_ge(qrstd_ok, count(0, i, j))
                            dve.tensor_tensor(by_head(qn[:, j, :]), by_head(qn[:, j, :]),
                                              rstd[:, j, :].unsqueeze(2).broadcast_to([P, 16, 64]), ALU.mult)\
                               .then_inc(qn_ok, 1)
                    for j in range(B):
                        dve.wait_ge(sc_ps, count(8 * l, i, j))
                        raw = psum[:, 4 * j * BANK:(4 * j + nb) * BANK].rearrange("p (c n) -> p c n", n=BANK)[:, :, 0:4 * KV]
                        e = E[:, j, 0:NH * KV]
                        top = small[:, j, 0:NH]
                        if c["mask"]:
                            step.then(dve.scalar_tensor_tensor(
                                e.rearrange("p (c n) -> p c n", c=nb), raw, dh ** -0.5,
                                ext[:, j, :].unsqueeze(1).broadcast_to([P, nb, 4 * KV]), ALU.mult, ALU.add))
                            eh = e.rearrange("p (h k) -> p h k", k=KV)
                            step.then(dve.tensor_reduce(top, eh, AX_X, ALU.max))
                            dve.tensor_tensor(eh, eh, top.unsqueeze(2).broadcast_to([P, NH, KV]), ALU.subtract)\
                               .then_inc(e_ok, 1)
                        else:
                            rawh = raw.rearrange("p c (h k) -> p c h k", k=KV)
                            toph = top.rearrange("p (c h) -> p c h", c=nb)
                            step.then(dve.tensor_reduce(toph, rawh, AX_X, ALU.max))
                            dve.tensor_tensor(e.rearrange("p (c h k) -> p c h k", c=nb, k=KV), rawh,
                                              toph.unsqueeze(3).broadcast_to([P, nb, 4, KV]), ALU.subtract)\
                               .then_inc(e_ok, 1)
                    for j in range(B):
                        dve.wait_ge(pT_ps, count(8 * l, i, j))
                        lo = nb // 2 * BANK
                        dve.tensor_copy(PT[0:KV, j, lo:nb * BANK], psum[0:KV, 4 * j * BANK + lo:(4 * j + nb) * BANK])\
                           .then_inc(pT_dve, 1)
                    for j in range(B):
                        dve.wait_ge(o_ps, count(8 * l, i, j))
                        raw = psum[:, 4 * j * BANK:(4 * j + nb) * BANK].rearrange("p (c n) -> p c n", n=BANK)
                        raw = raw[:, :, 0:4 * (dh + 1)].rearrange("p c (h d) -> p c h d", d=dh + 1)
                        inv = small[:, j, 16:16 + NH].rearrange("p (c h) -> p c h", c=nb)
                        step.then(dve.reciprocal(inv.unsqueeze(3), raw[:, :, :, dh:dh + 1]))
                        dve.tensor_tensor(O[:, j, 0:G * P].rearrange("p (c h d) -> p c h d", c=nb, d=dh),
                                          raw[:, :, :, 0:dh], inv.unsqueeze(3).broadcast_to([P, nb, 4, dh]), ALU.mult)\
                           .then_inc(o_ok, 1)
                    for j in range(B):
                        dve.wait_ge(y_ps, count(8 * l, i, j))
                        t = x_res[:, tile(i, j)]
                        last = dve.tensor_tensor(t, t, bank(4 * j + 2, 0, P), ALU.add)
                        if c["bias"]:
                            step.then(last)
                            last = dve.tensor_tensor(t, t, w(f"x{l}_bo"), ALU.add)
                        last.then_inc(x_done, 1)
                    if l == 3:
                        for side in range(2):
                            dve.wait_ge(n_ps, i * 2 + (side + 2))
                            raw = bank(4 * side + 3, 0, 5)
                            dve.tensor_scalar(s1_all[:, bass.ds(i * 8 + side * 4, 4)], raw[:, 0:4], 1e-24, None, ALU.max)
                            dve.tensor_scalar(s2_col[:, bass.ds(i * 2 + side, 1)], raw[:, 4:5], 1e-24, None, ALU.max)\
                               .then_inc(n_max, 1)
                step.end(TB)
                dve.wait_ge(x_done, NT * (l + 1))

            def selfattn(u):
                l = 2 * u
                held_in(dve, [1, 3][u])
                if u == 0:
                    dve.wait_ge(zeros_out, 16 * (SLOTS // 1024))
                ones = v_all.rearrange("p (n d) -> p n d", d=DS + 1)[:, :, DS:DS + 1]
                step.then(dve.memset(ones, 1.0))
                with dve.Fori(0, TB) as i:
                    step.loop(i, [10, 12][u])
                    for j in range(B):
                        moments(j, x_res[:, tile(i, j)], a_stat)
                    for j in range(B):
                        dve.wait_ge(a_rstd, count(8 * l, i, j))
                        step.then(scaled(j, r_res[:, tile(i, j)], x_res[:, tile(i, j)]))
                        moments(j, r_res[:, tile(i, j)], b_stat, rms=(u == 1), eps=[EPS_LN, 1e-6][u])
                    for j in range(B):
                        dve.wait_ge(b_rstd, count(8 * u, i, j))
                        scaled(j, xn[:, j, :], r_res[:, tile(i, j)], rms=(u == 1)).then_inc(b_xn, 1)
                    for j in range(B):
                        dve.wait_ge(qkv_ps, count(8 * l, i, j))
                        qp, kp, vp = (bank(4 * j + 1, n * P, n * P + P) for n in range(3))
                        vd = v_all[:, bass.ds(i * 144 + j * 576, 144)].rearrange("p (h d) -> p h d", d=DS + 1)[:, :, 0:DS]
                        vp = vp.rearrange("p (h d) -> p h d", d=DS)
                        if u == 0:
                            dve.tensor_scalar(q_all[:, tile(i, j)], qp, w("s0_q_b"), DS ** -0.5, ALU.add, ALU.mult)
                            dve.tensor_scalar(k_all[:, tile(i, j)], kp, w("s0_k_b"), None, ALU.add)
                            last = dve.tensor_tensor(vd, vp, w("s0_v_b").rearrange("p (h d) -> p h d", d=DS), ALU.add)
                        else:
                            dve.tensor_scalar(q_all[:, tile(i, j)], qp, DS ** -0.5, None, ALU.mult)
                            dve.tensor_copy(k_all[:, tile(i, j)], kp)
                            last = dve.tensor_copy(vd, vp)
                        last.then_inc(qkv_ok, 1)
                step.end(TB)
                dve.wait_ge(qkv_ok, NT * (u + 1))
                for h in range(HS):
                    last = dve.tensor_scalar(kself[:, h * S:(h + 1) * S], k_all[:, 0:S],
                                             w("headmask", h, h + 1), None, ALU.mult)
                last.then_inc(kself0, 1)
                for o, b, qt, W in q_tiles(dve, u):
                    base = u * UNITS
                    for h in range(HS + 1):
                        if h < HS:
                            dve.wait_ge(us_ps, o * HS + (LEAD + base + h + 1))
                            dve.tensor_reduce(small[:, 0, h:h + 1], bank(h % 4, 0, W), AX_X, ALU.max, negate=True)\
                               .then_inc(um_ok, 1)
                        g = h - 1
                        if g > 0 and g % 2:
                            dve.wait_ge(upT_ps, o * HS + (LEAD + base + g + 1))
                            dve.wait_ge(uo_ps, o * HS + (LEAD + base + g - 3))
                            dve.tensor_copy(ptself[:, (g % 4) * BANK:(g % 4) * BANK + W], bank(5, 0, W)).then_inc(upT_dve, 1)
                    dve.wait_ge(uo_ps, o * HS + (LEAD + base + HS))
                    raw = bank(6, 0, HS * (DS + 1)).rearrange("p (h d) -> p h d", d=DS + 1)
                    inv = small[:, 1, 0:HS].unsqueeze(2)
                    dve.reciprocal(inv, raw[:, :, DS:DS + 1]).then_inc(inv_ok, 1)
                    dve.wait_ge(inv_ok, o + (NT * u + 1))
                    dve.tensor_tensor(ctx_all[:, bass.ds(b * S + qt * P, P)].rearrange("p (h d) -> p h d", d=DS),
                                      raw[:, :, 0:DS], inv.broadcast_to([P, HS, DS]), ALU.mult).then_inc(ctx_ok, 1)

            def logits_out(l, i):
                E_ = MOE[l]["E"]
                for j in range(B):
                    dve.wait_ge(lg_ps, count(8 * l, i, j))
                    dst = logits[:, bass.ds(i * E_ + j * TB * E_, E_)]
                    src = bank(4 * j + 2, 0, E_)
                    if l == 3:
                        dve.tensor_tensor(dst, src, w("m3_gate_b"), ALU.add).then_inc(lg_ok, 1)
                    else:
                        dve.tensor_scalar(dst, src, 1.0, None, ALU.mult).then_inc(lg_ok, 1)

            def moe_input(l):
                held_in(dve, [1, 2, 3, 4][l])
                with dve.Fori(0, TB) as i:
                    step.loop(i, [10, 0, 10, 4][l])
                    for j in range(B):
                        x_t, r_t = x_res[:, tile(i, j)], r_res[:, tile(i, j)]
                        if l == 3:
                            moments(j, x_t, m_stat)
                            continue
                        dve.wait_ge(t_y, count(8 * l, i, j))
                        step.then(dve.tensor_tensor(r_t, r_t, bank(4 * j + 1, 0, P), ALU.add))
                        if l == 0:
                            step.then(dve.tensor_tensor(r_t, r_t, w("s0_o_b"), ALU.add))
                        step.then(dve.tensor_tensor(x_t, x_t, r_t, ALU.add))
                        moments(j, r_t, m_stat, rms=(l == 2), eps=[EPS_LN, 0, 1e-6][l])
                    for j in range(B):
                        dve.wait_ge(m_rstd, count(8 * l, i, j))
                        src = x_res if l == 3 else r_res
                        scaled(j, xn[:, j, :], src[:, tile(i, j)], rms=(l == 2)).then_inc(m_xn, 1)
                    logits_out(l, i)
                step.end(TB)

            def two_token():
                held_in(dve, 2)
                sc = H["sc"]
                heads = lambda v: v.rearrange("p (h d) -> p h d", d=32)
                with dve.Fori(0, TB) as i:
                    step.loop(i, 33)
                    for j in range(B):
                        moments(j, x_res[:, tile(i, j)], a_stat)
                    for j in range(B):
                        dve.wait_ge(a_rstd, count(8, i, j))
                        scaled(j, xn[:, j, :], x_res[:, tile(i, j)]).then_inc(h0_ok, 1)
                        step.then(scaled(j, r_res[:, tile(i, j)], x_res[:, tile(i, j)]))
                    for j in range(B):
                        dve.wait_ge(qkv_ps, count(8, i, j))
                        step.then(dve.tensor_tensor(qkv[:, j, :], bank(4 * j + 1, 0, 384), w("h_bqkv"), ALU.add))
                    for j in range(B):
                        step.then(dve.tensor_tensor(prod[:, j * 256:j * 256 + 256].rearrange("p (b n) -> p b n", b=B),
                                                    qkv[:, j, 0:P].unsqueeze(1).broadcast_to([P, B, P]),
                                                    qkv[:, :, P:2 * P], ALU.mult))
                    step.then(dve.tensor_reduce(sc[:, 0:16], heads(prod), AX_X, ALU.add))
                    s4 = sc[:, 0:16].rearrange("p (q k h) -> p q k h", q=2, k=2)
                    top = sc[:, 16:24].rearrange("p (q h) -> p q h", q=2)
                    step.then(dve.tensor_tensor(top, s4[:, :, 0, :], s4[:, :, 1, :], ALU.max))
                    dve.tensor_tensor(s4, s4, top.unsqueeze(2).broadcast_to([P, 2, 2, 4]), ALU.subtract).then_inc(t1_e, 1)
                    dve.wait_ge(t1_p, i + 1)
                    step.then(dve.tensor_tensor(top, s4[:, :, 0, :], s4[:, :, 1, :], ALU.add))
                    step.then(dve.reciprocal(top, top))
                    step.then(dve.tensor_tensor(s4, s4, top.unsqueeze(2).broadcast_to([P, 2, 2, 4]), ALU.mult))
                    for j in range(B):
                        for k in range(B):
                            step.then(dve.tensor_tensor(heads(prod[:, k * P:k * P + P]), heads(qkv[:, k, 2 * P:3 * P]),
                                                        s4[:, j, k, :].unsqueeze(2).broadcast_to([P, 4, 32]), ALU.mult))
                        dve.tensor_tensor(cc[:, j, :], prod[:, 0:P], prod[:, P:2 * P], ALU.add).then_inc(t1_av, 1)
                        dve.wait_ge(t1_av, count(0, i, j))
                    for j in range(B):
                        r_t = r_res[:, tile(i, j)]
                        dve.wait_ge(t_y, count(8, i, j))
                        step.then(dve.tensor_tensor(r_t, r_t, bank(4 * j + 1, 0, P), ALU.add))
                        step.then(dve.tensor_tensor(r_t, r_t, w("h_bo"), ALU.add))
                        moments(j, r_t, m_stat)
                    for j in range(B):
                        r_t = r_res[:, tile(i, j)]
                        dve.wait_ge(m_rstd, count(8, i, j))
                        step.then(scaled(j, yb[:, j, :], r_t))
                        step.then(dve.tensor_tensor(yb[:, j, :], yb[:, j, :], w("h_g1"), ALU.mult))
                        dve.tensor_tensor(yb[:, j, :], yb[:, j, :], w("h_be1"), ALU.add).then_inc(m_xn, 1)
                        dve.wait_ge(m_xn, count(8, i, j))
                        step.then(dve.tensor_scalar(r_t, yb[:, j, :], 1.0, None, ALU.mult))
                    logits_out(1, i)
                step.end(TB)

            def norms3():
                dve.wait_ge(n_gv, 1)
                dve.tensor_scalar(small[0:8, 0, 33:34], small[0:8, 0, 32:33], 1e-24, None, ALU.max).then_inc(n_max, 1)
                dve.wait_ge(n_pow, 1)
                dve.tensor_scalar(M["gv"][0:8, :], w("m3_gate_v"), small[0:8, 0, 33:34], None, ALU.mult).then_inc(n_pow, 1)

            def norm_rows3():
                dve.wait_ge(n_ok, 1)
                for n in range(2):
                    for e in range(4 * n, 4 * n + 4):
                        last = dve.tensor_scalar(M["diag"][:, e * P:(e + 1) * P], w("ident"), s2_col[:, e:e + 1], None, ALU.mult)
                    last.then_inc(n_diag, 1)

            def top_mask(dst, src, n, shape):
                bc = lambda v: v.unsqueeze(2).broadcast_to(shape)
                best = small[:, 0, 0:NT] if n == 0 else small[:, 0, 8:16]
                first = small[:, 0, 16:24]
                step.then(dve.tensor_reduce(best, src, AX_X, ALU.max))
                step.then(dve.tensor_tensor(dst, src, bc(best), ALU.is_equal))
                step.then(dve.tensor_tensor(dst, dst, w("firstness", 0, shape[2]).unsqueeze(1).broadcast_to(shape), ALU.mult))
                step.then(dve.tensor_reduce(first, dst, AX_X, ALU.max))
                step.then(dve.tensor_tensor(dst, dst, bc(first), ALU.is_equal))

            def gating(l):
                E_ = MOE[l]["E"]
                shape = [P, NT, E_]
                n = NT * E_
                bc = lambda v: v.unsqueeze(2).broadcast_to(shape)
                t3 = lambda v: v[:, 0:n].rearrange("p (t e) -> p t e", e=E_)
                LG, ga, gb, gc = t3(logits), t3(M["ga"]), t3(M["gb"]), t3(M["gc"])
                G_ = gates[:, :, 0:E_]
                total = small[:, 0, 24:32]
                dve.wait_ge(lg_ok, NT * (l + 1))
                if l == 1:
                    top_mask(ga, LG, 0, shape)
                    dve.tensor_copy(G_, ga).then_inc(gate_ok, 1)
                elif l == 3:
                    top_mask(ga, LG, 0, shape)
                    step.then(dve.scalar_tensor_tensor(M["gc"][:, 0:n], M["ga"][:, 0:n], FMIN, logits[:, 0:n], ALU.mult, ALU.add))
                    top_mask(gb, gc, 1, shape)
                    dve.tensor_tensor(G_, ga, gb, ALU.add).then_inc(gate_ok, 1)
                else:
                    m1, m2 = (M["m12"][:, k * n:k * n + n] for k in range(2))
                    top_mask(t3(m1), LG, 0, shape)
                    step.then(dve.scalar_tensor_tensor(M["gc"][:, 0:n], m1, FMIN, logits[:, 0:n], ALU.mult, ALU.add))
                    top_mask(t3(m2), gc, 1, shape)
                    dve.tensor_tensor(gc, LG, bc(small[:, 0, 0:NT]), ALU.subtract).then_inc(g_sub, 1)
                    dve.wait_ge(g_exp, [1, 0, 2][l])
                    step.then(dve.tensor_reduce(total, gc, AX_X, ALU.add))
                    step.then(dve.reciprocal(total, total))
                    step.then(dve.tensor_tensor(gc, gc, bc(total), ALU.mult))
                if l == 0:
                    m12 = M["m12"].rearrange("p (k t e) -> p k t e", k=2, t=NT)
                    pre = M["pre"].rearrange("p (k t e) -> p k t e", k=2, t=NT)
                    step.then(dve.memset(pre[:, :, 0, :], 0.0))
                    for t in range(1, NT):
                        step.then(dve.tensor_tensor(pre[:, :, t, :], pre[:, :, t - 1, :], m12[:, :, t - 1, :], ALU.add))
                    dve.tensor_tensor(M["tot"], pre[:, 0, NT - 1, :], m12[:, 0, NT - 1, :], ALU.add).then_inc(g_m, 1)
                    dve.wait_ge(g_loc, 1)
                    step.then(dve.scalar_tensor_tensor(M["mk"], bank(0, 0, 2 * n), float(CAPACITY), M["m12"], ALU.is_le, ALU.mult))
                    q3 = lambda v: v.rearrange("p (n e) -> p n e", e=E_)
                    place, kept, to = (D["slot"][:, a:a + 16] for a in (0, 16, 32))
                    step.then(dve.tensor_tensor(q3(D["loc"]), q3(bank(0, 0, 2 * n)),
                                                w("queue").unsqueeze(1).broadcast_to([P, 2 * NT, E_]), ALU.add))
                    step.then(dve.tensor_tensor(D["loc"], D["loc"], M["mk"], ALU.mult))
                    step.then(dve.tensor_reduce(place, q3(D["loc"]), AX_X, ALU.add))
                    step.then(dve.tensor_reduce(kept, q3(M["mk"]), AX_X, ALU.add))
                    step.then(dve.tensor_scalar(to, kept, -float(DROPPED), float(DROPPED), ALU.mult, ALU.add))
                    step.then(dve.tensor_tensor(to, to, place, ALU.add))
                    dve.tensor_copy(slot_i[:, 16:32], place)
                    dve.tensor_copy(slot_i[:, 0:16], to).then_inc(slots_ok, 1)
                    step.then(dve.tensor_tensor(M["ga"], M["mk"][:, 0:n], M["mk"][:, n:2 * n], ALU.add))
                    step.then(dve.tensor_tensor(M["ga"], M["ga"], M["gc"], ALU.mult))
                    step.then(dve.tensor_reduce(total, ga, AX_X, ALU.add))
                    step.then(dve.tensor_scalar(total, total, float(np.finfo(np.float32).eps), None, ALU.max))
                    step.then(dve.reciprocal(total, total))
                    step.then(dve.tensor_scalar(total, total, 0.8, None, ALU.mult))
                    dve.tensor_tensor(G_, ga, bc(total), ALU.mult).then_inc(gate_ok, 1)
                    dve.wait_ge(gate_ok, 1)
                    mk4 = M["mk"].rearrange("p (k t e) -> p k t e", k=2, t=NT)
                    for k in range(2):
                        step.then(dve.tensor_tensor(mk4[:, k], mk4[:, k], G_, ALU.mult))
                    step.then(dve.tensor_reduce(D["slot"][:, 48:64], q3(M["mk"]), AX_X, ALU.add))
                if l == 2:
                    step.then(dve.tensor_reduce(small[:, 0, 0:NT], gc, AX_X, ALU.max))
                    dve.tensor_tensor(gc, gc, bc(small[:, 0, 0:NT]), ALU.subtract).then_inc(g_sub, 1)
                    dve.wait_ge(g_exp, 3)
                    step.then(dve.tensor_tensor(M["ga"][:, 0:n], m1, m2, ALU.add))
                    step.then(dve.tensor_tensor(ga, ga, gc, ALU.mult))
                    step.then(dve.tensor_reduce(total, ga, AX_X, ALU.add))
                    step.then(dve.reciprocal(total, total))
                    step.then(dve.tensor_tensor(G_, ga, bc(total), ALU.mult))
                    step.then(dve.memset(gates[:, :, E_:E_ + 1], 1.0))
                if l != 2:
                    acc = r_res if l == 1 else x_res
                    dve.wait_ge(b2_ps, [1, 2, 0, 3][l])
                    dve.wait_ge(gate_ok, [1, 2, 0, 3][l])
                    dve.tensor_tensor(acc[:, :], acc[:, :], psum[:, 2 * BANK:4 * BANK], ALU.add).then_inc(b2_ok, 1)
                    dve.wait_ge(b2_ok, [1, 2, 0, 3][l])

            def experts(l):
                acc = r_res if l == 1 else x_res
                gflat = gates[:, :, :].rearrange("p t e -> p (t e)")

                def product(e, side, b):
                    if l != 2:
                        return
                    for c in range(2):
                        dve.wait_ge(sg_ok, e * 4 + (2 + 2 * b + c + 1))
                        dve.wait_ge(h_ps, e * 8 + (HPB[l] + 4 * b + 2 + c + 1))
                        if c == 0:
                            dve.wait_ge(ye_ps, e * 2 + (2 + KB[l] + b - 1))
                        dve.tensor_tensor(hT[:, b, c * BANK:(c + 1) * BANK], sg[:, b, c * BANK:(c + 1) * BANK],
                                          bank(2 + c, 0, BANK), ALU.mult).then_inc(h2_ok, 1)

                def gather(e, side, b):
                    dve.wait_ge(ye_ps, e * 2 + (2 + KB[l] + b + 1))
                    dve.wait_ge(acc_ok, e * 2 + (2 + KB[l] + b - 1))
                    for t in range(TB):
                        a = acc[:, b * S + t * P:b * S + t * P + P]
                        last = dve.scalar_tensor_tensor(a, bank(4 + b, t * P, t * P + P),
                                                        gflat[:, bass.ds(e + (b * TB + t) * 16, 1)], a, ALU.mult, ALU.add)
                    last.then_inc(acc_ok, 1)

                expert_order(dve, l, product, gather)
                dve.wait_ge(acc_ok, 2 + KB[l + 1])

            def experts0():
                def features(e, side, i):
                    dve.wait_ge(d_T, e + 1)
                    dve.tensor_scalar(D["xe"][:, side % 2 * P:(side % 2 + 1) * P], bank(side % 2, 0, P),
                                      w("s0_ln2_w"), w("s0_ln2_b"), ALU.mult, ALU.add).then_inc(d_xe, 1)

                def answer(e, side, i):
                    dve.wait_ge(d_O, e + 1)
                    dve.wait_ge(d_stored[side], i * 16 + 16)
                    dve.tensor_copy(D["y"][:, side * P:(side + 1) * P], bank(4 + side % 2, 0, P)).then_inc(d_y, 1)

                run_queues(dve, (features, 2), (answer, 0))
                for n in range(2 * NT):
                    if n % 4 == 0:
                        dve.wait_ge(d_back[n // 4], 16 * 4)
                    a = x_res[:, n % NT * P:(n % NT + 1) * P]
                    last = dve.scalar_tensor_tensor(a, D["back"][:, n * P:(n + 1) * P], D["slot"][:, 48 + n:49 + n], a,
                                                    ALU.mult, ALU.add)
                    if n == NT - 1:
                        step.then(last)
                last.then_inc(d_done, 1)
                dve.wait_ge(d_done, 1)

            def last_norm():
                with dve.Fori(0, TB) as i:
                    step.loop(i, 10)
                    for j in range(B):
                        moments(j, r_res[:, tile(i, j)], f_stat)
                    for j in range(B):
                        r_t, x_t = r_res[:, tile(i, j)], x_res[:, tile(i, j)]
                        dve.wait_ge(f_rstd, count(0, i, j))
                        step.then(scaled(j, r_t, r_t))
                        step.then(dve.tensor_tensor(r_t, r_t, w("h_g2"), ALU.mult))
                        step.then(dve.tensor_tensor(r_t, r_t, w("h_be2"), ALU.add))
                        dve.tensor_tensor(x_t, x_t, r_t, ALU.add).then_inc(f_done, 1)
                step.end(TB)
                dve.wait_ge(f_done, NT)

            for l in range(4):
                if STAGES > 2 * l:
                    xattn(l)
                if STAGES > 2 * l + 1:
                    if l == 1:
                        two_token()
                    elif l == 3:
                        norms3()
                        moe_input(l)
                        norm_rows3()
                    else:
                        selfattn(l // 2)
                        moe_input(l)
                    gating(l)
                    experts(l) if l else experts0()
                    if l == 1:
                        last_norm()

        @block.tensor
        def _(pe):
            pe.sem_inc(us_ps, LEAD)
            pe.sem_inc(upT_ps, LEAD)
            pe.sem_inc(uo_ps, LEAD)
            pe.sem_inc(ye_ps, 2)
            pe.sem_inc(n_ps, 1)
            ident = w("ident")
            mm, turn = pe.matmul, pe.transpose

            def xattn(l):
                c = XATTN[l]
                G, NH, dh = c["G"], c["H"], c["dh"]
                wq, wk, wv, wo, cT = (w(n) for n in (f"x{l}_wq", f"x{l}_wk", f"x{l}_wv", f"x{l}_wo", "ctxT"))
                block_done(pe, 2 * l)
                held_in(pe, [0, 2, 3, 4][l])
                for b in range(B):
                    for n in range(max(1, NH * dh // BANK)):
                        cols = min(BANK, NH * dh)
                        mm(bank(4 + 2 * b + n, 0, cols, KV), cT[:, b * KV:(b + 1) * KV],
                           wv[:, n * BANK:n * BANK + cols], start=True, stop=True)
                if c["qk_norm"]:
                    for b in range(B):
                        for n in range(2):
                            last = mm(bank(2 * b + n, 0, BANK, KV), cT[:, b * KV:(b + 1) * KV],
                                      wk[:, n * BANK:(n + 1) * BANK], start=True, stop=True)
                    last.then_inc(kv_ps, 1)
                    pe.wait_ge(kn_ok, B)
                    for g in range(G):
                        for b in range(B):
                            a = g % 3 * 154 + b * KV
                            last = turn(bank(g // 3, a, a + KV), kn[0:KV, b, g * P:(g + 1) * P], ident[0:KV, 0:KV])
                    last.then_inc(kT_ps, 1)
                else:
                    for g in range(G):
                        last = mm(bank(g // 3, g % 3 * 154, g % 3 * 154 + 154), wk[:, g * P:(g + 1) * P], cT,
                                  start=True, stop=True)
                    last.then_inc(kv_ps, 1)
                pe.wait_ge(k_ok, l + 1)
                pe.wait_ge(v_ok, l + 1)
                K = kbd[:, 0:B * NH * KV].rearrange("p (b n) -> p b n", b=B)
                V = vx[:, 0:B * NH * (dh + 1)].rearrange("p (b h d) -> p b h d", b=B, d=dh + 1)
                with pe.Fori(0, TB) as i:
                    at = lambda j: count(8 * l, i, j)
                    for j in range(B):
                        pe.wait_ge(x_xn, at(j))
                        turn(bank(4 * j, 0, P), xn[:, j, :], ident).then_inc(x_xTp, 1)
                    for j in range(B):
                        pe.wait_ge(x_xT, at(j))
                        if c["qk_norm"]:
                            for n in range(2):
                                last = mm(bank(4 * j + n, 0, BANK), xT[:, j, :], wq[:, n * BANK:(n + 1) * BANK],
                                          start=True, stop=True)
                        else:
                            for g in range(G):
                                last = mm(psum[:, 4 * j * BANK + g * P:4 * j * BANK + g * P + P],
                                          wq[:, g * P:(g + 1) * P], xT[:, j, :], start=True, stop=True)
                        last.then_inc(q_ps, 1)
                    if c["qk_norm"]:
                        for j in range(B):
                            pe.wait_ge(qn_ok, count(0, i, j))
                            for g in range(G):
                                a = (4 * j + 2) * BANK + g * P
                                last = turn(psum[:, a:a + P], qn[:, j, g * P:(g + 1) * P], ident)
                            last.then_inc(qnT_ps, 1)
                    for j in range(B):
                        pe.wait_ge(qT_ok, at(j))
                        if G == 1:
                            for n in range(4):
                                last = mm(bank(4 * j + n, 0, 4 * KV), qT[:, j, 0:P], K[:, j, n * 4 * KV:(n + 1) * 4 * KV],
                                          start=True, stop=True)
                        else:
                            for g in range(G):
                                last = mm(bank(4 * j + g // 2, g % 2 * 154, g % 2 * 154 + 154), qT[:, j, g * P:(g + 1) * P],
                                          K[:, j, g * 154:(g + 1) * 154], start=True, stop=True)
                        last.then_inc(sc_ps, 1)
                    for j in range(B):
                        pe.wait_ge(p_ok, at(j))
                        for h in range(NH):
                            a = 4 * j * BANK + h * P
                            last = turn(psum[0:KV, a:a + P], E[:, j, h * KV:(h + 1) * KV], ident)
                        last.then_inc(pT_ps, 1)
                    for j in range(B):
                        pe.wait_ge(pT_act, at(j))
                        pe.wait_ge(pT_dve, at(j))
                        for h in range(NH):
                            a = h % 4 * (dh + 1)
                            last = mm(bank(4 * j + h // 4, a, a + dh + 1), PT[0:KV, j, h * P:(h + 1) * P], V[:, j, h, :],
                                      start=True, stop=True)
                        last.then_inc(o_ps, 1)
                    for j in range(B):
                        pe.wait_ge(o_ok, at(j))
                        for g in range(G):
                            a = 4 * j * BANK + g * P
                            last = turn(psum[:, a:a + P], O[:, j, g * P:(g + 1) * P], ident)
                        last.then_inc(oT_ps, 1)
                    for j in range(B):
                        pe.wait_ge(oT_ok, at(j))
                        for g in range(G):
                            last = mm(bank(4 * j + 2, 0, P), OT[:, j, g * P:(g + 1) * P], wo[:, g * P:(g + 1) * P],
                                      start=(g == 0), stop=(g == G - 1))
                        last.then_inc(y_ps, 1)
                    if l == 3:
                        for side in range(2):
                            pe.wait_ge(n_sq, i * 2 + (side + 1))
                            for c in range(8):
                                at_ = min(c, 4)
                                last = mm(bank(4 * side + 3, at_, at_ + 1), sq[:, side, c * P:(c + 1) * P],
                                          w("ones", 0, 1), start=(c <= 4), stop=(c < 4 or c == 7))
                            last.then_inc(n_ps, 1)

            def selfattn(u):
                l = 2 * u
                held_in(pe, [1, 3][u])
                wq, wk, wv = (w(f"s{l}_{n}_w") for n in "qkv")
                with pe.Fori(0, TB) as i:
                    for j in range(B):
                        pe.wait_ge(b_xn, count(8 * u, i, j))
                        turn(bank(4 * j, 0, P), xn[:, j, :], ident).then_inc(s_xTp, 1)
                    for j in range(B):
                        pe.wait_ge(s_xT, count(8 * l, i, j))
                        for n, (lhs, rhs) in enumerate(((wq, xT[:, j, :]), (wk, xT[:, j, :]), (xT[:, j, :], wv))):
                            last = mm(bank(4 * j + 1, n * P, n * P + P), lhs, rhs, start=True, stop=True)
                        last.then_inc(qkv_ps, 1)
                pe.wait_ge(kself0, u + 1)
                pe.wait_ge(kself1, u + 1)
                pe.wait_ge(const_ok, 1)
                base = u * UNITS
                for o, b, qt, W in q_tiles(pe, u):
                    pe.wait_ge(qcur_ok, o + (NT * u + 1))
                    for step in range(HS + 2):
                        h = step
                        if h < HS:
                            pe.wait_ge(up_ok, o * HS + (LEAD + base + h - 3))
                            last = mm(bank(h % 4, 0, W), qcur, kself[:, bass.ds(b * (HS * S) + h * S, W)],
                                      start=True, stop=True)
                            if u == 0:
                                last = mm(bank(h % 4, W - P, W), ident_bf[:, :], later_bf[:, :], start=False, stop=True,
                                          skip_group_check=True)
                            last.then_inc(us_ps, 1)
                        h = step - 1
                        if 0 <= h < HS:
                            pe.wait_ge(up_ok, o * HS + (LEAD + base + h + 1))
                            free = upT_dve if h % 2 else upT_act
                            pe.wait_ge(free, o * (HS // 2) + (LEAD + base // 2 + h // 2))
                            for k in range(W // P):
                                last = turn(bank(4 + h % 2, k * P, k * P + P),
                                            pself[:, (h % 4) * BANK + k * P:(h % 4) * BANK + k * P + P], ident)
                            last.then_inc(upT_ps, 1)
                        h = step - 2
                        if 0 <= h:
                            done = upT_dve if h % 2 else upT_act
                            pe.wait_ge(done, o * (HS // 2) + (LEAD + base // 2 + h // 2 + 1))
                            if h == 0:
                                pe.wait_ge(ctx_ok, o + (NT * u + 1))
                            for k in range(W // P):
                                last = mm(bank(6, h * (DS + 1), (h + 1) * (DS + 1)),
                                          ptself[:, (h % 4) * BANK + k * P:(h % 4) * BANK + k * P + P],
                                          v_all[:, bass.ds(b * 576 + k * 144 + h * (DS + 1), DS + 1)],
                                          start=(k == 0), stop=(k == W // P - 1))
                            last.then_inc(uo_ps, 1)

            def router(l, i):
                for j in range(B):
                    pe.wait_ge(m_xT, count(8 * l, i, j))
                    router_w = M["gwT"] if l == 3 else w(f"m{l}_router")
                    mm(bank(4 * j + 2, 0, MOE[l]["E"]), xT[:, j, :], router_w, start=True, stop=True).then_inc(lg_ps, 1)

            def moe_input(l):
                held_in(pe, [1, 2, 3, 4][l])
                with pe.Fori(0, TB) as i:
                    if l in (0, 2):
                        for j in range(B):
                            pe.wait_ge(t_cc, count(8 * (l // 2), i, j))
                            turn(bank(4 * j, 0, P), cc[:, j, :], ident).then_inc(t_ccT, 1)
                        for j in range(B):
                            pe.wait_ge(t_ccS, count(8 * l, i, j))
                            mm(bank(4 * j + 1, 0, P), yb[:, j, :], w(f"s{l}_o_w"), start=True, stop=True).then_inc(t_y, 1)
                    for j in range(B):
                        pe.wait_ge(m_xn, count(8 * l, i, j))
                        turn(bank(4 * j, 0, P), xn[:, j, :], ident).then_inc(m_xTp, 1)
                    router(l, i)

            def two_token():
                held_in(pe, 2)
                with pe.Fori(0, TB) as i:
                    for j in range(B):
                        pe.wait_ge(h0_ok, count(0, i, j))
                        turn(bank(4 * j, 0, P), xn[:, j, :], ident).then_inc(s_xTp, 1)
                    for j in range(B):
                        pe.wait_ge(s_xT, count(8, i, j))
                        mm(bank(4 * j + 1, 0, 384), xT[:, j, :], w("h_wqkv"), start=True, stop=True).then_inc(qkv_ps, 1)
                    for j in range(B):
                        pe.wait_ge(t1_av, count(0, i, j))
                        turn(bank(4 * j, 0, P), cc[:, j, :], ident).then_inc(t_ccT, 1)
                    for j in range(B):
                        pe.wait_ge(t_ccS, count(8, i, j))
                        mm(bank(4 * j + 1, 0, P), xT[:, j, :], w("h_wo"), start=True, stop=True).then_inc(t_y, 1)
                    for j in range(B):
                        pe.wait_ge(m_xn, count(8, i, j))
                        turn(bank(4 * j, 0, P), yb[:, j, :], ident).then_inc(m_xTp, 1)
                    router(1, i)

            def norms3():
                held_in(pe, 4)
                pe.wait_ge(n_pow, 2)
                turn(bank(7, 0, 8), M["gv"][0:8, :], ident[0:8, 0:8]).then_inc(n_gvT, 1)
                pe.wait_ge(n_gv, 2)

            def norm_rows3():
                for n in range(2):
                    pe.wait_ge(n_diag, n + 1)
                    mm(bank(4 + n, 0, BANK), w("ones"), M["diag"][:, n * BANK:(n + 1) * BANK],
                       start=True, stop=True).then_inc(n_row, 1)

            def gating(l):
                E_ = MOE[l]["E"]
                if l == 0:
                    pe.wait_ge(g_m, 1)
                    mm(bank(0, 0, 256), w("before"), M["m12"], start=True, stop=True)
                    mm(bank(0, 0, 256), w("ones"), M["pre"], start=False, stop=True, skip_group_check=True)
                    mm(bank(0, P, 256), w("ones"), M["tot"].unsqueeze(1).broadcast_to([P, NT, E_]),
                       start=False, stop=True, skip_group_check=True).then_inc(g_loc, 1)
                if l != 2:
                    n = [1, 2, 0, 3][l]
                    pe.wait_ge(gate_ok, n)
                    for t in range(NT):
                        last = turn(psum[0:E_, t * P:(t + 1) * P], gates[:, t, 0:E_], ident)
                    last.then_inc(gT_ps, 1)
                    pe.wait_ge(gT_ok, n)
                    for t in range(NT):
                        last = mm(psum[:, 2 * BANK + t * P:2 * BANK + (t + 1) * P], gatesT[0:E_, t * P:(t + 1) * P],
                                  w(f"m{l}_b2"), start=True, stop=True)
                    last.then_inc(b2_ps, 1)
                    pe.wait_ge(b2_ok, n)

            def experts(l):
                m = MOE[l]
                C = m["C"]

                def hidden(e, side, b):
                    if b == 0:
                        pe.wait_ge(w_in[side], load_count(l, e, side))
                    for c in range(4):
                        if l != 2:
                            pe.wait_ge(h_ok, e * 8 + (HB[l] + 4 * b + c + 1))
                        elif c < 2:
                            pe.wait_ge(sg_ok, e * 4 + (2 * b + c + 1))
                        else:
                            pe.wait_ge(h2_ok, e * 4 + (2 * b + c - 2 + 3))
                        mm(bank(c, 0, BANK), wexp[:, side, c * P:(c + 1) * P], xT_all[:, b * S:(b + 1) * S],
                           start=True, stop=True).then_inc(h_ps, 1)

                def output(e, side, b):
                    if l == 2:
                        pe.wait_ge(h2_ok, e * 4 + (4 + 2 * b + 2))
                    else:
                        pe.wait_ge(h_ok, e * 8 + (4 + HB[l] + 4 * b + 4))
                    pe.wait_ge(acc_ok, e * 2 + (KB[l] + b + 1))
                    if l == 3:
                        pe.wait_ge(w2n_ok, e + 1)
                    for t in range(TB):
                        for c in range(C):
                            down = w2n[:, side, c * P:(c + 1) * P] if l == 3 else wexp[:, side, BANK + c * P:BANK + (c + 1) * P]
                            last = mm(bank(4 + b, t * P, (t + 1) * P), hT[:, b, c * BANK + t * P:c * BANK + (t + 1) * P], down,
                                      start=(c == 0), stop=(c == C - 1))
                    last.then_inc(ye_ps, 1)

                pe.wait_ge(m_copy, NT * (l + 1))
                pe.wait_ge(lg_ok, NT * (l + 1))
                expert_order(pe, l, hidden, output)

            def experts0():
                def turned(e, side, i):
                    pe.wait_ge(d_in[side], i * 16 + 16)
                    pe.wait_ge(d_xe, e + 1)
                    turn(bank(side % 2, 0, P), D["xin"][:, side * P:(side + 1) * P], ident).then_inc(d_T, 1)

                def hidden(e, side, i):
                    pe.wait_ge(w0_in[side], i * 16 + 16)
                    pe.wait_ge(d_xe, e + 3)
                    pe.wait_ge(d_h, e + 1)
                    for c in range(4):
                        last = mm(bank(2 + side % 2, c * P, (c + 1) * P), W0[side][:, c * P:(c + 1) * P],
                                  D["xe"][:, side % 2 * P:(side % 2 + 1) * P], start=True, stop=True)
                    last.then_inc(d_H, 1)

                def output(e, side, i):
                    pe.wait_ge(d_h, e + 3)
                    pe.wait_ge(d_y, e + 1)
                    for c in range(4):
                        last = mm(bank(4 + side % 2, 0, P), D["h"][:, side % 2 * BANK + c * P:side % 2 * BANK + (c + 1) * P],
                                  W0[side][:, BANK + c * P:BANK + (c + 1) * P], start=(c == 0), stop=(c == 3))
                    last.then_inc(d_O, 1)

                run_queues(pe, (turned, 2), (hidden, 1), (output, 0))

            for l in range(4):
                if STAGES > 2 * l:
                    xattn(l)
                if STAGES > 2 * l + 1:
                    if l == 1:
                        two_token()
                    elif l == 3:
                        norms3()
                        moe_input(l)
                        norm_rows3()
                    else:
                        selfattn(l // 2)
                        moe_input(l)
                    gating(l)
                    experts(l) if l else experts0()


def kernel(**inputs):
    import concourse.bacc as bacc
    from concourse.bass_utils import run_bass_kernel_spmd

    inp = {k: np.asarray(v) for k, v in inputs.items()}
    blocks = layout(inp)
    at, first = {}, 0
    for name, block in blocks.items():
        at[name] = (first, block.shape[0], block.shape[1])
        first += block.shape[1]
    packed = np.zeros((P, first), np.float32)
    for name, block in blocks.items():
        a, rows, cols = at[name]
        packed[0:rows, a:a + cols] = block
    mask = np.ascontiguousarray(np.broadcast_to(np.tile(inp["mask_BxS2_ik0"], (1, 4)), (P, B, 4 * KV)))
    arrays = {"x": np.ascontiguousarray(inp["x"].reshape(B * S, P)), "mask": mask, "packed": packed}
    for l, e in enumerate(expert_layout(inp)):
        arrays[f"experts{l}"] = np.ascontiguousarray(e)

    nc = bacc.Bacc("TRN2", target_bir_lowering=False, num_devices=1)
    ap = {n: nc.dram_tensor(n, a.shape, mybir.dt.from_np(a.dtype), kind="ExternalInput").ap() for n, a in arrays.items()}
    out = nc.dram_tensor("out", (B * S, P), F32, kind="ExternalOutput").ap()
    queued, answers = (nc.dram_tensor(n, (SLOTS, P), F32, kind="Internal").ap() for n in ("queued", "answers"))
    program(nc, ap["x"], ap["mask"], ap["packed"], [ap[f"experts{l}"] for l in range(4)], out, queued, answers, at)
    r = run_bass_kernel_spmd(nc, [arrays], core_ids=[0])
    return r.results[0]["out"].reshape(B, S, P)
```

```python
from contextlib import ExitStack

import numpy as np

import concourse.bass as bass
from concourse import mybir

ALU = mybir.AluOpType
ACT = mybir.ActivationFunctionType
F32 = mybir.dt.float32
BF16 = mybir.dt.bfloat16
I32 = mybir.dt.int32
AX_X = mybir.AxisListType.X

P = 128
B = 2
S = 512
TB = S // P
NT = B * TB
KV = 77
BANK = 512
EPS_LN = 1e-5
ARENA = 23680
FMIN = float(np.finfo(np.float32).min)
STAGES = 8
NMOE = 4

XATTN = [
    dict(G=1, H=16, dh=8, mask=True, qk_norm=False, bias=False),
    dict(G=4, H=8, dh=64, mask=False, qk_norm=False, bias=True),
    dict(G=8, H=16, dh=64, mask=False, qk_norm=True, bias=True),
    dict(G=8, H=16, dh=64, mask=False, qk_norm=False, bias=True),
]
MOE = [
    dict(E=16, C=4, act=ACT.Gelu, W=1028),
    dict(E=8, C=4, act=ACT.Relu, W=1028),
    dict(E=8, C=2, act=ACT.Silu, W=768),
    dict(E=8, C=4, act=ACT.Silu, W=1028),
]
CAPACITY = 2 * -(-B * S // 16)
E0 = 16
SLOTS = E0 * CAPACITY
DROPPED = 2 * SLOTS
assert CAPACITY == P
HS, DS = 16, 8


def constants():
    p = np.arange(P)
    f = np.float32
    return {
        "ident": np.eye(P, dtype=f),
        "headmask": (p[:, None] // DS == np.arange(HS)).astype(f),
        "halfmask": (p[:, None] // 64 == np.arange(2)).astype(f),
        "later": np.triu(np.ones((P, P), f), 1) * f(-1e30),
        "before": np.triu(np.ones((P, P), f)),
        "firstness": np.broadcast_to(16.0 - np.arange(16, dtype=f), (P, 16)),
        "neghalf": np.full((P, 16), -0.5, f),
        "ones": np.ones((P, P), f),
        "queue": np.broadcast_to(np.arange(E0, dtype=f) * CAPACITY - 1, (P, E0)),
    }


def layout(inp):
    col = lambda v: v.reshape(-1, 1)
    row = lambda v: np.broadcast_to(v.reshape(1, -1), (P, v.size))
    blocks = dict(constants())
    blocks["ctxT"] = inp["ctx_1024"].transpose(2, 0, 1).reshape(P, B * KV)
    for l in range(4):
        n = f"L{l}_xattn_"
        out = inp[n + ("Wu" if l == 2 else "Wo")]
        if l >= 2:
            wq, wk, wv, out = inp[n + "Wq"].T, inp[n + "Wk"].T, inp[n + "Wv"].T, out.T
        else:
            wq, wk, wv = inp[n + "Wq"], inp[n + "Wk"], inp[n + "Wv"]
        G = XATTN[l]["G"]
        blocks[f"x{l}_wk"], blocks[f"x{l}_wv"], blocks[f"x{l}_wq"] = wk, wv, wq
        blocks[f"x{l}_wo"] = out.reshape(G, P, P).transpose(1, 0, 2).reshape(P, G * P)
        if l:
            blocks[f"x{l}_bo"] = row(inp[n + ("bu" if l == 2 else "bo")])
        if l == 2:
            for k in ("qn_w", "qn_b", "kn_w", "kn_b"):
                blocks[k] = col(np.concatenate([inp[n + k]] * 2))
        m = f"L{l}_ffn_"
        if l == 0:
            for k in ("q_w", "k_w", "v_w", "o_w"):
                blocks["s0_" + k] = inp[m + k]
            for k in ("q_b", "k_b", "ln1_w", "ln1_b", "ln2_w", "ln2_b"):
                blocks["s0_" + k] = col(inp[m + k])
            blocks["s0_v_b"], blocks["s0_o_b"] = row(inp[m + "v_b"]), row(inp[m + "o_b"])
            blocks["m0_router"] = inp[m + "router_w"]
            blocks["m0_b2"] = inp[m + "fc2_b"]
        if l == 1:
            blocks["h_wqkv"] = inp[m + "Wqkv"].T
            blocks["h_wo"] = inp[m + "Wo"].T
            for k in ("bqkv", "bo", "g1", "be1", "g2", "be2"):
                blocks["h_" + k] = row(inp[m + k])
            blocks["m1_router"] = inp[m + "Wg"].T
            blocks["m1_b2"] = inp[m + "b2"]
        if l == 2:
            for k in ("wq", "wk", "wv", "wo"):
                blocks["s2_" + k[1] + "_w"] = inp[m + k]
            blocks["s2_norm1"], blocks["s2_norm2"] = col(inp[m + "norm1_w"]), col(inp[m + "norm2_w"])
            blocks["m2_router"] = inp[m + "router_w"]
        if l == 3:
            blocks["m3_gate_v"] = inp[m + "gate_v"]
            blocks["m3_gate_g"] = col(inp[m + "gate_g"])
            blocks["m3_gate_b"] = row(inp[m + "gate_b"])
            blocks["m3_g1"] = inp[m + "w1_g"].reshape(8, 4, P).transpose(2, 0, 1).reshape(P, 32)
            blocks["m3_g2"] = inp[m + "w2_g"].T
            blocks["m3_b2"] = inp[m + "b2"]
    return blocks


def expert_layout(inp):
    up = lambda w: w
    down = lambda w: w.reshape(w.shape[0], -1, P, P).transpose(0, 2, 1, 3).reshape(w.shape[0], P, -1)
    bias = lambda v: v.reshape(v.shape[0], 4, P).transpose(0, 2, 1)
    out = []
    out.append(np.concatenate([up(inp["L0_ffn_fc1_w"]), down(inp["L0_ffn_fc2_w"]), bias(inp["L0_ffn_fc1_b"])], 2))
    out.append(np.concatenate([up(inp["L1_ffn_W1"]), down(inp["L1_ffn_W2"]), bias(inp["L1_ffn_b1"])], 2))
    m = "L2_ffn_"
    routed = np.concatenate([inp[m + "e_gate"], inp[m + "e_up"], down(inp[m + "e_down"])], 2)
    shared = np.concatenate([inp[m + "sh_gate"][None], inp[m + "sh_up"][None], down(inp[m + "sh_down"][None])], 2)
    out.append(np.concatenate([routed, shared]))
    m = "L3_ffn_"
    out.append(np.concatenate([inp[m + "w1_v"].transpose(0, 2, 1), down(inp[m + "w2_v"].transpose(0, 2, 1)), bias(inp[m + "b1"])], 2))
    return out



def cuts(at):
    return [at[n][0] + at[n][2] for n in ("x0_wo", "m0_b2", "m1_b2", "m2_router", "m3_b2")]


def program(nc, x, mask, packed, experts, out, queued, answers, at):
    ctx = ExitStack()
    with ctx:
        def sb(name, shape, dt=F32):
            return ctx.enter_context(nc.sbuf_tensor(name, shape, dt))

        def sem(name):
            return ctx.enter_context(nc.semaphore(name))

        def sems(names):
            return [sem(n) for n in names.split()]

        ends = cuts(at)
        held = sb("held", [P, ends[-1]])

        def w(name, lo=0, hi=None):
            a, r, c = at[name]
            return held[0:r, a + lo:a + (c if hi is None else hi)]

        def w_at(name, lo, n=1):
            return held[0:at[name][1], bass.ds(lo + at[name][0], n)]

        x_res = sb("x_res", [P, NT * P])
        r_res = sb("r_res", [P, NT * P])
        xT_all = sb("xT_all", [P, NT * P])
        kbd = sb("kbd", [P, B * 16 * KV])
        vx = sb("vx", [KV, B * 16 * 65])
        wexp = sb("wexp", [P, 2, 1028])
        mask_i = sb("mask_i", [P, B, 4 * KV], I32)
        stats = sb("stats", [P, NT, 6])
        mv = sb("mv", [P, NT, 2])
        var = sb("var", [P, 4, 16])
        rstd = sb("rstd", [P, 4, 16])
        small = sb("small", [P, 4, 64])
        chain = sb("chain", [P, 8 * P])
        arena = sb("arena", [P, ARENA])
        pool_pad = sb("pool_pad", [P, 8])
        n_sum = sb("n_sum", [P, 40])
        slot_i = sb("slot_i", [P, 32], I32)
        s1_now = sb("s1_now", [P, 2, 4])
        ident_bf = sb("ident_bf", [P, P], BF16)
        later_bf = sb("later_bf", [P, P], BF16)
        spread_q = sb("spread_q", [P, HS, 160], BF16)
        spread_k = sb("spread_k", [P, HS, 112], BF16)
        act_pad = sb("act_pad", [P, 4])
        psum = ctx.enter_context(nc.psum_tensor("psum", [P, 8 * BANK], F32))

        def bank(n, lo, hi, rows=P):
            return psum[0:rows, n * BANK + lo:n * BANK + hi]

        def take(sizes):
            views, a = {}, 0
            for name, n in sizes.items():
                views[name] = arena[:, a:a + n]
                a += n
            assert a <= ARENA, a
            return views

        def two(v):
            return v.rearrange("p (j n) -> p j n", j=2)

        xn, xT, cc, yb = (two(chain[:, n * 256:n * 256 + 256]) for n in range(4))
        A = take(dict(qT=8192, qcur=2048, E=2 * 1232, PT=4096, O=2048, OT=2048, sq=2048))
        qcur2, E, PT, O, OT = (two(A[k]) for k in ("qcur", "E", "PT", "O", "OT"))
        qT_all, xn_all = A["qT"], A["PT"][:, 0:NT * P]
        ext = two(A["qT"][:, 7000:7000 + 8 * KV])
        kn, kaff = two(A["E"][:, 0:2048]), A["qcur"][:, 0:8 * 154]
        four = lambda v: v.rearrange("p (c n) -> p c n", c=4)
        qn4, qsq4 = four(A["PT"]), four(arena[:, 8192 + 2048 + 2464 + 4096:8192 + 2048 + 2464 + 2 * 4096])
        U = take(dict(rep=2 * HS * S, P=4 * BANK, PT=4 * BANK, qa=NT * P, ka=NT * P, va=NT * P))
        pself, ptself, q_all, k_all, v_all = (U[n] for n in ("P", "PT", "qa", "ka", "va"))
        v_wide = arena[:, 2 * HS * S + 8 * BANK:2 * HS * S + 8 * BANK + 2 * NT * P]
        ROWS = 96
        q_rep, k_rep = (U["rep"].bitcast(BF16)[0:ROWS, n * HS * B * S:(n + 1) * HS * B * S] for n in range(2))
        q_parts, k_parts = (U[n].bitcast(BF16).rearrange("p (n t) -> p n t", t=B * S) for n in ("P", "PT"))
        ctxT_all = xT_all[:, :]
        H = take(dict(qkv=2 * 384, prod=512, sc=64))
        qkv, prod = two(H["qkv"]), H["prod"]
        M = take(dict(h=2 * 2048, s=2048, w2n=1024, s2=8 * P, diag=8 * P, gv=P, gwT=8, ga=P, gb=P, gc=P,
                      m12=256, pre=256, tot=16, mk=256, gT=NT * P,
                      lg=NT * 16, gates=NT * 16))
        logits = M["lg"]
        gates = M["gates"].rearrange("p (t e) -> p t e", t=NT)
        gatesT = M["gT"][0:16, :]
        sq = two(A["sq"])
        s1_all, s2_col = n_sum[:, 0:32], n_sum[:, 32:40]
        hT, sg, w2n = two(M["h"]), two(M["s"]), two(M["w2n"])

        D = take(dict(skip=12032, w=2 * 1028, xin=4 * P, xe=2 * P, h=2 * 512, y=4 * P, back=16 * P, loc=256, slot=64))
        W0 = [wexp[:, 0, :], wexp[:, 1, :], D["w"][:, 0:1028], D["w"][:, 1028:2056]]

        in_x, in_mask, stored, const_ok = sems("in_x in_mask stored const_ok")
        in_held = [sem(f"in_held{n}") for n in range(5)]
        dve_step, act_step, pool_step = sems("dve_step act_step pool_step")
        x_stat, x_rstd, x_xn, x_xTp, x_xT = sems("x_stat x_rstd x_xn x_xTp x_xT")
        kv_ps, kn_ok, kT_ps, k_ok, v_ok = sems("kv_ps kn_ok kT_ps k_ok v_ok")
        kc_ok, ksq_ok, kvar_ok, krstd_ok = sems("kc_ok ksq_ok kvar_ok krstd_ok")
        q_act, q_dve, xq_ok, q_nat = sems("q_act q_dve xq_ok q_nat")
        q_ps, qc_ok, qsq_ok, qvar_ok, qrstd_ok, qn_ok, qnT_ps, qT_ok = sems(
            "q_ps qc_ok qsq_ok qvar_ok qrstd_ok qn_ok qnT_ps qT_ok")
        sc_ps, e_ok, p_ok, pT_ps, pT_act, pT_dve = sems("sc_ps e_ok p_ok pT_ps pT_act pT_dve")
        o_ps, o_ok, oT_ps, oT_ok, y_ps, x_done = sems("o_ps o_ok oT_ps oT_ok y_ps x_done")
        a_stat, a_rstd, h0_ok, b_stat, b_rstd, b_xn, s_xTp, s_xT, qkv_ps, qkv_ok = sems(
            "a_stat a_rstd h0_ok b_stat b_rstd b_xn s_xTp s_xT qkv_ps qkv_ok")
        split_ok, rk_ps, rq_ps, rk_ok, rq_ok, us_ps, um_ok, up_ok, upT_ps, upT_act, upT_dve, uo_ps, ctx_ok, inv_ok, r_ps, v_wide_ok, invT_ok = sems(
            "split_ok rk_ps rq_ps rk_ok rq_ok us_ps um_ok up_ok upT_ps upT_act upT_dve uo_ps ctx_ok inv_ok r_ps v_wide_ok invT_ok")
        t_cc, t_ccT, t_ccS, t_y, r_ok = sems("t_cc t_ccT t_ccS t_y r_ok")
        m_stat, m_rstd, m_xn, m_xTp, m_xT, m_copy, lg_ps, lg_ok = sems(
            "m_stat m_rstd m_xn m_xTp m_xT m_copy lg_ps lg_ok")
        g_sub, g_exp, g_m, g_loc, gate_ok, gT_ps, gT_ok, b2_ps, b2_ok = sems(
            "g_sub g_exp g_m g_loc gate_ok gT_ps gT_ok b2_ps b2_ok")
        w_in = [sem(f"w_in{n}") for n in range(2)]
        h_ps, h_ok, sg_ok, h2_ok, ye_ps, acc_ok, w2n_ok = sems("h_ps h_ok sg_ok h2_ok ye_ps acc_ok w2n_ok")
        n_sq, n_ps, n_max, n_pow, n_ok, n_gv, n_gvT, n_diag, n_row, n_s2 = sems(
            "n_sq n_ps n_max n_pow n_ok n_gv n_gvT n_diag n_row n_s2")
        w0_in = [sem(f"w0_in{n}") for n in range(4)]
        d_in = [sem(f"d_in{n}") for n in range(4)]
        d_stored = [sem(f"d_stored{n}") for n in range(4)]
        d_back = [sem(f"d_back{n}") for n in range(4)]
        zeros_set, zeros_out, slots_ok, scattered = sems("zeros_set zeros_out slots_ok scattered")
        d_T, d_xe, d_H, d_h, d_O, d_y, d_done = sems("d_T d_xe d_H d_h d_O d_y d_done")
        f_stat, f_rstd, f_done = sems("f_stat f_rstd f_done")
        t1_e, t1_p, t1_av = sems("t1_e t1_p t1_av")

        block = ctx.enter_context(nc.Block())

        def tile(i, j):
            return bass.ds(i * P + j * S, P)

        class Steps:
            def __init__(self, eng, semaphore):
                self.eng, self.sem, self.base, self.n, self.i, self.per = eng, semaphore, 0, 0, None, 0

            def loop(self, i, per):
                self.base, self.n, self.i, self.per = self.base + self.n, 0, i, per

            def end(self, trips):
                assert self.n == self.per, (self.n, self.per)
                self.base, self.n, self.i = self.base + trips * self.per, 0, None

            def then(self, instruction):
                self.n += 1
                instruction.then_inc(self.sem, 1)
                at = self.base + self.n
                self.eng.wait_ge(self.sem, at if self.i is None else self.i * self.per + at)

        def count(base, i, j):
            return i * 2 + (base + j + 1)

        UNITS = NT * HS
        LATE = 4
        LEAD = 4
        KB = [2 * n for n in np.cumsum([0, 0, 8, 9, 8]).tolist()]
        HB = [0, 0, 64, 64, 128]
        HPB = [4 * n for n in KB]
        WB = [[0, 0], [0, 0], [4, 4], [9, 8]]

        YBANK = [2, 2, 1, 1]
        PARTS = [1, 2, 2, 2]
        XB = [8, 16, 32, 48]
        QB = [2 * n for n in (0, 1, 5, 5, 13)]
        PB = [0, 8, 16, 32]

        def chains(l):
            return [(j * PARTS[l] + part, j, part) for j in range(B) for part in range(PARTS[l])]

        def unit(l, i, c):
            return i * (B * PARTS[l]) + (XB[l] - 8 + c + 1)

        def turned_by(l, i, j, part):
            if l == 1:
                n = i * 2 + (PB[1] + j + 1)
                return (n, None) if part == 0 else (None, n)
            n = i * (B * PARTS[l]) + (PB[l] + j * PARTS[l] + part + 1)
            return n, n

        def block_done(eng, n):
            if n == 0:
                eng.wait_ge(in_x, 16)
            elif n % 2:
                eng.wait_ge(x_done, 2 + NT * (n // 2 + 1))
            elif n == 2:
                eng.wait_ge(d_done, 1)
            elif n == 4:
                eng.wait_ge(f_done, NT)
            else:
                eng.wait_ge(acc_ok, 2 + KB[n // 2])

        def held_in(eng, n):
            eng.wait_ge(in_held[n], 16)

        def q_tiles(eng, u, at_batch=None):
            with eng.Fori(0, B) as b:
                if at_batch is not None:
                    at_batch(b)
                for qt in range(TB):
                    yield b * TB + qt, b, qt, (qt + 1) * P if u == 0 else S

        def load_count(l, e, side):
            before = 16 * (WB[l][side] + (4 if l == 3 else 0) + 1) - 8 * side
            return e * 8 + before

        def run_queues(eng, *lagged):
            def steps(e, k, i):
                for do, ahead in lagged:
                    if isinstance(e, int) and not 0 <= e + ahead < E0:
                        continue
                    do(e + ahead, (k + ahead) % 4, i + (k + ahead) // 4)

            for e in range(-max(ahead for _, ahead in lagged), 0):
                steps(e, e, 0)
            with eng.Fori(0, E0 // 4 - 1) as i:
                for k in range(4):
                    steps(i * 4 + k, k, i)
            for k in range(4):
                steps(E0 - 4 + k, k, E0 // 4 - 1)

        def expert_order(eng, l, first, second):
            n = MOE[l]["E"] + (l == 2)

            def pair(e0, more):
                for side in range(2):
                    e = e0 + side
                    first(e, side, 1)
                    second(e, side, 0)
                    if side == 0 or more:
                        first(e + 1, 1 - side, 0)
                    second(e, side, 1)

            first(0, 0, 0)
            trips = n // 2 if n % 2 else n // 2 - 1
            with eng.Fori(0, trips) as i:
                pair(i * 2, True)
            if n % 2:
                first(n - 1, 0, 1)
                second(n - 1, 0, 0)
                second(n - 1, 0, 1)
            else:
                pair(n - 2, False)

        @block.sync
        def _(sp):
            first = 0
            for n, end in enumerate(ends):
                sp.dma_start(held[:, first:end], packed[:, first:end]).then_inc(in_held[n], 16)
                first = end
                if n == 0:
                    sp.dma_start(x_res[:, :].rearrange("p (t d) -> p t d", d=P),
                                 x.rearrange("(t p) d -> p t d", p=P)).then_inc(in_x, 16)
                    sp.dma_start(mask_i[:, :, :], mask).then_inc(in_mask, 16)

            def load(l, e, side):
                W = MOE[l]["W"]
                src = experts[l].rearrange("e p n -> p e n")[:, bass.ds(e, 1), :]
                sp.dma_start(wexp[:, side:side + 1, 0:W], src).then_inc(w_in[side], 16)

            sp.wait_ge(zeros_set, 1)
            for n in range(SLOTS // 1024):
                sp.dma_start(queued[n * 1024:(n + 1) * 1024, :].rearrange("(p t) d -> p (t d)", p=P),
                             r_res[:, :]).then_inc(zeros_out, 16)

            def load0(e, side):
                src = experts[0].rearrange("e p n -> p e n")[:, bass.ds(e, 1), :]
                sp.dma_start(W0[side].unsqueeze(1), src).then_inc(w0_in[side], 16)

            def load_queue(e, side):
                src = queued.rearrange("(e p) d -> p e d", p=P)[:, bass.ds(e, 1), :]
                sp.dma_start(D["xin"][:, side * P:(side + 1) * P].unsqueeze(1), src).then_inc(d_in[side], 16)

            def store_answer(e, side):
                sp.wait_ge(d_y, e + 3)
                dst = answers.rearrange("(e p) d -> p e d", p=P)[:, bass.ds(e, 1), :]
                sp.dma_start(dst, D["y"][:, side * P:(side + 1) * P].unsqueeze(1)).then_inc(d_stored[side], 16)

            def load_ahead(e, side):
                sp.wait_ge(d_O, e + 1)
                load0(e + 4, side)
                load_queue(e + 4, side)

            for side in range(4):
                if side == 2:
                    sp.wait_ge(ctx_ok, 2 + NT)
                load0(side, side)
            sp.wait_ge(scattered, 16 * 16)
            for side in range(4):
                load_queue(side, side)
            with sp.Fori(0, E0 // 4 - 1) as i:
                for k in range(4):
                    load_ahead(i * 4 + k, k)
                    store_answer(i * 4 + k, k)
            for k in range(4):
                store_answer(E0 - 4 + k, k)

            for l in range(1, NMOE):
                n = MOE[l]["E"] + (l == 2)
                if l == 3:
                    for side in range(2):
                        sp.wait_ge(ye_ps, 2 + KB[l])
                        load(l, side, side)
                    with sp.Fori(0, 3) as i:
                        for side in range(2):
                            sp.wait_ge(n_sq, i * 2 + (side + 1))
                            load(l, i * 2 + (side + 2), side)
                    sp.wait_ge(n_sq, 8)
                else:
                    sp.wait_ge(ye_ps, 2 + KB[l])
                for side in range(2):
                    load(l, side, side)
                with sp.Fori(0, (n - 2) // 2) as i:
                    for side in range(2):
                        sp.wait_ge(ye_ps, i * 4 + (2 + KB[l] + 2 * side + 2))
                        load(l, i * 2 + (side + 2), side)
                if n % 2:
                    sp.wait_ge(ye_ps, 2 + KB[l] + 2 * (n - 2))
                    load(l, n - 1, 0)
            block_done(sp, STAGES)
            sp.dma_start(out.rearrange("(t p) d -> p t d", p=P),
                         x_res[:, :].rearrange("p (t d) -> p t d", d=P)).then_inc(stored, 16)
            sp.wait_ge(stored, 16)

        @block.gpsimd
        def _(pool):
            step = Steps(pool, pool_step)
            half = w("neghalf")

            def carry(n):
                pool.tensor_tensor(pool_pad[:, n:n + 1], half[:, 0:1], half[:, 0:1], ALU.mult)

            def rsqrt(dst, src, ready, at, done):
                pool.wait_ge(ready, at)
                n = src.shape[-1]
                pool.tensor_tensor(dst, src, half[0:src.shape[0], 0:n], ALU.pow).then_inc(done, 1)

            held_in(pool, 0)

            def xattn(l):
                def all_tiles():
                    pool.wait_ge(x_stat, l + 1)
                    pool.tensor_tensor(rstd[:, 0, 0:NT], var[:, 0, 0:NT], half[:, 0:NT], ALU.pow).then_inc(x_rstd, 1)

                all_tiles()
                if l == 2:
                    for b in range(B):
                        rsqrt(rstd[0:KV, 1 + b, :], var[0:KV, 1 + b, :], kvar_ok, b + 1, krstd_ok)
                    for n in range(NT):
                        rsqrt(rstd[:, n % 4, :], var[:, n % 4, :], qvar_ok, n + 1, qrstd_ok)
                    pool.wait_ge(qT_ok, NT)
                else:
                    pool.wait_ge(q_act, QB[l] // 2 + XATTN[l]["G"])
                    pool.wait_ge(q_dve, QB[l] // 2 + XATTN[l]["G"])
                G = XATTN[l]["G"]
                Q = qT_all[:, 0:B * G * S].rearrange("p (b g t) -> p b g t", b=B, g=G)
                with pool.Fori(0, TB) as i:
                    for j in range(B):
                        pool.wait_ge(sc_ps, i * (B * PARTS[l]) + (XB[l] - B * PARTS[l] + (j + 1) * PARTS[l]))
                        carry(j)
                        pool.tensor_copy(qcur2[:, j, 0:G * P].rearrange("p (g t) -> p g t", g=G),
                                         Q[:, j, :, bass.ds(i * P, P)]).then_inc(xq_ok, 1)

            def selfattn(u):
                with pool.Fori(0, TB) as i:
                    for j in range(B):
                        rsqrt(rstd[:, j, 0:1], var[:, j, 0:1], a_stat, count(16 * u, i, j), a_rstd)
                    for j in range(B):
                        rsqrt(rstd[:, j, 0:1], var[:, j, 0:1], b_stat, count(8 * u, i, j), b_rstd)

            def moe_input(l):
                with pool.Fori(0, TB) as i:
                    if l in (0, 2):
                        for j in range(B):
                            pool.wait_ge(ctx_ok, 2 + NT * (l // 2 + 1))
                            carry(j)
                            pool.tensor_copy(cc[:, j, :], ctxT_all[:, tile(i, j)]).then_inc(t_cc, 1)
                    for j in range(B):
                        rsqrt(rstd[:, j, 0:1], var[:, j, 0:1], m_stat, count(8 * l, i, j), m_rstd)
                    for j in range(B):
                        pool.wait_ge(m_xn if l == 0 else m_xT, count(8 * l, i, j))
                        carry(2 + j)
                        pool.tensor_copy(xT_all[:, tile(i, j)], (xn if l == 0 else xT)[:, j, :]).then_inc(m_copy, 1)

            def queues():
                pool.wait_ge(slots_ok, 1)
                pool.wait_ge(zeros_out, 16 * (SLOTS // 1024))
                pool.wait_ge(m_copy, NT)
                for k in range(2):
                    for t in range(NT):
                        pool.indirect_dma_start(
                            queued, bass.IndirectOffsetOnAxis(ap=slot_i[:, k * NT + t:k * NT + t + 1], axis=0),
                            xT_all[:, t * P:(t + 1) * P], None, bounds_check=SLOTS - 1, oob_is_err=False)\
                            .then_inc(scattered, 16)
                for side in range(4):
                    pool.wait_ge(d_stored[side], 16 * (1 + E0 // 4))
                for n in range(2 * NT):
                    pool.indirect_dma_start(
                        D["back"][:, n * P:(n + 1) * P], None, answers,
                        bass.IndirectOffsetOnAxis(ap=slot_i[:, 2 * NT + n:2 * NT + n + 1], axis=0))\
                        .then_inc(d_back[n // 4], 16)

            def norms3():
                held_in(pool, 4)
                pool.wait_ge(n_max, 2 + 8 + 1)
                gv = small[0:8, 0, 33:34]
                step.then(pool.tensor_tensor(gv, gv, half[0:8, 0:1], ALU.pow))
                pool.tensor_tensor(gv, gv, w("m3_gate_g"), ALU.mult).then_inc(n_pow, 1)
                step.then(pool.tensor_tensor(n_sum[:, :], n_sum[:, :], half[:, 0:1].broadcast_to([P, 40]), ALU.pow))
                pool.tensor_tensor(s1_all, s1_all, w("m3_g1"), ALU.mult)
                pool.tensor_tensor(s2_col, s2_col, w("m3_g2"), ALU.mult).then_inc(n_ok, 1)
                pool.wait_ge(n_ok, 1)

            def experts3():
                pool.wait_ge(n_s2, 2)
                with pool.Fori(0, 4) as i:
                    for side in range(2):
                        pool.wait_ge(w_in[side], i * 16 + 16 * (WB[3][side] + 4 + 1))
                        carry(5 + side)
                        pool.tensor_copy(s1_now[:, side, :], s1_all[:, bass.ds(i * 8 + side * 4, 4)])
                        pool.tensor_tensor(w2n[:, side, :].rearrange("p (c d) -> p c d", d=P),
                                           wexp[:, side, 512:1024].rearrange("p (c d) -> p c d", d=P),
                                           M["s2"][:, bass.ds(i * 256 + side * P, P)].unsqueeze(1).broadcast_to([P, 4, P]),
                                           ALU.mult).then_inc(w2n_ok, 1)

            for l in range(4):
                if STAGES > 2 * l:
                    xattn(l)
                if STAGES > 2 * l + 1:
                    if l == 1:
                        with pool.Fori(0, TB) as i:
                            for j in range(B):
                                rsqrt(rstd[:, j, 0:1], var[:, j, 0:1], a_stat, count(8, i, j), a_rstd)
                            for j in range(B):
                                rsqrt(rstd[:, j, 0:1], var[:, j, 0:1], m_stat, count(8, i, j), m_rstd)
                            for j in range(B):
                                pool.wait_ge(m_xT, count(8, i, j))
                                carry(2 + j)
                                pool.tensor_copy(xT_all[:, tile(i, j)], xT[:, j, :]).then_inc(m_copy, 1)
                        with pool.Fori(0, TB) as i:
                            for j in range(B):
                                rsqrt(rstd[:, j, 0:1], var[:, j, 0:1], f_stat, count(0, i, j), f_rstd)
                    elif l == 3:
                        norms3()
                        moe_input(l)
                        experts3()
                    else:
                        selfattn(l // 2)
                        moe_input(l)
                        if l == 0:
                            queues()

        @block.scalar
        def _(act):
            step = Steps(act, act_step)
            act.sem_inc(up_ok, LEAD)
            act.sem_inc(upT_act, LEAD)
            act.sem_inc(h_ok, 4)
            act.sem_inc(d_h, 2)
            act.sem_inc(rq_ok, 4)
            act.sem_inc(sg_ok, 2)

            def copy_tile(ready, at, dst, src, done, func=ACT.Copy, **kw):
                act.wait_ge(ready, at)
                act.activation(dst, src, func, **kw).then_inc(done, 1)

            def xattn(l):
                L = XATTN[l]
                G, NH, dh = L["G"], L["H"], L["dh"]
                nb = NH // 4
                held_in(act, [0, 2, 3, 4][l])
                if l == 2:
                    for b in range(B):
                        act.wait_ge(kc_ok, b + 1)
                        act.activation(O[0:KV, b, :], kn[0:KV, b, :], ACT.Square).then_inc(ksq_ok, 1)
                act.wait_ge(kv_ps, l + 1)
                V = vx[:, 0:B * NH * (dh + 1)].rearrange("p (b h d) -> p b h d", b=B, d=dh + 1)
                for b in range(B):
                    first = 4 + 2 * b
                    last = act.activation(V[:, b, :, 0:dh],
                                          psum[0:KV, first * BANK:first * BANK + NH * dh].rearrange("p (h d) -> p h d", d=dh),
                                          ACT.Copy)
                last.then_inc(v_ok, 1)
                for b in range(B):
                    copy_tile(x_xTp, 2 * l + b + 1, xT_all[:, b * S:(b + 1) * S], bank(b, 0, BANK), x_xT)
                if l == 2:
                    for b in range(B):
                        for c in range(4):
                            act.wait_ge(qc_ok, 4 * b + c + 1)
                            act.activation(qsq4[:, c, :], qn4[:, c, :], ACT.Square).then_inc(qsq_ok, 1)
                        for c in range(4):
                            copy_tile(qnT_ps, 4 * b + c + 1,
                                      qT_all[:, b * G * S:(b + 1) * G * S].rearrange("p (g t) -> p g t", g=G)[:, :, c * P:(c + 1) * P],
                                      psum[:, 2 * c * BANK:(2 * c + 2) * BANK].rearrange("p (g t) -> p g t", g=G),
                                      qT_ok, ACT.Identity, scale=w("qn_w"), bias=w("qn_b"))
                else:
                    for n in range(0, B * G, 2):
                        copy_tile(q_ps, QB[l] + n + 1, qT_all[:, n * S:(n + 1) * S], bank((2 + n) % 8, 0, BANK), q_act)
                with act.Fori(0, TB) as i:
                    for c, j, part in chains(l):
                        act.wait_ge(e_ok, unit(l, i, c))
                        n = NH // PARTS[l] * KV
                        e = E[:, j, part * n:(part + 1) * n]
                        act.activation(e, e, ACT.Exp, scale=1.0 if L["mask"] else dh ** -0.5).then_inc(p_ok, 1)
                    for c, j, part in chains(l):
                        if l != 1 or part == 0:
                            lo, n = part * nb // PARTS[l], max(1, nb // PARTS[l] // 2)
                            copy_tile(pT_ps, unit(l, i, c), PT[0:KV, j, lo * BANK:(lo + n) * BANK],
                                      psum[0:KV, (4 * j + lo) * BANK:(4 * j + lo + n) * BANK], pT_act)
                    for c, j, part in chains(l):
                        n = G * P // PARTS[l]
                        first = 4 * j + part * nb // PARTS[l]
                        copy_tile(oT_ps, unit(l, i, c), OT[:, j, part * n:(part + 1) * n],
                                  psum[:, first * BANK:first * BANK + n], oT_ok)
                    if l == 3:
                        for side in range(2):
                            act.wait_ge(w_in[side], i * 16 + 16 * (WB[3][side] + 1))
                            act.wait_ge(n_ps, i * 2 + (side + 1))
                            act.activation(sq[:, side, :], wexp[:, side, 0:1024], ACT.Square).then_inc(n_sq, 1)

            def selfattn(u):
                held_in(act, [1, 3][u])
                with act.Fori(0, TB) as i:
                    for j in range(B):
                        act.wait_ge(s_xTp, count(16 * u, i, j))
                        if u == 0:
                            act.activation(xT[:, j, :], bank(4 * j, 0, P), ACT.Identity,
                                           scale=w("s0_ln1_w"), bias=w("s0_ln1_b")).then_inc(s_xT, 1)
                        else:
                            act.activation(xT[:, j, :], bank(4 * j, 0, P), ACT.Copy,
                                           scale=w("s2_norm1")).then_inc(s_xT, 1)
                for b in range(B):
                    with act.Fori(0, HS // 4) as i:
                        for k in range(4):
                            act.wait_ge(rq_ps, i * 4 + ((u * B + b) * HS + k + 1))
                            act.activation(act_pad[:, k:k + 1], w("neghalf", 0, 1), ACT.Copy)
                            act.activation(q_rep[:, bass.ds(i * (4 * B * S) + (k * B * S + b * S), S)],
                                           bank(2 * k + 1, 0, BANK, ROWS), ACT.Copy).then_inc(rq_ok, 1)
                for o, b, qt, W in q_tiles(act, u):
                    base = u * UNITS
                    for h in range(HS + 2):
                        if h < HS:
                            act.wait_ge(um_ok, o * HS + (base + h + 1))
                            act.wait_ge(upT_ps, o * HS + (LEAD + base + h - 3))
                            act.activation(pself[:, (h % 4) * BANK:(h % 4) * BANK + W], bank(h % 4, 0, W), ACT.Exp,
                                           bias=small[:, 0, h:h + 1], accum_out=small[:, 1 + qt % 2, h:h + 1]).then_inc(up_ok, 1)
                        g = h - 2
                        if g >= 0 and g % 2 == 0:
                            act.wait_ge(upT_ps, o * HS + (LEAD + base + g + 1))
                            act.wait_ge(uo_ps, o * HS + (LEAD + base + g - 3))
                            act.activation(ptself[:, (g % 4) * BANK:(g % 4) * BANK + W], bank(4 + g % 2, 0, W),
                                           ACT.Copy).then_inc(upT_act, 1)

            def moe_input(l):
                held_in(act, [1, 2, 3, 4][l])
                with act.Fori(0, TB) as i:
                    for j in range(B):
                        act.wait_ge(m_xTp, count(8 * l, i, j))
                        src = bank(4 * j, 0, P)
                        if l == 0:
                            ins = act.activation(xT[:, j, :], src, ACT.Identity, scale=w("s0_ln2_w"), bias=w("s0_ln2_b"))
                        elif l == 2:
                            ins = act.activation(xT[:, j, :], src, ACT.Copy, scale=w("s2_norm2"))
                        else:
                            ins = act.activation(xT[:, j, :], src, ACT.Copy)
                        ins.then_inc(m_xT, 1)

            def two_token():
                held_in(act, 2)
                with act.Fori(0, TB) as i:
                    for j in range(B):
                        copy_tile(s_xTp, count(8, i, j), xT[:, j, :], bank(4 * j, 0, P), s_xT)
                    act.wait_ge(t1_e, i + 1)
                    act.activation(H["sc"][:, 0:16], H["sc"][:, 0:16], ACT.Exp, scale=32 ** -0.5).then_inc(t1_p, 1)
                    for j in range(B):
                        copy_tile(t_ccT, count(0, i, j), xT[:, j, :], bank(4 * j, 0, P), t_ccS)
                    for j in range(B):
                        copy_tile(m_xTp, count(8, i, j), xT[:, j, :], bank(4 * j, 0, P), m_xT)

            def gating(l):
                E_ = MOE[l]["E"]
                if l in (0, 2):
                    act.wait_ge(g_sub, [1, 0, 2][l])
                    act.activation(M["gc"][:, 0:NT * E_], M["gc"][:, 0:NT * E_], ACT.Exp).then_inc(g_exp, 1)
                if l == 2:
                    act.wait_ge(g_sub, 3)
                    act.activation(M["gc"][:, 0:NT * E_], M["gc"][:, 0:NT * E_], ACT.Exp).then_inc(g_exp, 1)
                if l != 2:
                    act.wait_ge(gT_ps, [1, 2, 0, 3][l])
                    act.activation(gatesT[0:E_, :], psum[0:E_, 0:2 * BANK], ACT.Copy).then_inc(gT_ok, 1)

            def experts(l):
                m = MOE[l]
                n, func = m["E"], m["act"]

                def hidden(e, side, b):
                    if l == 2:
                        for c in range(2):
                            act.wait_ge(h_ps, e * 8 + (HPB[l] + 4 * b + c + 1))
                            act.wait_ge(h2_ok, e * 4 + (2 * b + c + 1))
                            act.activation(sg[:, b, c * BANK:(c + 1) * BANK], bank(c, 0, BANK), func).then_inc(sg_ok, 1)
                        return
                    for c in range(4):
                        act.wait_ge(h_ps, e * 8 + (HPB[l] + 4 * b + c + 1))
                        if c == 0:
                            act.wait_ge(ye_ps, e * 2 + (2 + KB[l] + b - 1))
                        kw = dict(bias=wexp[:, side, 1024 + c:1025 + c])
                        if l == 3:
                            if c == 0:
                                act.wait_ge(w2n_ok, e + 1)
                            kw["scale"] = s1_now[:, side, c:c + 1]
                        act.activation(hT[:, b, c * BANK:(c + 1) * BANK], bank(c, 0, BANK), func, **kw).then_inc(h_ok, 1)

                act.preload_act_table(func)
                with act.Fori(0, n // 2) as i:
                    for side in range(2):
                        for b in range(B):
                            hidden(i * 2 + side, side, b)
                if l == 2:
                    for b in range(B):
                        hidden(n, 0, b)
                act.preload_act_table(ACT.Exp)

            def norms3():
                held_in(act, 4)
                block_done(act, 7)
                act.activation(M["gv"][0:8, :], w("m3_gate_v"), ACT.Square, accum_out=small[0:8, 0, 32:33]).then_inc(n_gv, 1)
                act.wait_ge(n_gvT, 1)
                act.activation(M["gwT"], bank(7, 0, 8), ACT.Copy).then_inc(n_gv, 1)

            def norm_rows3():
                for n in range(2):
                    act.wait_ge(n_row, n + 1)
                    act.activation(M["s2"][:, n * BANK:(n + 1) * BANK], bank(4 + n, 0, BANK), ACT.Copy).then_inc(n_s2, 1)

            def experts0():
                def activate(e, side, i):
                    act.wait_ge(d_H, e + 1)
                    act.wait_ge(w0_in[side], i * 16 + 16)
                    for c in range(4):
                        last = act.activation(D["h"][:, side % 2 * BANK + c * P:side % 2 * BANK + (c + 1) * P],
                                              bank(2 + side % 2, c * P, (c + 1) * P), ACT.Gelu,
                                              bias=W0[side][:, 1024 + c:1025 + c])
                    last.then_inc(d_h, 1)

                act.preload_act_table(ACT.Gelu)
                run_queues(act, (activate, 0))
                act.preload_act_table(ACT.Exp)

            act.preload_act_table(ACT.Exp)
            for l in range(4):
                if STAGES > 2 * l:
                    xattn(l)
                if STAGES > 2 * l + 1:
                    if l == 1:
                        two_token()
                    elif l == 3:
                        norms3()
                        moe_input(l)
                        norm_rows3()
                    else:
                        selfattn(l // 2)
                        moe_input(l)
                    gating(l)
                    experts(l) if l else experts0()

        @block.vector
        def _(dve):
            step = Steps(dve, dve_step)
            dve.sem_inc(upT_dve, LEAD)
            dve.sem_inc(h2_ok, 4)
            dve.sem_inc(acc_ok, 2)
            dve.sem_inc(ctx_ok, 2)
            dve.sem_inc(d_xe, 2)
            dve.sem_inc(rk_ok, 4)
            dve.sem_inc(x_done, 2)
            dve.sem_inc(n_max, 2)
            dve.sem_inc(d_y, 2)
            for side in range(4):
                dve.sem_inc(d_stored[side], 16)
            dve.memset(r_res[:, :], 0.0).then_inc(zeros_set, 1)
            held_in(dve, 0)
            dve.tensor_copy(ident_bf[:, :], w("ident"))
            dve.tensor_copy(later_bf[:, :], w("later"))
            dve.memset(spread_q[:, :, :], 0.0)
            step.then(dve.memset(spread_k[:, :, :], 0.0))
            by_8 = w("ident").rearrange("p (h d) -> p h d", d=DS)
            for n in range(4):
                dve.tensor_copy(spread_q[:, :, 64 + 8 * n:72 + 8 * n], by_8)
            for n in range(3):
                last = dve.tensor_copy(spread_k[:, :, 16 + 32 * n:24 + 32 * n], by_8)
            last.then_inc(const_ok, 1)
            dve.wait_ge(in_mask, 16)
            step.then(dve.tensor_copy(A["qT"][:, 7000:7000 + 8 * KV], mask_i[:, :, :].rearrange("p b n -> p (b n)")))
            step.then(dve.tensor_scalar(A["qT"][:, 7000:7000 + 8 * KV], A["qT"][:, 7000:7000 + 8 * KV], 1.0, -FMIN, ALU.subtract, ALU.mult))

            def carry(j):
                dve.memset(small[:, j, 63:64], 0.0)

            def moments(j, src, done, rms=False, eps=EPS_LN):
                carry(j)
                step.then(dve.bn_stats(stats[:, j, :], src))
                carry(j)
                step.then(dve.bn_aggr(mv[:, j, :], stats[:, j, :]))
                v = mv[:, j, 1:2]
                if rms:
                    v = var[:, j, 1:2]
                    step.then(dve.scalar_tensor_tensor(v, mv[:, j, 0:1], mv[:, j, 0:1], mv[:, j, 1:2], ALU.mult, ALU.add))
                dve.tensor_scalar(var[:, j, 0:1], v, eps, None, ALU.add).then_inc(done, 1)

            def scaled(j, dst, src, rms=False):
                if rms:
                    return dve.tensor_scalar(dst, src, rstd[:, j, 0:1], None, ALU.mult)
                return dve.tensor_scalar(dst, src, mv[:, j, 0:1], rstd[:, j, 0:1], ALU.subtract, ALU.mult)

            def heads_centre(rows, j, dst, src, sm, done):
                step.then(dve.tensor_reduce(sm[0:rows, j, 0:16], src, AX_X, ALU.add))
                step.then(dve.tensor_scalar(sm[0:rows, j, 16:32], sm[0:rows, j, 0:16], 1.0 / 64, None, ALU.mult))
                dve.tensor_tensor(dst, src, sm[0:rows, j, 16:32].unsqueeze(2).broadcast_to([rows, 16, 64]),
                                  ALU.subtract).then_inc(done, 1)

            def heads_var(rows, j, squares, sm, done):
                step.then(dve.tensor_reduce(sm[0:rows, j, 32:48], squares, AX_X, ALU.add))
                dve.tensor_scalar(var[0:rows, j, :], sm[0:rows, j, 32:48], 1.0 / 64, EPS_LN, ALU.mult, ALU.add)\
                   .then_inc(done, 1)

            def by_head(v):
                return v.rearrange("p (h d) -> p h d", d=64)

            def xattn(l):
                L = XATTN[l]
                G, NH, dh = L["G"], L["H"], L["dh"]
                nb = NH // 4
                block_done(dve, 2 * l)
                held_in(dve, [0, 2, 3, 4][l])
                for t in range(NT):
                    last = dve.bn_stats(stats[:, t, :], x_res[:, t * P:(t + 1) * P])
                step.then(last)
                for t in range(NT):
                    last = dve.bn_aggr(mv[:, t, :], stats[:, t, :])
                step.then(last)
                dve.tensor_scalar(var[:, 0, 0:NT].unsqueeze(2), mv[:, :, 1:2], EPS_LN, None, ALU.add).then_inc(x_stat, 1)
                K = kbd[:, 0:B * NH * KV].rearrange("p (b h k) -> p b h k", b=B, k=KV)
                if L["qk_norm"]:
                    dve.wait_ge(kv_ps, l + 1)
                    for b in range(B):
                        heads_centre(KV, 1 + b, by_head(kn[0:KV, b, :]),
                                     by_head(psum[0:KV, 2 * b * BANK:(2 * b + 2) * BANK]), small, kc_ok)
                    for b in range(B):
                        dve.wait_ge(ksq_ok, b + 1)
                        heads_var(KV, 1 + b, by_head(O[0:KV, b, :]), small, kvar_ok)
                    for b in range(B):
                        dve.wait_ge(krstd_ok, b + 1)
                        dve.tensor_tensor(by_head(kn[0:KV, b, :]), by_head(kn[0:KV, b, :]),
                                          rstd[0:KV, 1 + b, :].unsqueeze(2).broadcast_to([KV, 16, 64]), ALU.mult)\
                           .then_inc(kn_ok, 1)
                    dve.wait_ge(kT_ps, 1)
                    for n in range(3):
                        cols = min(3, G - 3 * n) * 2 * KV
                        last = dve.tensor_scalar(kaff[:, n * 462:n * 462 + cols], bank(n, 0, cols),
                                                 w("kn_w"), w("kn_b"), ALU.mult, ALU.add)
                    step.then(last)
                else:
                    dve.wait_ge(kv_ps, l + 1)
                for h in range(NH):
                    g = h * dh // P
                    src = kaff[:, g * 154:g * 154 + 154] if L["qk_norm"] else bank(g // 3, g % 3 * 154, g % 3 * 154 + 154)
                    own = w("headmask", h, h + 1) if dh == DS else w("halfmask", h % 2, h % 2 + 1)
                    dve.tensor_scalar(K[:, :, h, :], src.rearrange("p (b k) -> p b k", b=B), own, None, ALU.mult)
                V = vx[:, 0:B * NH * (dh + 1)].rearrange("p (n d) -> p n d", d=dh + 1)
                dve.memset(V[:, :, dh:dh + 1], 1.0).then_inc(k_ok, 1)

                dve.wait_ge(x_rstd, l + 1)
                for t in range(NT):
                    last = dve.tensor_scalar(xn_all[:, t * P:(t + 1) * P], x_res[:, t * P:(t + 1) * P],
                                             mv[:, t, 0:1], rstd[:, 0, t:t + 1], ALU.subtract, ALU.mult)
                    if t % TB == TB - 1:
                        last.then_inc(x_xn, 1)
                if L["qk_norm"]:
                    for b in range(B):
                        for c in range(4):
                            dve.wait_ge(q_nat, 4 * b + c + 1)
                            heads_centre(P, c, by_head(qn4[:, c, :]), by_head(psum[:, 2 * c * BANK:(2 * c + 2) * BANK]),
                                         small, qc_ok)
                        for c in range(4):
                            dve.wait_ge(qsq_ok, 4 * b + c + 1)
                            heads_var(P, c, by_head(qsq4[:, c, :]), small, qvar_ok)
                        for c in range(4):
                            dve.wait_ge(qrstd_ok, 4 * b + c + 1)
                            dve.tensor_tensor(by_head(qn4[:, c, :]), by_head(qn4[:, c, :]),
                                              rstd[:, c, :].unsqueeze(2).broadcast_to([P, 16, 64]), ALU.mult)\
                               .then_inc(qn_ok, 1)
                else:
                    for n in range(1, B * G, 2):
                        dve.wait_ge(q_ps, QB[l] + n + 1)
                        dve.tensor_copy(qT_all[:, n * S:(n + 1) * S], bank((2 + n) % 8, 0, BANK)).then_inc(q_dve, 1)
                nh, nbp = NH // PARTS[l], nb // PARTS[l]
                with dve.Fori(0, TB) as i:
                    step.loop(i, [6, 10, 10, 10][l])
                    for c, j, part in chains(l):
                        dve.wait_ge(sc_ps, unit(l, i, c) + 8)
                        first = 4 * j + part * nbp
                        raw = psum[:, first * BANK:(first + nbp) * BANK].rearrange("p (c n) -> p c n", n=BANK)[:, :, 0:4 * KV]
                        e = E[:, j, part * nh * KV:(part + 1) * nh * KV]
                        top = small[:, c, 0:nh]
                        if L["mask"]:
                            step.then(dve.scalar_tensor_tensor(
                                e.rearrange("p (c n) -> p c n", c=nb), raw, dh ** -0.5,
                                ext[:, j, :].unsqueeze(1).broadcast_to([P, nb, 4 * KV]), ALU.mult, ALU.add))
                            eh = e.rearrange("p (h k) -> p h k", k=KV)
                            step.then(dve.tensor_reduce(top, eh, AX_X, ALU.max))
                            dve.tensor_tensor(eh, eh, top.unsqueeze(2).broadcast_to([P, NH, KV]), ALU.subtract)\
                               .then_inc(e_ok, 1)
                        else:
                            rawh = raw.rearrange("p c (h k) -> p c h k", k=KV)
                            toph = top.rearrange("p (c h) -> p c h", c=nbp)
                            step.then(dve.tensor_reduce(toph, rawh, AX_X, ALU.max))
                            dve.tensor_tensor(e.rearrange("p (c h k) -> p c h k", c=nbp, k=KV), rawh,
                                              toph.unsqueeze(3).broadcast_to([P, nbp, 4, KV]), ALU.subtract)\
                               .then_inc(e_ok, 1)
                    for c, j, part in chains(l):
                        if l != 1 or part == 1:
                            dve.wait_ge(pT_ps, unit(l, i, c))
                            n = max(1, nbp // 2)
                            lo = (part + 1) * nbp - n
                            dve.tensor_copy(PT[0:KV, j, lo * BANK:(lo + n) * BANK],
                                            psum[0:KV, (4 * j + lo) * BANK:(4 * j + lo + n) * BANK]).then_inc(pT_dve, 1)
                    for c, j, part in chains(l):
                        dve.wait_ge(o_ps, unit(l, i, c))
                        first = 4 * j + part * nbp
                        raw = psum[:, first * BANK:(first + nbp) * BANK].rearrange("p (c n) -> p c n", n=BANK)
                        raw = raw[:, :, 0:4 * (dh + 1)].rearrange("p c (h d) -> p c h d", d=dh + 1)
                        inv = small[:, c, 16:16 + nh].rearrange("p (c h) -> p c h", c=nbp)
                        step.then(dve.reciprocal(inv.unsqueeze(3), raw[:, :, :, dh:dh + 1]))
                        n = G * P // PARTS[l]
                        dve.tensor_tensor(O[:, j, part * n:(part + 1) * n].rearrange("p (c h d) -> p c h d", c=nbp, d=dh),
                                          raw[:, :, :, 0:dh], inv.unsqueeze(3).broadcast_to([P, nbp, 4, dh]), ALU.mult)\
                           .then_inc(o_ok, 1)
                    for j in range(B):
                        dve.wait_ge(y_ps, count(8 * l, i, j))
                        t = x_res[:, tile(i, j)]
                        last = dve.tensor_tensor(t, t, bank(4 * j + YBANK[l], 0, P), ALU.add)
                        if L["bias"]:
                            step.then(last)
                            last = dve.tensor_tensor(t, t, w(f"x{l}_bo"), ALU.add)
                        last.then_inc(x_done, 1)
                    if l == 3:
                        for side in range(2):
                            dve.wait_ge(n_ps, i * 2 + (side + 2))
                            raw = bank(4 * side + 3, 0, 5)
                            dve.tensor_scalar(s1_all[:, bass.ds(i * 8 + side * 4, 4)], raw[:, 0:4], 1e-24, None, ALU.max)
                            dve.tensor_scalar(s2_col[:, bass.ds(i * 2 + side, 1)], raw[:, 4:5], 1e-24, None, ALU.max)\
                               .then_inc(n_max, 1)
                step.end(TB)
                dve.wait_ge(x_done, 2 + NT * (l + 1))

            def selfattn(u):
                l = 2 * u
                held_in(dve, [1, 3][u])
                if u == 0:
                    dve.wait_ge(zeros_out, 16 * (SLOTS // 1024))
                with dve.Fori(0, TB) as i:
                    step.loop(i, [10, 12][u])
                    for j in range(B):
                        moments(j, x_res[:, tile(i, j)], a_stat)
                    for j in range(B):
                        dve.wait_ge(a_rstd, count(8 * l, i, j))
                        step.then(scaled(j, r_res[:, tile(i, j)], x_res[:, tile(i, j)]))
                        moments(j, r_res[:, tile(i, j)], b_stat, rms=(u == 1), eps=[EPS_LN, 1e-6][u])
                    for j in range(B):
                        dve.wait_ge(b_rstd, count(8 * u, i, j))
                        scaled(j, xn[:, j, :], r_res[:, tile(i, j)], rms=(u == 1)).then_inc(b_xn, 1)
                    for j in range(B):
                        dve.wait_ge(qkv_ps, count(8 * l, i, j))
                        qp, kp, vp = (bank(4 * j + 1, n * P, n * P + P) for n in range(3))
                        vd = v_all[:, tile(i, j)]
                        if u == 0:
                            dve.tensor_scalar(q_all[:, tile(i, j)], qp, w("s0_q_b"), DS ** -0.5, ALU.add, ALU.mult)
                            dve.tensor_scalar(k_all[:, tile(i, j)], kp, w("s0_k_b"), None, ALU.add)
                            last = dve.tensor_tensor(vd, vp, w("s0_v_b"), ALU.add)
                        else:
                            dve.tensor_scalar(q_all[:, tile(i, j)], qp, DS ** -0.5, None, ALU.mult)
                            dve.tensor_copy(k_all[:, tile(i, j)], kp)
                            last = dve.tensor_copy(vd, vp)
                        last.then_inc(qkv_ok, 1)
                step.end(TB)
                dve.wait_ge(qkv_ok, NT * (u + 1))
                for b in range(B):
                    pair = [(x[:, b * S:(b + 1) * S], parts[:, :, b * S:(b + 1) * S])
                            for x, parts in ((k_all, k_parts), (q_all, q_parts))]
                    for n in range(3):
                        for x_, parts in pair:
                            last = dve.tensor_copy(parts[:, n, :], x_)
                        if n == 2:
                            last.then_inc(split_ok, 1)
                            continue
                        step.then(last)
                        for x_, parts in pair:
                            last = dve.tensor_tensor(x_, x_, parts[:, n, :], ALU.subtract)
                        step.then(last)
                    with dve.Fori(0, HS // 4) as i:
                        for k in range(4):
                            dve.wait_ge(rk_ps, i * 4 + ((u * B + b) * HS + k + 1))
                            dve.tensor_scalar(k_rep[:, bass.ds(i * (4 * B * S) + (k * B * S + b * S), S)],
                                              bank(2 * k, 0, BANK, ROWS), 1.0, None, ALU.mult).then_inc(rk_ok, 1)
                dve.wait_ge(split_ok, B * (u + 1))
                step.then(dve.memset(v_wide, 0.0))

                def widen(b):
                    wide = v_wide.rearrange("p (n r c) -> p n r c", r=4, c=32)
                    now = v_all[:, bass.ds(b * S, S)].rearrange("p (n r d) -> p n r d", r=4, d=DS)
                    for n in range(4):
                        last = dve.tensor_copy(wide[:, :, n, DS * n:DS * n + DS], now[:, :, n, :])
                    last.then_inc(v_wide_ok, 1)

                def normalise(o, par):
                    dve.wait_ge(up_ok, o * HS + (LEAD + u * UNITS + HS))
                    dve.reciprocal(small[:, 3, 0:HS], small[:, 1 + par, 0:HS]).then_inc(inv_ok, 1)
                    dve.wait_ge(inv_ok, o * 2 + (2 * NT * u + 1))
                    dve.tensor_copy(cc[:, 0, :].rearrange("p (h d) -> p h d", d=DS),
                                    small[:, 3, 0:HS].unsqueeze(2).broadcast_to([P, HS, DS])).then_inc(inv_ok, 1)
                    dve.wait_ge(r_ps, o + (NT * u + 1))
                    carry(3)
                    dve.tensor_copy(xn[:, 0, :], bank(6 + par, P, 2 * P)).then_inc(invT_ok, 1)
                    dve.wait_ge(invT_ok, o + (NT * u + 1))
                    dve.tensor_tensor(ctxT_all[:, bass.ds(o * P, P)], bank(6 + par, 0, P), xn[:, 0, :],
                                      ALU.mult).then_inc(ctx_ok, 1)

                for o, b, qt, W in q_tiles(dve, u, widen):
                    base = u * UNITS
                    for h in range(HS + 2):
                        if h < HS:
                            dve.wait_ge(us_ps, o * HS + (LEAD + base + h + 1))
                            dve.tensor_reduce(small[:, 0, h:h + 1], bank(h % 4, 0, W), AX_X, ALU.max, negate=True)\
                               .then_inc(um_ok, 1)
                        g = h - 2
                        if g > 0 and g % 2:
                            dve.wait_ge(upT_ps, o * HS + (LEAD + base + g + 1))
                            dve.wait_ge(uo_ps, o * HS + (LEAD + base + g - 3))
                            dve.tensor_copy(ptself[:, (g % 4) * BANK:(g % 4) * BANK + W], bank(5, 0, W)).then_inc(upT_dve, 1)
                        if h == LATE and qt:
                            normalise(o - 1, (qt - 1) % 2)
                    if qt == TB - 1:
                        normalise(o, qt % 2)

            def logits_out(l, i):
                E_ = MOE[l]["E"]
                for j in range(B):
                    dve.wait_ge(lg_ps, count(8 * l, i, j))
                    dst = logits[:, bass.ds(i * E_ + j * TB * E_, E_)]
                    src = bank(4 * j + 2, 0, E_)
                    if l == 3:
                        dve.tensor_tensor(dst, src, w("m3_gate_b"), ALU.add).then_inc(lg_ok, 1)
                    else:
                        dve.tensor_scalar(dst, src, 1.0, None, ALU.mult).then_inc(lg_ok, 1)

            def moe_input(l):
                held_in(dve, [1, 2, 3, 4][l])
                with dve.Fori(0, TB) as i:
                    step.loop(i, [10, 0, 10, 4][l])
                    for j in range(B):
                        x_t, r_t = x_res[:, tile(i, j)], r_res[:, tile(i, j)]
                        if l == 3:
                            moments(j, x_t, m_stat)
                            continue
                        dve.wait_ge(t_y, count(8 * l, i, j))
                        step.then(dve.tensor_tensor(r_t, r_t, bank(4 * j + 1, 0, P), ALU.add))
                        if l == 0:
                            step.then(dve.tensor_tensor(r_t, r_t, w("s0_o_b"), ALU.add))
                        step.then(dve.tensor_tensor(x_t, x_t, r_t, ALU.add))
                        moments(j, r_t, m_stat, rms=(l == 2), eps=[EPS_LN, 0, 1e-6][l])
                    for j in range(B):
                        dve.wait_ge(m_rstd, count(8 * l, i, j))
                        src = x_res if l == 3 else r_res
                        scaled(j, xn[:, j, :], src[:, tile(i, j)], rms=(l == 2)).then_inc(m_xn, 1)
                    logits_out(l, i)
                step.end(TB)

            def two_token():
                held_in(dve, 2)
                sc = H["sc"]
                heads = lambda v: v.rearrange("p (h d) -> p h d", d=32)
                with dve.Fori(0, TB) as i:
                    step.loop(i, 33)
                    for j in range(B):
                        moments(j, x_res[:, tile(i, j)], a_stat)
                    for j in range(B):
                        dve.wait_ge(a_rstd, count(8, i, j))
                        scaled(j, xn[:, j, :], x_res[:, tile(i, j)]).then_inc(h0_ok, 1)
                        step.then(scaled(j, r_res[:, tile(i, j)], x_res[:, tile(i, j)]))
                    for j in range(B):
                        dve.wait_ge(qkv_ps, count(8, i, j))
                        step.then(dve.tensor_tensor(qkv[:, j, :], bank(4 * j + 1, 0, 384), w("h_bqkv"), ALU.add))
                    for j in range(B):
                        step.then(dve.tensor_tensor(prod[:, j * 256:j * 256 + 256].rearrange("p (b n) -> p b n", b=B),
                                                    qkv[:, j, 0:P].unsqueeze(1).broadcast_to([P, B, P]),
                                                    qkv[:, :, P:2 * P], ALU.mult))
                    step.then(dve.tensor_reduce(sc[:, 0:16], heads(prod), AX_X, ALU.add))
                    s4 = sc[:, 0:16].rearrange("p (q k h) -> p q k h", q=2, k=2)
                    top = sc[:, 16:24].rearrange("p (q h) -> p q h", q=2)
                    step.then(dve.tensor_tensor(top, s4[:, :, 0, :], s4[:, :, 1, :], ALU.max))
                    dve.tensor_tensor(s4, s4, top.unsqueeze(2).broadcast_to([P, 2, 2, 4]), ALU.subtract).then_inc(t1_e, 1)
                    dve.wait_ge(t1_p, i + 1)
                    step.then(dve.tensor_tensor(top, s4[:, :, 0, :], s4[:, :, 1, :], ALU.add))
                    step.then(dve.reciprocal(top, top))
                    step.then(dve.tensor_tensor(s4, s4, top.unsqueeze(2).broadcast_to([P, 2, 2, 4]), ALU.mult))
                    for j in range(B):
                        for k in range(B):
                            step.then(dve.tensor_tensor(heads(prod[:, k * P:k * P + P]), heads(qkv[:, k, 2 * P:3 * P]),
                                                        s4[:, j, k, :].unsqueeze(2).broadcast_to([P, 4, 32]), ALU.mult))
                        dve.tensor_tensor(cc[:, j, :], prod[:, 0:P], prod[:, P:2 * P], ALU.add).then_inc(t1_av, 1)
                        dve.wait_ge(t1_av, count(0, i, j))
                    for j in range(B):
                        r_t = r_res[:, tile(i, j)]
                        dve.wait_ge(t_y, count(8, i, j))
                        step.then(dve.tensor_tensor(r_t, r_t, bank(4 * j + 1, 0, P), ALU.add))
                        step.then(dve.tensor_tensor(r_t, r_t, w("h_bo"), ALU.add))
                        moments(j, r_t, m_stat)
                    for j in range(B):
                        r_t = r_res[:, tile(i, j)]
                        dve.wait_ge(m_rstd, count(8, i, j))
                        step.then(scaled(j, yb[:, j, :], r_t))
                        step.then(dve.tensor_tensor(yb[:, j, :], yb[:, j, :], w("h_g1"), ALU.mult))
                        dve.tensor_tensor(yb[:, j, :], yb[:, j, :], w("h_be1"), ALU.add).then_inc(m_xn, 1)
                        dve.wait_ge(m_xn, count(8, i, j))
                        step.then(dve.tensor_scalar(r_t, yb[:, j, :], 1.0, None, ALU.mult))
                    logits_out(1, i)
                step.end(TB)

            def norms3():
                dve.wait_ge(n_gv, 1)
                dve.tensor_scalar(small[0:8, 0, 33:34], small[0:8, 0, 32:33], 1e-24, None, ALU.max).then_inc(n_max, 1)
                dve.wait_ge(n_pow, 1)
                dve.tensor_scalar(M["gv"][0:8, :], w("m3_gate_v"), small[0:8, 0, 33:34], None, ALU.mult).then_inc(n_pow, 1)

            def norm_rows3():
                dve.wait_ge(n_ok, 1)
                for n in range(2):
                    for e in range(4 * n, 4 * n + 4):
                        last = dve.tensor_scalar(M["diag"][:, e * P:(e + 1) * P], w("ident"), s2_col[:, e:e + 1], None, ALU.mult)
                    last.then_inc(n_diag, 1)

            def top_mask(dst, src, n, shape):
                bc = lambda v: v.unsqueeze(2).broadcast_to(shape)
                best = small[:, 0, 0:NT] if n == 0 else small[:, 0, 8:16]
                first = small[:, 0, 16:24]
                step.then(dve.tensor_reduce(best, src, AX_X, ALU.max))
                step.then(dve.tensor_tensor(dst, src, bc(best), ALU.is_equal))
                step.then(dve.tensor_tensor(dst, dst, w("firstness", 0, shape[2]).unsqueeze(1).broadcast_to(shape), ALU.mult))
                step.then(dve.tensor_reduce(first, dst, AX_X, ALU.max))
                step.then(dve.tensor_tensor(dst, dst, bc(first), ALU.is_equal))

            def gating(l):
                E_ = MOE[l]["E"]
                shape = [P, NT, E_]
                n = NT * E_
                bc = lambda v: v.unsqueeze(2).broadcast_to(shape)
                t3 = lambda v: v[:, 0:n].rearrange("p (t e) -> p t e", e=E_)
                LG, ga, gb, gc = t3(logits), t3(M["ga"]), t3(M["gb"]), t3(M["gc"])
                G_ = gates[:, :, 0:E_]
                total = small[:, 0, 24:32]
                dve.wait_ge(lg_ok, NT * (l + 1))
                if l == 1:
                    top_mask(ga, LG, 0, shape)
                    dve.tensor_copy(G_, ga).then_inc(gate_ok, 1)
                elif l == 3:
                    top_mask(ga, LG, 0, shape)
                    step.then(dve.scalar_tensor_tensor(M["gc"][:, 0:n], M["ga"][:, 0:n], FMIN, logits[:, 0:n], ALU.mult, ALU.add))
                    top_mask(gb, gc, 1, shape)
                    dve.tensor_tensor(G_, ga, gb, ALU.add).then_inc(gate_ok, 1)
                else:
                    m1, m2 = (M["m12"][:, k * n:k * n + n] for k in range(2))
                    top_mask(t3(m1), LG, 0, shape)
                    step.then(dve.scalar_tensor_tensor(M["gc"][:, 0:n], m1, FMIN, logits[:, 0:n], ALU.mult, ALU.add))
                    top_mask(t3(m2), gc, 1, shape)
                    dve.tensor_tensor(gc, LG, bc(small[:, 0, 0:NT]), ALU.subtract).then_inc(g_sub, 1)
                    dve.wait_ge(g_exp, [1, 0, 2][l])
                    step.then(dve.tensor_reduce(total, gc, AX_X, ALU.add))
                    step.then(dve.reciprocal(total, total))
                    step.then(dve.tensor_tensor(gc, gc, bc(total), ALU.mult))
                if l == 0:
                    m12 = M["m12"].rearrange("p (k t e) -> p k t e", k=2, t=NT)
                    pre = M["pre"].rearrange("p (k t e) -> p k t e", k=2, t=NT)
                    step.then(dve.memset(pre[:, :, 0, :], 0.0))
                    for t in range(1, NT):
                        step.then(dve.tensor_tensor(pre[:, :, t, :], pre[:, :, t - 1, :], m12[:, :, t - 1, :], ALU.add))
                    dve.tensor_tensor(M["tot"], pre[:, 0, NT - 1, :], m12[:, 0, NT - 1, :], ALU.add).then_inc(g_m, 1)
                    dve.wait_ge(g_loc, 1)
                    step.then(dve.scalar_tensor_tensor(M["mk"], bank(0, 0, 2 * n), float(CAPACITY), M["m12"], ALU.is_le, ALU.mult))
                    q3 = lambda v: v.rearrange("p (n e) -> p n e", e=E_)
                    place, kept, to = (D["slot"][:, a:a + 16] for a in (0, 16, 32))
                    step.then(dve.tensor_tensor(q3(D["loc"]), q3(bank(0, 0, 2 * n)),
                                                w("queue").unsqueeze(1).broadcast_to([P, 2 * NT, E_]), ALU.add))
                    step.then(dve.tensor_tensor(D["loc"], D["loc"], M["mk"], ALU.mult))
                    step.then(dve.tensor_reduce(place, q3(D["loc"]), AX_X, ALU.add))
                    step.then(dve.tensor_reduce(kept, q3(M["mk"]), AX_X, ALU.add))
                    step.then(dve.tensor_scalar(to, kept, -float(DROPPED), float(DROPPED), ALU.mult, ALU.add))
                    step.then(dve.tensor_tensor(to, to, place, ALU.add))
                    dve.tensor_copy(slot_i[:, 16:32], place)
                    dve.tensor_copy(slot_i[:, 0:16], to).then_inc(slots_ok, 1)
                    step.then(dve.tensor_tensor(M["ga"], M["mk"][:, 0:n], M["mk"][:, n:2 * n], ALU.add))
                    step.then(dve.tensor_tensor(M["ga"], M["ga"], M["gc"], ALU.mult))
                    step.then(dve.tensor_reduce(total, ga, AX_X, ALU.add))
                    step.then(dve.tensor_scalar(total, total, float(np.finfo(np.float32).eps), None, ALU.max))
                    step.then(dve.reciprocal(total, total))
                    step.then(dve.tensor_scalar(total, total, 0.8, None, ALU.mult))
                    dve.tensor_tensor(G_, ga, bc(total), ALU.mult).then_inc(gate_ok, 1)
                    dve.wait_ge(gate_ok, 1)
                    mk4 = M["mk"].rearrange("p (k t e) -> p k t e", k=2, t=NT)
                    for k in range(2):
                        step.then(dve.tensor_tensor(mk4[:, k], mk4[:, k], G_, ALU.mult))
                    step.then(dve.tensor_reduce(D["slot"][:, 48:64], q3(M["mk"]), AX_X, ALU.add))
                if l == 2:
                    step.then(dve.tensor_reduce(small[:, 0, 0:NT], gc, AX_X, ALU.max))
                    dve.tensor_tensor(gc, gc, bc(small[:, 0, 0:NT]), ALU.subtract).then_inc(g_sub, 1)
                    dve.wait_ge(g_exp, 3)
                    step.then(dve.tensor_tensor(M["ga"][:, 0:n], m1, m2, ALU.add))
                    step.then(dve.tensor_tensor(ga, ga, gc, ALU.mult))
                    step.then(dve.tensor_reduce(total, ga, AX_X, ALU.add))
                    step.then(dve.reciprocal(total, total))
                    step.then(dve.tensor_tensor(G_, ga, bc(total), ALU.mult))
                    step.then(dve.memset(gates[:, :, E_:E_ + 1], 1.0))
                if l != 2:
                    acc = r_res if l == 1 else x_res
                    dve.wait_ge(b2_ps, [1, 2, 0, 3][l])
                    dve.wait_ge(gate_ok, [1, 2, 0, 3][l])
                    dve.tensor_tensor(acc[:, :], acc[:, :], psum[:, 2 * BANK:4 * BANK], ALU.add).then_inc(b2_ok, 1)
                    dve.wait_ge(b2_ok, [1, 2, 0, 3][l])

            def experts(l):
                acc = r_res if l == 1 else x_res
                gflat = M["gates"]

                def product(e, side, b):
                    if l != 2:
                        return
                    for c in range(2):
                        dve.wait_ge(sg_ok, e * 4 + (2 + 2 * b + c + 1))
                        dve.wait_ge(h_ps, e * 8 + (HPB[l] + 4 * b + 2 + c + 1))
                        if c == 0:
                            dve.wait_ge(ye_ps, e * 2 + (2 + KB[l] + b - 1))
                        dve.tensor_tensor(hT[:, b, c * BANK:(c + 1) * BANK], sg[:, b, c * BANK:(c + 1) * BANK],
                                          bank(2 + c, 0, BANK), ALU.mult).then_inc(h2_ok, 1)

                def gather(e, side, b):
                    dve.wait_ge(ye_ps, e * 2 + (2 + KB[l] + b + 1))
                    dve.wait_ge(acc_ok, e * 2 + (2 + KB[l] + b - 1))
                    for t in range(TB):
                        a = acc[:, b * S + t * P:b * S + t * P + P]
                        last = dve.scalar_tensor_tensor(a, bank(4 + b, t * P, t * P + P),
                                                        gflat[:, bass.ds(e + (b * TB + t) * 16, 1)], a, ALU.mult, ALU.add)
                    last.then_inc(acc_ok, 1)

                expert_order(dve, l, product, gather)
                dve.wait_ge(acc_ok, 2 + KB[l + 1])

            def experts0():
                def features(e, side, i):
                    dve.wait_ge(d_T, e + 1)
                    dve.tensor_scalar(D["xe"][:, side % 2 * P:(side % 2 + 1) * P], bank(side % 2, 0, P),
                                      w("s0_ln2_w"), w("s0_ln2_b"), ALU.mult, ALU.add).then_inc(d_xe, 1)

                def answer(e, side, i):
                    dve.wait_ge(d_O, e + 1)
                    dve.wait_ge(d_stored[side], i * 16 + 16)
                    dve.tensor_copy(D["y"][:, side * P:(side + 1) * P], bank(4 + side % 2, 0, P)).then_inc(d_y, 1)

                run_queues(dve, (features, 2), (answer, 0))
                for n in range(2 * NT):
                    if n % 4 == 0:
                        dve.wait_ge(d_back[n // 4], 16 * 4)
                    a = x_res[:, n % NT * P:(n % NT + 1) * P]
                    last = dve.scalar_tensor_tensor(a, D["back"][:, n * P:(n + 1) * P], D["slot"][:, 48 + n:49 + n], a,
                                                    ALU.mult, ALU.add)
                    if n == NT - 1:
                        step.then(last)
                last.then_inc(d_done, 1)
                dve.wait_ge(d_done, 1)

            def last_norm():
                with dve.Fori(0, TB) as i:
                    step.loop(i, 10)
                    for j in range(B):
                        moments(j, r_res[:, tile(i, j)], f_stat)
                    for j in range(B):
                        r_t, x_t = r_res[:, tile(i, j)], x_res[:, tile(i, j)]
                        dve.wait_ge(f_rstd, count(0, i, j))
                        step.then(scaled(j, r_t, r_t))
                        step.then(dve.tensor_tensor(r_t, r_t, w("h_g2"), ALU.mult))
                        step.then(dve.tensor_tensor(r_t, r_t, w("h_be2"), ALU.add))
                        dve.tensor_tensor(x_t, x_t, r_t, ALU.add).then_inc(f_done, 1)
                step.end(TB)
                dve.wait_ge(f_done, NT)

            for l in range(4):
                if STAGES > 2 * l:
                    xattn(l)
                if STAGES > 2 * l + 1:
                    if l == 1:
                        two_token()
                    elif l == 3:
                        norms3()
                        moe_input(l)
                        norm_rows3()
                    else:
                        selfattn(l // 2)
                        moe_input(l)
                    gating(l)
                    experts(l) if l else experts0()
                    if l == 1:
                        last_norm()

        @block.tensor
        def _(pe):
            pe.sem_inc(us_ps, LEAD)
            pe.sem_inc(sc_ps, 8)
            pe.sem_inc(upT_ps, LEAD)
            pe.sem_inc(uo_ps, LEAD)
            pe.sem_inc(ye_ps, 2)
            pe.sem_inc(n_ps, 1)
            ident = w("ident")
            mm, turn = pe.matmul, pe.transpose

            def xattn(l):
                L = XATTN[l]
                G, NH, dh = L["G"], L["H"], L["dh"]
                wq, wk, wv, wo, cT = (w(n) for n in (f"x{l}_wq", f"x{l}_wk", f"x{l}_wv", f"x{l}_wo", "ctxT"))
                block_done(pe, 2 * l)
                held_in(pe, [0, 2, 3, 4][l])
                for b in range(B):
                    for n in range(max(1, NH * dh // BANK)):
                        cols = min(BANK, NH * dh)
                        mm(bank(4 + 2 * b + n, 0, cols, KV), cT[:, b * KV:(b + 1) * KV],
                           wv[:, n * BANK:n * BANK + cols], start=True, stop=True)
                if L["qk_norm"]:
                    for b in range(B):
                        for n in range(2):
                            last = mm(bank(2 * b + n, 0, BANK, KV), cT[:, b * KV:(b + 1) * KV],
                                      wk[:, n * BANK:(n + 1) * BANK], start=True, stop=True)
                    last.then_inc(kv_ps, 1)
                    pe.wait_ge(kn_ok, B)
                    for g in range(G):
                        for b in range(B):
                            a = g % 3 * 154 + b * KV
                            last = turn(bank(g // 3, a, a + KV), kn[0:KV, b, g * P:(g + 1) * P], ident[0:KV, 0:KV])
                    last.then_inc(kT_ps, 1)
                else:
                    for g in range(G):
                        last = mm(bank(g // 3, g % 3 * 154, g % 3 * 154 + 154), wk[:, g * P:(g + 1) * P], cT,
                                  start=True, stop=True)
                    last.then_inc(kv_ps, 1)
                pe.wait_ge(k_ok, l + 1)
                pe.wait_ge(v_ok, l + 1)
                K = kbd[:, 0:B * NH * KV].rearrange("p (b n) -> p b n", b=B)
                V = vx[:, 0:B * NH * (dh + 1)].rearrange("p (b h d) -> p b h d", b=B, d=dh + 1)
                for b in range(B):
                    pe.wait_ge(x_xn, 2 * l + b + 1)
                    for t in range(TB):
                        last = turn(bank(b, t * P, (t + 1) * P), xn_all[:, b * S + t * P:b * S + (t + 1) * P], ident)
                    last.then_inc(x_xTp, 1)
                if L["qk_norm"]:
                    pe.wait_ge(x_xT, 2 * l + 2)
                    for b in range(B):
                        for c in range(4):
                            if b:
                                pe.wait_ge(qT_ok, c + 1)
                            for n in range(2):
                                last = mm(bank(2 * c + n, 0, BANK), xT_all[:, b * S + c * P:b * S + (c + 1) * P],
                                          wq[:, n * BANK:(n + 1) * BANK], start=True, stop=True)
                            last.then_inc(q_nat, 1)
                        for c in range(4):
                            pe.wait_ge(qn_ok, 4 * b + c + 1)
                            for g in range(G):
                                a = 2 * c * BANK + g * P
                                last = turn(psum[:, a:a + P], qn4[:, c, g * P:(g + 1) * P], ident)
                            last.then_inc(qnT_ps, 1)
                    pe.wait_ge(qT_ok, NT)
                else:
                    for n in range(B * G):
                        b, g = n // G, n % G
                        pe.wait_ge(x_xT, 2 * l + (1 if n < min(G, 6) else 2))
                        if n >= 8:
                            pe.wait_ge(q_dve if n % 2 else q_act, QB[l] // 2 + (n - 8) // 2 + 1)
                        mm(bank((2 + n) % 8, 0, BANK), wq[:, g * P:(g + 1) * P], xT_all[:, b * S:(b + 1) * S],
                           start=True, stop=True).then_inc(q_ps, 1)
                    pe.wait_ge(q_act, QB[l] // 2 + G)
                    pe.wait_ge(q_dve, QB[l] // 2 + G)
                nh, nbp, gp = NH // PARTS[l], NH // 4 // PARTS[l], max(1, G // PARTS[l])
                with pe.Fori(0, TB) as i:
                    for c, j, part in chains(l):
                        if part == 0:
                            pe.wait_ge(xq_ok, count(8 * l, i, j))
                            pe.wait_ge(x_done, count(8 * l, i, j))
                            if l == 3:
                                pe.wait_ge(n_max, count(0, i, j))
                        if G == 1:
                            for n in range(4):
                                last = mm(bank(4 * j + n, 0, 4 * KV), qcur2[:, j, 0:P], K[:, j, n * 4 * KV:(n + 1) * 4 * KV],
                                          start=True, stop=True)
                        else:
                            for g in range(part * gp, (part + 1) * gp):
                                last = mm(bank(4 * j + g // 2, g % 2 * 154, g % 2 * 154 + 154), qcur2[:, j, g * P:(g + 1) * P],
                                          K[:, j, g * 154:(g + 1) * 154], start=True, stop=True)
                        last.then_inc(sc_ps, 1)
                    for c, j, part in chains(l):
                        pe.wait_ge(p_ok, unit(l, i, c))
                        for h in range(part * nh, (part + 1) * nh):
                            a = 4 * j * BANK + h * P
                            last = turn(psum[0:KV, a:a + P], E[:, j, h * KV:(h + 1) * KV], ident)
                        last.then_inc(pT_ps, 1)
                    for c, j, part in chains(l):
                        by_act, by_dve = turned_by(l, i, j, part)
                        if by_act is not None:
                            pe.wait_ge(pT_act, by_act)
                        if by_dve is not None:
                            pe.wait_ge(pT_dve, by_dve)
                        for h in range(part * nh, (part + 1) * nh):
                            a = h % 4 * (dh + 1)
                            last = mm(bank(4 * j + h // 4, a, a + dh + 1), PT[0:KV, j, h * P:(h + 1) * P], V[:, j, h, :],
                                      start=True, stop=True)
                        last.then_inc(o_ps, 1)
                    for c, j, part in chains(l):
                        pe.wait_ge(o_ok, unit(l, i, c))
                        for g in range(gp):
                            a = (4 * j + part * nbp) * BANK + g * P
                            n = part * gp + g
                            last = turn(psum[:, a:a + P], O[:, j, n * P:(n + 1) * P], ident)
                        last.then_inc(oT_ps, 1)
                    for c, j, part in chains(l):
                        pe.wait_ge(oT_ok, unit(l, i, c))
                        for g in range(part * gp, (part + 1) * gp):
                            last = mm(bank(4 * j + YBANK[l], 0, P), OT[:, j, g * P:(g + 1) * P], wo[:, g * P:(g + 1) * P],
                                      start=(g == 0), stop=(g == G - 1))
                        if part == PARTS[l] - 1:
                            last.then_inc(y_ps, 1)
                    if l == 3:
                        for side in range(2):
                            pe.wait_ge(n_sq, i * 2 + (side + 1))
                            for c in range(8):
                                at_ = min(c, 4)
                                last = mm(bank(4 * side + 3, at_, at_ + 1), sq[:, side, c * P:(c + 1) * P],
                                          w("ones", 0, 1), start=(c <= 4), stop=(c < 4 or c == 7))
                            last.then_inc(n_ps, 1)

            def selfattn(u):
                l = 2 * u
                held_in(pe, [1, 3][u])
                wq, wk, wv = (w(f"s{l}_{n}_w") for n in "qkv")
                with pe.Fori(0, TB) as i:
                    for j in range(B):
                        pe.wait_ge(b_xn, count(8 * u, i, j))
                        turn(bank(4 * j, 0, P), xn[:, j, :], ident).then_inc(s_xTp, 1)
                    for j in range(B):
                        pe.wait_ge(s_xT, count(8 * l, i, j))
                        for n, (lhs, rhs) in enumerate(((wq, xT[:, j, :]), (wk, xT[:, j, :]), (xT[:, j, :], wv))):
                            last = mm(bank(4 * j + 1, n * P, n * P + P), lhs, rhs, start=True, stop=True)
                        last.then_inc(qkv_ps, 1)
                pe.wait_ge(const_ok, 1)
                flat_q, flat_k = (v[:, :, :].rearrange("p h n -> p (h n)") for v in (spread_q, spread_k))
                for b in range(B):
                    pe.wait_ge(split_ok, B * u + b + 1)
                    with pe.Fori(0, HS // 4) as i:
                        for k in range(4):
                            pe.wait_ge(rk_ok, i * 4 + ((u * B + b) * HS + k + 1))
                            for n in range(3):
                                onto = flat_k[:, bass.ds(i * 448 + (k * 112 + 16 - 8 * n), ROWS)]
                                last = mm(bank(2 * k, 0, BANK, ROWS), onto,
                                          k_parts[:, n, b * S:(b + 1) * S], start=(n == 0), stop=(n == 2))
                            last.then_inc(rk_ps, 1)
                            pe.wait_ge(rq_ok, i * 4 + ((u * B + b) * HS + k + 1))
                            for n in range(3):
                                onto = flat_q[:, bass.ds(i * 640 + (k * 160 + 64 - 32 * n), ROWS)]
                                last = mm(bank(2 * k + 1, 0, BANK, ROWS), onto,
                                          q_parts[:, n, b * S:(b + 1) * S], start=(n == 0), stop=(n == 2))
                            last.then_inc(rq_ps, 1)
                pe.wait_ge(rk_ok, LEAD + B * HS * (u + 1))
                pe.wait_ge(rq_ok, LEAD + B * HS * (u + 1))
                base = u * UNITS
                def turn_inverse(o, par):
                    pe.wait_ge(inv_ok, o * 2 + (2 * NT * u + 2))
                    turn(bank(6 + par, P, 2 * P), cc[:, 0, :], ident).then_inc(r_ps, 1)

                for o, b, qt, W in q_tiles(pe, u):
                    par = qt % 2
                    for step in range(HS + 3):
                        h = step
                        if h < HS:
                            pe.wait_ge(up_ok, o * HS + (LEAD + base + h - 3))
                            last = mm(bank(h % 4, 0, W), q_rep[:, bass.ds(b * S + qt * P + h * B * S, P)],
                                      k_rep[:, bass.ds(b * S + h * B * S, W)], start=True, stop=True)
                            if u == 0:
                                last = mm(bank(h % 4, W - P, W), ident_bf[:, :], later_bf[:, :], start=False, stop=True,
                                          skip_group_check=True)
                            last.then_inc(us_ps, 1)
                        h = step - 2
                        if 0 <= h < HS:
                            pe.wait_ge(up_ok, o * HS + (LEAD + base + h + 1))
                            free = upT_dve if h % 2 else upT_act
                            pe.wait_ge(free, o * (HS // 2) + (LEAD + base // 2 + h // 2))
                            for k in range(W // P):
                                last = turn(bank(4 + h % 2, k * P, k * P + P),
                                            pself[:, (h % 4) * BANK + k * P:(h % 4) * BANK + k * P + P], ident)
                            last.then_inc(upT_ps, 1)
                        h = step - 3
                        if 0 <= h:
                            done = upT_dve if h % 2 else upT_act
                            pe.wait_ge(done, o * (HS // 2) + (LEAD + base // 2 + h // 2 + 1))
                            if h == 0:
                                pe.wait_ge(v_wide_ok, b + (B * u + 1))
                                pe.wait_ge(ctx_ok, o + (NT * u + 1))
                            for k in range(W // P):
                                a = h // 4 * 32
                                last = mm(psum[a:a + 32, (6 + par) * BANK:(6 + par) * BANK + P],
                                          v_wide[:, k * BANK + h * 32:k * BANK + h * 32 + 32],
                                          ptself[:, (h % 4) * BANK + k * P:(h % 4) * BANK + k * P + P],
                                          start=(h % 4 == 0 and k == 0), stop=(h % 4 == 3 and k == W // P - 1),
                                          skip_group_check=True)
                            last.then_inc(uo_ps, 1)
                        if step == LATE and qt:
                            turn_inverse(o - 1, (qt - 1) % 2)
                    if qt == TB - 1:
                        turn_inverse(o, par)

            def router(l, i):
                for j in range(B):
                    pe.wait_ge(m_xT, count(8 * l, i, j))
                    router_w = M["gwT"] if l == 3 else w(f"m{l}_router")
                    mm(bank(4 * j + 2, 0, MOE[l]["E"]), xT[:, j, :], router_w, start=True, stop=True).then_inc(lg_ps, 1)

            def moe_input(l):
                held_in(pe, [1, 2, 3, 4][l])
                with pe.Fori(0, TB) as i:
                    if l in (0, 2):
                        for j in range(B):
                            pe.wait_ge(t_cc, count(8 * (l // 2), i, j))
                            mm(bank(4 * j + 1, 0, P), cc[:, j, :], w(f"s{l}_o_w"), start=True, stop=True).then_inc(t_y, 1)
                    for j in range(B):
                        pe.wait_ge(m_xn, count(8 * l, i, j))
                        turn(bank(4 * j, 0, P), xn[:, j, :], ident).then_inc(m_xTp, 1)
                    router(l, i)

            def two_token():
                held_in(pe, 2)
                with pe.Fori(0, TB) as i:
                    for j in range(B):
                        pe.wait_ge(h0_ok, count(0, i, j))
                        turn(bank(4 * j, 0, P), xn[:, j, :], ident).then_inc(s_xTp, 1)
                    for j in range(B):
                        pe.wait_ge(s_xT, count(8, i, j))
                        mm(bank(4 * j + 1, 0, 384), xT[:, j, :], w("h_wqkv"), start=True, stop=True).then_inc(qkv_ps, 1)
                    for j in range(B):
                        pe.wait_ge(t1_av, count(0, i, j))
                        turn(bank(4 * j, 0, P), cc[:, j, :], ident).then_inc(t_ccT, 1)
                    for j in range(B):
                        pe.wait_ge(t_ccS, count(0, i, j))
                        mm(bank(4 * j + 1, 0, P), xT[:, j, :], w("h_wo"), start=True, stop=True).then_inc(t_y, 1)
                    for j in range(B):
                        pe.wait_ge(m_xn, count(8, i, j))
                        turn(bank(4 * j, 0, P), yb[:, j, :], ident).then_inc(m_xTp, 1)
                    router(1, i)

            def norms3():
                held_in(pe, 4)
                pe.wait_ge(n_pow, 2)
                turn(bank(7, 0, 8), M["gv"][0:8, :], ident[0:8, 0:8]).then_inc(n_gvT, 1)
                pe.wait_ge(n_gv, 2)

            def norm_rows3():
                for n in range(2):
                    pe.wait_ge(n_diag, n + 1)
                    mm(bank(4 + n, 0, BANK), w("ones"), M["diag"][:, n * BANK:(n + 1) * BANK],
                       start=True, stop=True).then_inc(n_row, 1)

            def gating(l):
                E_ = MOE[l]["E"]
                if l == 0:
                    pe.wait_ge(g_m, 1)
                    mm(bank(0, 0, 256), w("before"), M["m12"], start=True, stop=True)
                    mm(bank(0, 0, 256), w("ones"), M["pre"], start=False, stop=True, skip_group_check=True)
                    mm(bank(0, P, 256), w("ones"), M["tot"].unsqueeze(1).broadcast_to([P, NT, E_]),
                       start=False, stop=True, skip_group_check=True).then_inc(g_loc, 1)
                if l != 2:
                    n = [1, 2, 0, 3][l]
                    pe.wait_ge(gate_ok, n)
                    for t in range(NT):
                        last = turn(psum[0:E_, t * P:(t + 1) * P], gates[:, t, 0:E_], ident)
                    last.then_inc(gT_ps, 1)
                    pe.wait_ge(gT_ok, n)
                    for t in range(NT):
                        last = mm(psum[:, 2 * BANK + t * P:2 * BANK + (t + 1) * P], gatesT[0:E_, t * P:(t + 1) * P],
                                  w(f"m{l}_b2"), start=True, stop=True)
                    last.then_inc(b2_ps, 1)
                    pe.wait_ge(b2_ok, n)

            def experts(l):
                m = MOE[l]
                C = m["C"]

                def hidden(e, side, b):
                    if b == 0:
                        pe.wait_ge(w_in[side], load_count(l, e, side))
                    for c in range(4):
                        if l != 2:
                            pe.wait_ge(h_ok, e * 8 + (HB[l] + 4 * b + c + 1))
                        elif c < 2:
                            pe.wait_ge(sg_ok, e * 4 + (2 * b + c + 1))
                        else:
                            pe.wait_ge(h2_ok, e * 4 + (2 * b + c - 2 + 3))
                        mm(bank(c, 0, BANK), wexp[:, side, c * P:(c + 1) * P], xT_all[:, b * S:(b + 1) * S],
                           start=True, stop=True).then_inc(h_ps, 1)

                def output(e, side, b):
                    if l == 2:
                        pe.wait_ge(h2_ok, e * 4 + (4 + 2 * b + 2))
                    else:
                        pe.wait_ge(h_ok, e * 8 + (4 + HB[l] + 4 * b + 4))
                    pe.wait_ge(acc_ok, e * 2 + (KB[l] + b + 1))
                    if l == 3:
                        pe.wait_ge(w2n_ok, e + 1)
                    for t in range(TB):
                        for c in range(C):
                            down = w2n[:, side, c * P:(c + 1) * P] if l == 3 else wexp[:, side, BANK + c * P:BANK + (c + 1) * P]
                            last = mm(bank(4 + b, t * P, (t + 1) * P), hT[:, b, c * BANK + t * P:c * BANK + (t + 1) * P], down,
                                      start=(c == 0), stop=(c == C - 1))
                    last.then_inc(ye_ps, 1)

                pe.wait_ge(m_copy, NT * (l + 1))
                pe.wait_ge(lg_ok, NT * (l + 1))
                expert_order(pe, l, hidden, output)

            def experts0():
                def turned(e, side, i):
                    pe.wait_ge(d_in[side], i * 16 + 16)
                    pe.wait_ge(d_xe, e + 1)
                    turn(bank(side % 2, 0, P), D["xin"][:, side * P:(side + 1) * P], ident).then_inc(d_T, 1)

                def hidden(e, side, i):
                    pe.wait_ge(w0_in[side], i * 16 + 16)
                    pe.wait_ge(d_xe, e + 3)
                    pe.wait_ge(d_h, e + 1)
                    for c in range(4):
                        last = mm(bank(2 + side % 2, c * P, (c + 1) * P), W0[side][:, c * P:(c + 1) * P],
                                  D["xe"][:, side % 2 * P:(side % 2 + 1) * P], start=True, stop=True)
                    last.then_inc(d_H, 1)

                def output(e, side, i):
                    pe.wait_ge(d_h, e + 3)
                    pe.wait_ge(d_y, e + 1)
                    for c in range(4):
                        last = mm(bank(4 + side % 2, 0, P), D["h"][:, side % 2 * BANK + c * P:side % 2 * BANK + (c + 1) * P],
                                  W0[side][:, BANK + c * P:BANK + (c + 1) * P], start=(c == 0), stop=(c == 3))
                    last.then_inc(d_O, 1)

                run_queues(pe, (turned, 2), (hidden, 1), (output, 0))

            for l in range(4):
                if STAGES > 2 * l:
                    xattn(l)
                if STAGES > 2 * l + 1:
                    if l == 1:
                        two_token()
                    elif l == 3:
                        norms3()
                        moe_input(l)
                        norm_rows3()
                    else:
                        selfattn(l // 2)
                        moe_input(l)
                    gating(l)
                    experts(l) if l else experts0()


def kernel(**inputs):
    import concourse.bacc as bacc
    from concourse.bass_utils import run_bass_kernel_spmd

    inp = {k: np.asarray(v) for k, v in inputs.items()}
    blocks = layout(inp)
    at, first = {}, 0
    for name, block in blocks.items():
        at[name] = (first, block.shape[0], block.shape[1])
        first += block.shape[1]
    packed = np.zeros((P, first), np.float32)
    for name, block in blocks.items():
        a, rows, cols = at[name]
        packed[0:rows, a:a + cols] = block
    mask = np.ascontiguousarray(np.broadcast_to(np.tile(inp["mask_BxS2_ik0"], (1, 4)), (P, B, 4 * KV)))
    arrays = {"x": np.ascontiguousarray(inp["x"].reshape(B * S, P)), "mask": mask, "packed": packed}
    for l, e in enumerate(expert_layout(inp)):
        arrays[f"experts{l}"] = np.ascontiguousarray(e)

    nc = bacc.Bacc("TRN2", target_bir_lowering=False, num_devices=1)
    ap = {n: nc.dram_tensor(n, a.shape, mybir.dt.from_np(a.dtype), kind="ExternalInput").ap() for n, a in arrays.items()}
    out = nc.dram_tensor("out", (B * S, P), F32, kind="ExternalOutput").ap()
    queued, answers = (nc.dram_tensor(n, (SLOTS, P), F32, kind="Internal").ap() for n in ("queued", "answers"))
    program(nc, ap["x"], ap["mask"], ap["packed"], [ap[f"experts{l}"] for l in range(4)], out, queued, answers, at)
    r = run_bass_kernel_spmd(nc, [arrays], core_ids=[0])
    return r.results[0]["out"].reshape(B, S, P)
```

```python
from contextlib import ExitStack

import numpy as np

import concourse.bass as bass
from concourse import mybir

ALU = mybir.AluOpType
ACT = mybir.ActivationFunctionType
F32 = mybir.dt.float32
BF16 = mybir.dt.bfloat16
I32 = mybir.dt.int32
AX_X = mybir.AxisListType.X

P = 128
B = 2
S = 512
TB = S // P
NT = B * TB
KV = 77
BANK = 512
EPS_LN = 1e-5
ARENA = 23680
FMIN = float(np.finfo(np.float32).min)

XATTN = [
    dict(G=1, H=16, dh=8, mask=True, qk_norm=False, bias=False),
    dict(G=4, H=8, dh=64, mask=False, qk_norm=False, bias=True),
    dict(G=8, H=16, dh=64, mask=False, qk_norm=True, bias=True),
    dict(G=8, H=16, dh=64, mask=False, qk_norm=False, bias=True),
]
MOE = [
    dict(E=16, C=4, act=ACT.Gelu, W=1028),
    dict(E=8, C=4, act=ACT.Relu, W=1028),
    dict(E=8, C=2, act=ACT.Silu, W=768),
    dict(E=8, C=4, act=ACT.Silu, W=1028),
]
CAPACITY = 2 * -(-B * S // 16)
E0 = 16
SLOTS = E0 * CAPACITY
DROPPED = 2 * SLOTS
assert CAPACITY == P
HS, DS = 16, 8


def constants():
    p = np.arange(P)
    f = np.float32
    return {
        "ident": np.eye(P, dtype=f),
        "headmask": (p[:, None] // DS == np.arange(HS)).astype(f),
        "halfmask": (p[:, None] // 64 == np.arange(2)).astype(f),
        "later": np.triu(np.ones((P, P), f), 1) * f(-1e30),
        "before": np.triu(np.ones((P, P), f)),
        "firstness": np.broadcast_to(16.0 - np.arange(16, dtype=f), (P, 16)),
        "neghalf": np.full((P, 16), -0.5, f),
        "ones": np.ones((P, P), f),
        "queue": np.broadcast_to(np.arange(E0, dtype=f) * CAPACITY - 1, (P, E0)),
    }


def layout(inp):
    col = lambda v: v.reshape(-1, 1)
    row = lambda v: np.broadcast_to(v.reshape(1, -1), (P, v.size))
    blocks = dict(constants())
    blocks["ctxT"] = inp["ctx_1024"].transpose(2, 0, 1).reshape(P, B * KV)
    for l in range(4):
        n = f"L{l}_xattn_"
        out = inp[n + ("Wu" if l == 2 else "Wo")]
        if l >= 2:
            wq, wk, wv, out = inp[n + "Wq"].T, inp[n + "Wk"].T, inp[n + "Wv"].T, out.T
        else:
            wq, wk, wv = inp[n + "Wq"], inp[n + "Wk"], inp[n + "Wv"]
        G = XATTN[l]["G"]
        blocks[f"x{l}_wk"], blocks[f"x{l}_wv"], blocks[f"x{l}_wq"] = wk, wv, wq
        blocks[f"x{l}_wo"] = out.reshape(G, P, P).transpose(1, 0, 2).reshape(P, G * P)
        if l:
            blocks[f"x{l}_bo"] = row(inp[n + ("bu" if l == 2 else "bo")])
        if l == 2:
            for k in ("qn_w", "qn_b", "kn_w", "kn_b"):
                blocks[k] = col(np.concatenate([inp[n + k]] * 2))
        m = f"L{l}_ffn_"
        if l == 0:
            for k in ("q_w", "k_w", "v_w", "o_w"):
                blocks["s0_" + k] = inp[m + k]
            for k in ("q_b", "k_b", "ln1_w", "ln1_b", "ln2_w", "ln2_b"):
                blocks["s0_" + k] = col(inp[m + k])
            blocks["s0_v_b"], blocks["s0_o_b"] = row(inp[m + "v_b"]), row(inp[m + "o_b"])
            blocks["m0_router"] = inp[m + "router_w"]
            blocks["m0_b2"] = inp[m + "fc2_b"]
        if l == 1:
            blocks["h_wqkv"] = inp[m + "Wqkv"].T
            blocks["h_wo"] = inp[m + "Wo"].T
            for k in ("bqkv", "bo", "g1", "be1", "g2", "be2"):
                blocks["h_" + k] = row(inp[m + k])
            blocks["m1_router"] = inp[m + "Wg"].T
            blocks["m1_b2"] = inp[m + "b2"]
        if l == 2:
            for k in ("wq", "wk", "wv", "wo"):
                blocks["s2_" + k[1] + "_w"] = inp[m + k]
            blocks["s2_norm1"], blocks["s2_norm2"] = col(inp[m + "norm1_w"]), col(inp[m + "norm2_w"])
            blocks["m2_router"] = inp[m + "router_w"]
        if l == 3:
            blocks["m3_gate_v"] = inp[m + "gate_v"]
            blocks["m3_gate_g"] = col(inp[m + "gate_g"])
            blocks["m3_gate_b"] = row(inp[m + "gate_b"])
            blocks["m3_g1"] = inp[m + "w1_g"].reshape(8, 4, P).transpose(2, 0, 1).reshape(P, 32)
            blocks["m3_g2"] = inp[m + "w2_g"].T
            blocks["m3_b2"] = inp[m + "b2"]
    return blocks


def expert_layout(inp):
    up = lambda w: w
    down = lambda w: w.reshape(w.shape[0], -1, P, P).transpose(0, 2, 1, 3).reshape(w.shape[0], P, -1)
    bias = lambda v: v.reshape(v.shape[0], 4, P).transpose(0, 2, 1)
    out = []
    out.append(np.concatenate([up(inp["L0_ffn_fc1_w"]), down(inp["L0_ffn_fc2_w"]), bias(inp["L0_ffn_fc1_b"])], 2))
    out.append(np.concatenate([up(inp["L1_ffn_W1"]), down(inp["L1_ffn_W2"]), bias(inp["L1_ffn_b1"])], 2))
    m = "L2_ffn_"
    routed = np.concatenate([inp[m + "e_gate"], inp[m + "e_up"], down(inp[m + "e_down"])], 2)
    shared = np.concatenate([inp[m + "sh_gate"][None], inp[m + "sh_up"][None], down(inp[m + "sh_down"][None])], 2)
    out.append(np.concatenate([routed, shared]))
    m = "L3_ffn_"
    out.append(np.concatenate([inp[m + "w1_v"].transpose(0, 2, 1), down(inp[m + "w2_v"].transpose(0, 2, 1)), bias(inp[m + "b1"])], 2))
    return out



def cuts(at):
    return [at[n][0] + at[n][2] for n in ("x0_wo", "m0_b2", "m1_b2", "m2_router", "m3_b2")]


def program(nc, x, mask, packed, experts, out, queued, answers, at):
    ctx = ExitStack()
    with ctx:
        def sb(name, shape, dt=F32):
            return ctx.enter_context(nc.sbuf_tensor(name, shape, dt))

        def sem(name):
            return ctx.enter_context(nc.semaphore(name))

        def sems(names):
            return [sem(n) for n in names.split()]

        ends = cuts(at)
        held = sb("held", [P, ends[-1]])

        def w(name, lo=0, hi=None):
            a, r, c = at[name]
            return held[0:r, a + lo:a + (c if hi is None else hi)]

        x_res = sb("x_res", [P, NT * P])
        r_res = sb("r_res", [P, NT * P])
        xT_all = sb("xT_all", [P, NT * P])
        kbd = sb("kbd", [P, B * 16 * KV])
        vx = sb("vx", [KV, B * 16 * 65])
        wexp = sb("wexp", [P, 2, 1028])
        mask_i = sb("mask_i", [P, B, 4 * KV], I32)
        stats = sb("stats", [P, NT, 6])
        mv = sb("mv", [P, NT, 2])
        var = sb("var", [P, 4, 16])
        rstd = sb("rstd", [P, 4, 16])
        small = sb("small", [P, 4, 64])
        chain = sb("chain", [P, 2 * P])
        arena = sb("arena", [P, ARENA])
        pool_pad = sb("pool_pad", [P, 8])
        n_sum = sb("n_sum", [P, 40])
        slot_i = sb("slot_i", [P, 32], I32)
        s1_now = sb("s1_now", [P, 2, 4])
        ident_bf = sb("ident_bf", [P, P], BF16)
        later_bf = sb("later_bf", [P, P], BF16)
        spread_q = sb("spread_q", [P, HS, 160], BF16)
        spread_k = sb("spread_k", [P, HS, 112], BF16)
        act_pad = sb("act_pad", [P, 4])
        psum = ctx.enter_context(nc.psum_tensor("psum", [P, 8 * BANK], F32))

        def bank(n, lo, hi, rows=P):
            return psum[0:rows, n * BANK + lo:n * BANK + hi]

        def take(sizes):
            views, a = {}, 0
            for name, n in sizes.items():
                views[name] = arena[:, a:a + n]
                a += n
            assert a <= ARENA, a
            return views

        def two(v):
            return v.rearrange("p (j n) -> p j n", j=2)

        inv_wide, inv_turned = chain[:, 0:P], chain[:, P:2 * P]
        A = take(dict(qT=8192, qcur=2048, E=2 * 1232, PT=4096, O=2048, OT=2048, sq=2048))
        qcur2, E, PT, O, OT = (two(A[k]) for k in ("qcur", "E", "PT", "O", "OT"))
        qT_all, xn_all = A["qT"], A["PT"][:, 0:NT * P]
        mask_add = A["qT"][:, 7000:7000 + 8 * KV]
        ext = two(mask_add)
        kn, kaff = two(A["E"][:, 0:2048]), A["qcur"][:, 0:8 * 154]
        four = lambda v: v.rearrange("p (c n) -> p c n", c=4)
        qn4, qsq4 = four(A["PT"]), four(arena[:, 8192 + 2048 + 2464 + 4096:8192 + 2048 + 2464 + 2 * 4096])
        U = take(dict(rep=2 * HS * S, P=4 * BANK, PT=4 * BANK, qa=NT * P, ka=NT * P, va=NT * P))
        pself, ptself, q_all, k_all, v_all = (U[n] for n in ("P", "PT", "qa", "ka", "va"))
        v_wide = arena[:, 2 * HS * S + 8 * BANK:2 * HS * S + 8 * BANK + 2 * NT * P]
        ROWS = 96
        q_rep, k_rep = (U["rep"].bitcast(BF16)[0:ROWS, n * HS * B * S:(n + 1) * HS * B * S] for n in range(2))
        q_parts, k_parts = (U[n].bitcast(BF16).rearrange("p (n t) -> p n t", t=B * S) for n in ("P", "PT"))
        xn_self, xT_self = U["P"][:, 0:NT * P], U["PT"][:, 0:NT * P]
        ctxT_all = xT_all[:, :]
        H = take(dict(qkv=NT * 384, prod=4 * S, sc=128, cc=NT * P))
        M = take(dict(h=2 * 2048, s=2048, w2n=1024, s2=8 * P, diag=8 * P, gv=P, gwT=8, ga=P, gb=P, gc=P,
                      m12=256, pre=256, tot=16, mk=256, gT=NT * P,
                      lg=NT * 16, gates=NT * 16))
        logits, xn_moe = M["lg"], M["h"][:, 0:NT * P]
        gates = M["gates"].rearrange("p (t e) -> p t e", t=NT)
        gatesT = M["gT"][0:16, :]
        sq = two(A["sq"])
        s1_all, s2_col = n_sum[:, 0:32], n_sum[:, 32:40]
        hT, sg, w2n = two(M["h"]), two(M["s"]), two(M["w2n"])

        D = take(dict(past_M=12032, w=2 * 1028, xin=4 * P, xe=2 * P, h=2 * 512, y=4 * P, back=16 * P, loc=256, slot=64))
        W0 = [wexp[:, 0, :], wexp[:, 1, :], D["w"][:, 0:1028], D["w"][:, 1028:2056]]

        in_x, in_mask, stored, const_ok = sems("in_x in_mask stored const_ok")
        in_held = [sem(f"in_held{n}") for n in range(5)]
        dve_step, act_step, pool_step = sems("dve_step act_step pool_step")
        x_stat, x_rstd, x_xn, x_xTp, x_xT = sems("x_stat x_rstd x_xn x_xTp x_xT")
        kv_ps, kn_ok, kT_ps, k_ok, v_ok = sems("kv_ps kn_ok kT_ps k_ok v_ok")
        ksq_ok, kvar_ok, krstd_ok = sems("ksq_ok kvar_ok krstd_ok")
        q_act, q_dve, xq_ok, q_nat, centred = sems("q_act q_dve xq_ok q_nat centred")
        q_ps, qsq_ok, qvar_ok, qrstd_ok, qn_ok, qnT_ps, qT_ok = sems(
            "q_ps qsq_ok qvar_ok qrstd_ok qn_ok qnT_ps qT_ok")
        sc_ps, e_ok, p_ok, pT_ps, pT_act, pT_dve = sems("sc_ps e_ok p_ok pT_ps pT_act pT_dve")
        o_ps, o_ok, oT_ps, oT_ok, y_ps, x_done = sems("o_ps o_ok oT_ps oT_ok y_ps x_done")
        a_stat, a_rstd, h0_ok, b_stat, b_rstd, b_xn, s_xTp, s_xT, qkv_ps = sems(
            "a_stat a_rstd h0_ok b_stat b_rstd b_xn s_xTp s_xT qkv_ps")
        split_ok, rk_ps, rq_ps, rk_ok, rq_ok, v_wide_ok = sems("split_ok rk_ps rq_ps rk_ok rq_ok v_wide_ok")
        us_ps, um_ok, up_ok, upT_ps, upT_act, upT_dve, uo_ps = sems("us_ps um_ok up_ok upT_ps upT_act upT_dve uo_ps")
        inv_ok, r_ps, invT_ok, ctx_ok, vx_zero, spread_zero = sems("inv_ok r_ps invT_ok ctx_ok vx_zero spread_zero")
        t_ccT, t_ccS, t_y = sems("t_ccT t_ccS t_y")
        m_stat, m_rstd, m_xn, m_xTp, m_xT, lg_ps, lg_ok = sems("m_stat m_rstd m_xn m_xTp m_xT lg_ps lg_ok")
        g_sub, g_exp, g_m, g_loc, gate_ok, gT_ps, gT_ok, b2_ps, b2_ok = sems(
            "g_sub g_exp g_m g_loc gate_ok gT_ps gT_ok b2_ps b2_ok")
        w_in = [sem(f"w_in{n}") for n in range(2)]
        h_ps, h_ok, sg_ok, h2_ok, ye_ps, acc_ok, w2n_ok = sems("h_ps h_ok sg_ok h2_ok ye_ps acc_ok w2n_ok")
        n_sq, n_ps, n_max, n_inv, n_pow, n_ok, n_gv, n_gvT, n_diag, n_row, n_s2 = sems(
            "n_sq n_ps n_max n_inv n_pow n_ok n_gv n_gvT n_diag n_row n_s2")
        w0_in = [sem(f"w0_in{n}") for n in range(4)]
        d_in = [sem(f"d_in{n}") for n in range(4)]
        d_stored = [sem(f"d_stored{n}") for n in range(4)]
        d_back = [sem(f"d_back{n}") for n in range(4)]
        zeros_set, zeros_out, slots_ok, scattered = sems("zeros_set zeros_out slots_ok scattered")
        d_T, d_xe, d_H, d_h, d_O, d_y, d_done = sems("d_T d_xe d_H d_h d_O d_y d_done")
        f_stat, f_rstd, f_done = sems("f_stat f_rstd f_done")
        t1_e, t1_p, t1_av = sems("t1_e t1_p t1_av")

        block = ctx.enter_context(nc.Block())

        def tile(i, j):
            return bass.ds(i * P + j * S, P)

        class Steps:
            def __init__(self, eng, semaphore):
                self.eng, self.sem, self.base, self.n, self.i, self.per = eng, semaphore, 0, 0, None, 0

            def loop(self, i, per):
                self.base, self.n, self.i, self.per = self.base + self.n, 0, i, per

            def end(self, trips):
                assert self.n == self.per, (self.n, self.per)
                self.base, self.n, self.i = self.base + trips * self.per, 0, None

            def then(self, instruction):
                self.n += 1
                instruction.then_inc(self.sem, 1)
                at = self.base + self.n
                self.eng.wait_ge(self.sem, at if self.i is None else self.i * self.per + at)

        def count(base, i, j):
            return i * 2 + (base + j + 1)

        UNITS = NT * HS
        INVERT, TURN, FINISH = 3, 5, 6
        LEAD = 4
        KB = [2 * n for n in np.cumsum([0, 0, 8, 9, 8]).tolist()]
        HB = [0, 0, 64, 64, 128]
        HPB = [4 * n for n in KB]
        WB = [[0, 0], [0, 0], [4, 4], [9, 8]]

        YBANK = [2, 2, 1, 1]
        PARTS = [2, 2, 2, 2]
        XB = [8, 24, 40, 56]
        QKV = [0, 2, 10]
        GB, BB = [0, 6, 6, 6], [2, 6, 6, 6]
        XT = [2, 4, 2, 2]
        QB = [2 * n for n in (0, 1, 5, 5, 13)]
        PB = [0, 16, 24, 40]

        def chains(l):
            return [(j * PARTS[l] + part, j, part) for j in range(B) for part in range(PARTS[l])]

        def unit(l, i, c):
            return i * (B * PARTS[l]) + (XB[l] - 8 + c + 1)

        def out_chains(l):
            if XATTN[l]["G"] == 1:
                return [(lambda i, j=j: i * B + (j + 1), j, PARTS[l] - 1) for j in range(B)]
            return [(lambda i, c=c: i * (B * PARTS[l]) + (XB[l] - 16 + c + 1), j, part) for c, j, part in chains(l)]

        def turned_by(l, i, j, part):
            if l == 1:
                n = i * 2 + (PB[1] + j + 1)
                return (n, None) if part == 0 else (None, n)
            n = i * (B * PARTS[l]) + (PB[l] + j * PARTS[l] + part + 1)
            return n, n

        def block_done(eng, n):
            if n == 0:
                eng.wait_ge(in_x, 16)
            elif n % 2:
                eng.wait_ge(x_done, 2 + NT * (n // 2 + 1))
            elif n == 2:
                eng.wait_ge(d_done, 1)
            elif n == 4:
                eng.wait_ge(f_done, 1)
            else:
                eng.wait_ge(acc_ok, 2 + KB[n // 2])

        def held_in(eng, n):
            eng.wait_ge(in_held[n], 16)

        BU = TB * HS

        def keys_seen(u, qt):
            return (qt + 1) * P if u == 0 else S

        def load_count(l, e, side):
            before = 16 * (WB[l][side] + (4 if l == 3 else 0) + 1) - 8 * side
            return e * 8 + before

        def run_queues(eng, *lagged):
            def steps(e, k, i):
                for do, ahead in lagged:
                    if isinstance(e, int) and not 0 <= e + ahead < E0:
                        continue
                    do(e + ahead, (k + ahead) % 4, i + (k + ahead) // 4)

            for e in range(-max(ahead for _, ahead in lagged), 0):
                steps(e, e, 0)
            with eng.Fori(0, E0 // 4 - 1) as i:
                for k in range(4):
                    steps(i * 4 + k, k, i)
            for k in range(4):
                steps(E0 - 4 + k, k, E0 // 4 - 1)

        def expert_order(eng, l, first, second, between):
            n = MOE[l]["E"] + (l == 2)

            def pair(e0, more):
                for side in range(2):
                    e = e0 + side
                    first(e, side, 1)
                    second(e, side, 0)
                    if side == 0 or more:
                        first(e + 1, 1 - side, 0)
                    second(e, side, 1)

            first(0, 0, 0)
            first(0, 0, 1)
            between(False)
            second(0, 0, 0)
            first(1, 1, 0)
            between(True)
            second(0, 0, 1)
            first(1, 1, 1)
            second(1, 1, 0)
            first(2, 0, 0)
            second(1, 1, 1)
            trips = n // 2 if n % 2 else n // 2 - 1
            with eng.Fori(0, trips - 1) as i:
                pair(i * 2 + 2, True)
            if n % 2:
                first(n - 1, 0, 1)
                second(n - 1, 0, 0)
                second(n - 1, 0, 1)
            else:
                pair(n - 2, False)

        @block.sync
        def _(sp):
            sp.dma_start(x_res[:, :].rearrange("p (t d) -> p t d", d=P),
                         x.rearrange("(t p) d -> p t d", p=P)).then_inc(in_x, 16)
            first = 0
            for n, end in enumerate(ends):
                sp.dma_start(held[:, first:end], packed[:, first:end]).then_inc(in_held[n], 16)
                first = end
                if n == 0:
                    sp.dma_start(mask_i[:, :, :], mask).then_inc(in_mask, 16)

            sp.wait_ge(zeros_set, 1)
            for n in range(SLOTS // 1024):
                sp.dma_start(queued[n * 1024:(n + 1) * 1024, :].rearrange("(p t) d -> p (t d)", p=P),
                             r_res[:, :]).then_inc(zeros_out, 16)

            def load(l, e, side):
                W = MOE[l]["W"]
                src = experts[l].rearrange("e p n -> p e n")[:, bass.ds(e, 1), :]
                sp.dma_start(wexp[:, side:side + 1, 0:W], src).then_inc(w_in[side], 16)

            def load0(e, side):
                src = experts[0].rearrange("e p n -> p e n")[:, bass.ds(e, 1), :]
                sp.dma_start(W0[side].unsqueeze(1), src).then_inc(w0_in[side], 16)

            def load_queue(e, side):
                src = queued.rearrange("(e p) d -> p e d", p=P)[:, bass.ds(e, 1), :]
                sp.dma_start(D["xin"][:, side * P:(side + 1) * P].unsqueeze(1), src).then_inc(d_in[side], 16)

            def store_answer(e, side):
                sp.wait_ge(d_y, e + 3)
                dst = answers.rearrange("(e p) d -> p e d", p=P)[:, bass.ds(e, 1), :]
                sp.dma_start(dst, D["y"][:, side * P:(side + 1) * P].unsqueeze(1)).then_inc(d_stored[side], 16)

            def load_ahead(e, side):
                sp.wait_ge(d_O, e + 1)
                load0(e + 4, side)
                load_queue(e + 4, side)

            for side in range(4):
                if side == 2:
                    sp.wait_ge(ctx_ok, 2 + NT)
                load0(side, side)
            sp.wait_ge(scattered, 16 * 16)
            for side in range(4):
                load_queue(side, side)
            with sp.Fori(0, E0 // 4 - 1) as i:
                for k in range(4):
                    load_ahead(i * 4 + k, k)
                    store_answer(i * 4 + k, k)
            for k in range(4):
                store_answer(E0 - 4 + k, k)

            for l in range(1, 4):
                n = MOE[l]["E"] + (l == 2)
                if l == 3:
                    for side in range(2):
                        sp.wait_ge(ye_ps, 2 + KB[l])
                        load(l, side, side)
                    with sp.Fori(0, 3) as i:
                        for side in range(2):
                            sp.wait_ge(n_sq, i * 2 + (side + 1))
                            load(l, i * 2 + (side + 2), side)
                    sp.wait_ge(n_sq, 8)
                else:
                    sp.wait_ge(ye_ps, 2 + KB[l])
                for side in range(2):
                    load(l, side, side)
                with sp.Fori(0, (n - 2) // 2) as i:
                    for side in range(2):
                        sp.wait_ge(ye_ps, i * 4 + (2 + KB[l] + 2 * side + 2))
                        load(l, i * 2 + (side + 2), side)
                if n % 2:
                    sp.wait_ge(ye_ps, 2 + KB[l] + 2 * (n - 2))
                    load(l, n - 1, 0)
            block_done(sp, 8)
            sp.dma_start(out.rearrange("(t p) d -> p t d", p=P),
                         x_res[:, :].rearrange("p (t d) -> p t d", d=P)).then_inc(stored, 16)
            sp.wait_ge(stored, 16)

        @block.gpsimd
        def _(pool):
            step = Steps(pool, pool_step)
            half = w("neghalf")

            def carry(n):
                return pool.tensor_tensor(pool_pad[:, n:n + 1], half[:, 0:1], half[:, 0:1], ALU.mult)

            def rsqrt(dst, src, ready, at, done):
                pool.wait_ge(ready, at)
                n = src.shape[-1]
                pool.tensor_tensor(dst, src, half[0:src.shape[0], 0:n], ALU.pow).then_inc(done, 1)

            held_in(pool, 0)

            def all_tokens(ready, at, done):
                rsqrt(rstd[:, 0, 0:NT], var[:, 0, 0:NT], ready, at, done)

            def inverse_norms(f, d):
                for v in (s1_all[:, f], s2_col[:, d]):
                    pool.tensor_tensor(v, v, half[:, 0:v.shape[-1]], ALU.pow).then_inc(n_inv, 1)

            def xattn(l):
                all_tokens(x_stat, l + 1, x_rstd)
                if l == 2:
                    for n in range(NT):
                        rsqrt(rstd[:, n % 4, :], var[:, n % 4, :], qvar_ok, n + 1, qrstd_ok)
                G = XATTN[l]["G"]
                Q = qT_all[:, 0:B * G * S].rearrange("p (b g t) -> p b g t", b=B, g=G)
                at = qcur2[:, :, 0:G * P].rearrange("p j (g t) -> p j g t", t=P)
                for j in range(B):
                    if l == 2:
                        pool.wait_ge(qT_ok, TB * (j + 1))
                    else:
                        pool.wait_ge(q_act, (QB[l] + (j + 1) * G + 1) // 2)
                        if QB[l] + (j + 1) * G > 1:
                            pool.wait_ge(q_dve, (QB[l] + (j + 1) * G) // 2)
                    pool.tensor_copy(at[:, j], Q[:, j, :, 0:P]).then_inc(xq_ok, 1)
                if l == 3:
                    carry(4).then_inc(n_inv, 1)
                with pool.Fori(0, TB - 1) as i:
                    for j in range(B):
                        pool.wait_ge(sc_ps, i * (B * PARTS[l]) + (XB[l] + (j + 1) * PARTS[l]))
                        carry(j)
                        pool.tensor_copy(at[:, j], Q[:, j, :, bass.ds(i * P + P, P)]).then_inc(xq_ok, 1)
                    if l == 3:
                        pool.wait_ge(n_inv, i * 2 + 1)
                        pool.wait_ge(n_max, i * 2 + (2 + 2))
                        carry(4)
                        inverse_norms(bass.ds(i * 8, 8), bass.ds(i * 2, 2))
                if l == 3:
                    pool.wait_ge(n_max, 2 + 8)
                    inverse_norms(slice(24, 32), slice(6, 8))

            def selfattn(u):
                all_tokens(a_stat, 2 * u + 1, a_rstd)
                all_tokens(b_stat, u + 1, b_rstd)

            def queues():
                pool.wait_ge(slots_ok, 1)
                pool.wait_ge(zeros_out, 16 * (SLOTS // 1024))
                pool.wait_ge(m_xn, B)
                for k in range(2):
                    for t in range(NT):
                        pool.indirect_dma_start(
                            queued, bass.IndirectOffsetOnAxis(ap=slot_i[:, k * NT + t:k * NT + t + 1], axis=0),
                            xn_moe[:, t * P:(t + 1) * P], None, bounds_check=SLOTS - 1, oob_is_err=False)\
                            .then_inc(scattered, 16)
                for side in range(4):
                    pool.wait_ge(d_stored[side], 16 * (1 + E0 // 4))
                for n in range(2 * NT):
                    pool.indirect_dma_start(
                        D["back"][:, n * P:(n + 1) * P], None, answers,
                        bass.IndirectOffsetOnAxis(ap=slot_i[:, 2 * NT + n:2 * NT + n + 1], axis=0))\
                        .then_inc(d_back[n // 4], 16)

            def router_norm3():
                held_in(pool, 4)
                pool.wait_ge(n_max, 2 + 8 + 1)
                gv = small[0:8, 0, 33:34]
                step.then(pool.tensor_tensor(gv, gv, half[0:8, 0:1], ALU.pow))
                pool.tensor_tensor(gv, gv, w("m3_gate_g"), ALU.mult).then_inc(n_pow, 1)

            def row_norms3():
                pool.wait_ge(n_inv, 1 + 2 * TB)
                pool.tensor_tensor(s1_all, s1_all, w("m3_g1"), ALU.mult)
                pool.tensor_tensor(s2_col, s2_col, w("m3_g2"), ALU.mult).then_inc(n_ok, 1)
                pool.wait_ge(n_ok, 1)

            def experts3():
                pool.wait_ge(n_s2, 2)
                with pool.Fori(0, 4) as i:
                    for side in range(2):
                        pool.wait_ge(w_in[side], i * 16 + 16 * (WB[3][side] + 4 + 1))
                        carry(5 + side)
                        pool.tensor_copy(s1_now[:, side, :], s1_all[:, bass.ds(i * 8 + side * 4, 4)])
                        pool.tensor_tensor(w2n[:, side, :].rearrange("p (c d) -> p c d", d=P),
                                           wexp[:, side, 512:1024].rearrange("p (c d) -> p c d", d=P),
                                           M["s2"][:, bass.ds(i * 256 + side * P, P)].unsqueeze(1).broadcast_to([P, 4, P]),
                                           ALU.mult).then_inc(w2n_ok, 1)

            for l in range(4):
                xattn(l)
                if l == 1:
                    all_tokens(a_stat, l + 1, a_rstd)
                elif l != 3:
                    selfattn(l // 2)
                all_tokens(m_stat, l + 1, m_rstd)
                if l == 0:
                    queues()
                elif l == 1:
                    all_tokens(f_stat, 1, f_rstd)
                    for b in range(B):
                        rsqrt(rstd[0:KV, 1 + b, :], var[0:KV, 1 + b, :], kvar_ok, b + 1, krstd_ok)
                elif l == 3:
                    router_norm3()
                    row_norms3()
                    experts3()

        @block.scalar
        def _(act):
            step = Steps(act, act_step)
            act.sem_inc(up_ok, LEAD)
            act.sem_inc(upT_act, LEAD)
            act.sem_inc(h_ok, 4)
            act.sem_inc(d_h, 2)
            act.sem_inc(rq_ok, 4)
            act.sem_inc(sg_ok, 2)

            def copy_tile(ready, at, dst, src, done, func=ACT.Copy, **kw):
                act.wait_ge(ready, at)
                act.activation(dst, src, func, **kw).then_inc(done, 1)

            def xattn(l):
                L = XATTN[l]
                G, NH, dh = L["G"], L["H"], L["dh"]
                nb = NH // 4
                held_in(act, [0, 2, 3, 4][l])
                if l == 2:
                    act.wait_ge(kv_ps, l + 1)
                    for b in range(B):
                        act.activation(O[0:KV, b, :], psum[0:KV, 2 * b * BANK:(2 * b + 2) * BANK], ACT.Square)\
                           .then_inc(ksq_ok, 1)
                act.wait_ge(kv_ps, l + 1)
                if l == 0:
                    act.wait_ge(vx_zero, 1)
                    V = vx[:, 0:B * NH * 32].rearrange("p (b g r n) -> p b g r n", b=B, r=4, n=32)
                    for b in range(B):
                        src = psum[0:KV, (4 + 2 * b) * BANK:(4 + 2 * b) * BANK + P].rearrange("p (g r d) -> p g r d", r=4, d=dh)
                        for n in range(4):
                            last = act.activation(V[:, b, :, n, DS * n:DS * n + DS], src[:, :, n, :], ACT.Copy)
                    last.then_inc(v_ok, 1)
                    act.activation(ident_bf[:, :], w("ident"), ACT.Copy)
                    act.activation(later_bf[:, :], w("later"), ACT.Copy)
                    act.wait_ge(spread_zero, 1)
                    by_8 = w("ident").rearrange("p (h d) -> p h d", d=DS)
                    for n in range(4):
                        act.activation(spread_q[:, :, 64 + 8 * n:72 + 8 * n], by_8, ACT.Copy)
                    for n in range(3):
                        last = act.activation(spread_k[:, :, 16 + 32 * n:24 + 32 * n], by_8, ACT.Copy)
                    last.then_inc(const_ok, 1)
                V = vx[:, 0:B * NH * (dh + 1)].rearrange("p (b h d) -> p b h d", b=B, d=dh + 1)
                for b in range(B) if l else ():
                    first = 4 + 2 * b
                    last = act.activation(V[:, b, :, 0:dh],
                                          psum[0:KV, first * BANK:first * BANK + NH * dh].rearrange("p (h d) -> p h d", d=dh),
                                          ACT.Copy)
                if l:
                    last.then_inc(v_ok, 1)
                for b in range(B):
                    copy_tile(x_xTp, 2 * l + b + 1, xT_all[:, b * S:(b + 1) * S], bank(4 + b, 0, BANK), x_xT)
                if l == 2:
                    def square(n):
                        act.wait_ge(q_nat, n + 1)
                        first = 2 * (n % 3)
                        act.activation(qsq4[:, n % 4, :], psum[:, first * BANK:(first + 2) * BANK], ACT.Square).then_inc(qsq_ok, 1)

                    square(0)
                    square(1)
                    for n in range(NT):
                        if n + 2 < NT:
                            square(n + 2)
                        b, c = n // TB, n % TB
                        copy_tile(qnT_ps, n + 1,
                                  qT_all[:, b * G * S:(b + 1) * G * S].rearrange("p (g t) -> p g t", g=G)[:, :, c * P:(c + 1) * P],
                                  psum[:, 6 * BANK:8 * BANK].rearrange("p (g t) -> p g t", g=G),
                                  qT_ok, ACT.Identity, scale=w("qn_w"), bias=w("qn_b"))
                else:
                    for n in range(0, B * G, 2):
                        copy_tile(q_ps, QB[l] + n + 1, qT_all[:, n * S:(n + 1) * S], bank((6 + n) % 8, 0, BANK), q_act)
                with act.Fori(0, TB) as i:
                    if l == 3:
                        for side in range(2):
                            act.wait_ge(w_in[side], i * 16 + 16 * (WB[3][side] + 1))
                            act.wait_ge(n_ps, i * 2 + (side + 1))
                            act.activation(sq[:, side, :], wexp[:, side, 0:1024], ACT.Square).then_inc(n_sq, 1)
                    for c, j, part in chains(l):
                        act.wait_ge(e_ok, unit(l, i, c))
                        n = NH // PARTS[l] * KV
                        e = E[:, j, part * n:(part + 1) * n]
                        act.activation(e, e, ACT.Exp, scale=1.0 if L["mask"] else dh ** -0.5).then_inc(p_ok, 1)
                    for c, j, part in chains(l):
                        if l != 1 or part == 0:
                            lo, n = part * nb // PARTS[l], max(1, nb // PARTS[l] // 2)
                            copy_tile(pT_ps, unit(l, i, c), PT[0:KV, j, lo * BANK:(lo + n) * BANK],
                                      psum[0:KV, (4 * j + lo) * BANK:(4 * j + lo + n) * BANK], pT_act)
                    for at, j, part in out_chains(l) if G > 1 else ():
                        n = G * P // PARTS[l]
                        first = 4 * j + part * nb // PARTS[l]
                        copy_tile(oT_ps, at(i), OT[:, j, part * n:(part + 1) * n],
                                  psum[:, first * BANK:first * BANK + n], oT_ok)

            def selfattn(u):
                held_in(act, [1, 3][u])
                for b in range(B):
                    act.wait_ge(s_xTp, 4 * u + b + 1)
                    dst = xT_self[:, b * S:(b + 1) * S]
                    if u == 0:
                        act.activation(dst, bank(b, 0, BANK), ACT.Identity,
                                       scale=w("s0_ln1_w"), bias=w("s0_ln1_b")).then_inc(s_xT, 1)
                    else:
                        act.activation(dst, bank(b, 0, BANK), ACT.Copy, scale=w("s2_norm1")).then_inc(s_xT, 1)
                for b in range(B):
                    with act.Fori(0, HS // 4) as i:
                        for k in range(4):
                            act.wait_ge(rq_ps, i * 4 + ((u * B + b) * HS + k + 1))
                            act.activation(act_pad[:, k:k + 1], w("neghalf", 0, 1), ACT.Copy)
                            act.activation(q_rep[:, bass.ds(i * (4 * B * S) + (k * B * S + b * S), S)],
                                           bank(2 * k + 1, 0, BANK, ROWS), ACT.Copy).then_inc(rq_ok, 1)
                with act.Fori(0, B) as b:
                    for n in range(BU + 2):
                        qt, h = divmod(n, HS)
                        first = b * BU + (u * UNITS + n)
                        g = n - 2
                        if g >= 0 and g % 2 == 0:
                            W = keys_seen(u, g // HS)
                            act.wait_ge(upT_ps, first + (LEAD - 1))
                            act.wait_ge(uo_ps, first + (LEAD - 5))
                            act.activation(ptself[:, (g % 4) * BANK:(g % 4) * BANK + W], bank(4 + g % 2, 0, W),
                                           ACT.Copy).then_inc(upT_act, 1)
                        if n < BU:
                            W = keys_seen(u, qt)
                            act.wait_ge(um_ok, first + 1)
                            act.wait_ge(upT_ps, first + (LEAD - 3))
                            act.activation(pself[:, (h % 4) * BANK:(h % 4) * BANK + W], bank(h % 4, 0, W), ACT.Exp,
                                           bias=small[:, 0, h:h + 1], accum_out=small[:, 1 + qt % 2, h:h + 1]).then_inc(up_ok, 1)

            def moe_input(l):
                held_in(act, [1, 2, 3, 4][l])
                for b in range(B):
                    act.wait_ge(m_xTp, 2 * l + b + 1)
                    dst, src = xT_all[:, b * S:(b + 1) * S], bank(XT[l] + b, 0, BANK)
                    if l == 0:
                        ins = act.activation(dst, src, ACT.Identity, scale=w("s0_ln2_w"), bias=w("s0_ln2_b"))
                    elif l == 2:
                        ins = act.activation(dst, src, ACT.Copy, scale=w("s2_norm2"))
                    else:
                        ins = act.activation(dst, src, ACT.Copy)
                    ins.then_inc(m_xT, 1)

            def two_token():
                held_in(act, 2)
                for b in range(B):
                    copy_tile(s_xTp, 2 + b + 1, xT_all[:, b * S:(b + 1) * S], bank(b, 0, BANK), s_xT)
                act.wait_ge(t1_e, 1)
                act.activation(H["sc"][:, 0:64], H["sc"][:, 0:64], ACT.Exp, scale=32 ** -0.5).then_inc(t1_p, 1)
                for b in range(B):
                    copy_tile(t_ccT, b + 1, xT_all[:, b * S:(b + 1) * S], bank(b, 0, BANK), t_ccS)
                moe_input(1)

            def gating(l):
                E_ = MOE[l]["E"]
                if l in (0, 2):
                    act.wait_ge(g_sub, [1, 0, 2][l])
                    act.activation(M["gc"][:, 0:NT * E_], M["gc"][:, 0:NT * E_], ACT.Exp).then_inc(g_exp, 1)
                if l == 2:
                    act.wait_ge(g_sub, 3)
                    act.activation(M["gc"][:, 0:NT * E_], M["gc"][:, 0:NT * E_], ACT.Exp).then_inc(g_exp, 1)
                if l != 2:
                    act.wait_ge(gT_ps, [1, 2, 0, 3][l])
                    act.activation(gatesT[0:E_, :], psum[0:E_, GB[l] * BANK:(GB[l] + 2) * BANK], ACT.Copy).then_inc(gT_ok, 1)

            def experts(l):
                m = MOE[l]
                n, func = m["E"], m["act"]

                def hidden(e, side, b):
                    if l == 2:
                        for c in range(2):
                            act.wait_ge(h_ps, e * 8 + (HPB[l] + 4 * b + c + 1))
                            act.wait_ge(h2_ok, e * 4 + (2 * b + c + 1))
                            act.activation(sg[:, b, c * BANK:(c + 1) * BANK], bank(c, 0, BANK), func).then_inc(sg_ok, 1)
                        return
                    for c in range(4):
                        act.wait_ge(h_ps, e * 8 + (HPB[l] + 4 * b + c + 1))
                        if c == 0:
                            act.wait_ge(ye_ps, e * 2 + (2 + KB[l] + b - 1))
                        kw = dict(bias=wexp[:, side, 1024 + c:1025 + c])
                        if l == 3:
                            if c == 0:
                                act.wait_ge(w2n_ok, e + 1)
                            kw["scale"] = s1_now[:, side, c:c + 1]
                        act.activation(hT[:, b, c * BANK:(c + 1) * BANK], bank(c, 0, BANK), func, **kw).then_inc(h_ok, 1)

                act.preload_act_table(func)
                hidden(0, 0, 0)
                hidden(0, 0, 1)
                if l == 2:
                    gating(l)
                    act.preload_act_table(func)
                hidden(1, 1, 0)
                if l != 2:
                    gating(l)
                hidden(1, 1, 1)
                with act.Fori(0, n // 2 - 1) as i:
                    for side in range(2):
                        for b in range(B):
                            hidden(i * 2 + (side + 2), side, b)
                if l == 2:
                    for b in range(B):
                        hidden(n, 0, b)
                act.preload_act_table(ACT.Exp)

            def norms3():
                held_in(act, 4)
                block_done(act, 7)
                act.activation(M["gv"][0:8, :], w("m3_gate_v"), ACT.Square, accum_out=small[0:8, 0, 32:33]).then_inc(n_gv, 1)
                act.wait_ge(n_gvT, 1)
                act.activation(M["gwT"], bank(7, 0, 8), ACT.Copy).then_inc(n_gv, 1)

            def norm_rows3():
                for n in range(2):
                    act.wait_ge(n_row, n + 1)
                    act.activation(M["s2"][:, n * BANK:(n + 1) * BANK], bank(4 + n, 0, BANK), ACT.Copy).then_inc(n_s2, 1)

            def experts0():
                def activate(e, side, i):
                    act.wait_ge(d_H, e + 1)
                    act.wait_ge(w0_in[side], i * 16 + 16)
                    for c in range(4):
                        last = act.activation(D["h"][:, side % 2 * BANK + c * P:side % 2 * BANK + (c + 1) * P],
                                              bank(2 + side % 2, c * P, (c + 1) * P), ACT.Gelu,
                                              bias=W0[side][:, 1024 + c:1025 + c])
                    last.then_inc(d_h, 1)

                act.preload_act_table(ACT.Gelu)
                run_queues(act, (activate, 0))
                act.preload_act_table(ACT.Exp)

            act.preload_act_table(ACT.Exp)
            for l in range(4):
                xattn(l)
                if l == 1:
                    two_token()
                elif l == 3:
                    norms3()
                    moe_input(l)
                    norm_rows3()
                else:
                    selfattn(l // 2)
                    moe_input(l)
                if l:
                    experts(l)
                else:
                    gating(l)
                    experts0()

        @block.vector
        def _(dve):
            step = Steps(dve, dve_step)
            dve.sem_inc(upT_dve, LEAD)
            dve.sem_inc(h2_ok, 4)
            dve.sem_inc(acc_ok, 2)
            dve.sem_inc(ctx_ok, 2)
            dve.sem_inc(d_xe, 2)
            dve.sem_inc(rk_ok, 4)
            dve.sem_inc(x_done, 2)
            dve.sem_inc(n_max, 2)
            dve.sem_inc(d_y, 2)
            for side in range(4):
                dve.sem_inc(d_stored[side], 16)
            dve.memset(r_res[:, :], 0.0).then_inc(zeros_set, 1)
            dve.memset(vx[:, 0:B * HS * 32], 0.0).then_inc(vx_zero, 1)
            dve.memset(spread_q[:, :, :], 0.0)
            dve.memset(spread_k[:, :, :], 0.0).then_inc(spread_zero, 1)

            def mask_term():
                dve.wait_ge(in_mask, 16)
                step.then(dve.tensor_copy(mask_add, mask_i[:, :, :].rearrange("p b n -> p (b n)")))
                step.then(dve.tensor_scalar(mask_add, mask_add, 1.0, -FMIN, ALU.subtract, ALU.mult))

            def carry(j):
                dve.memset(small[:, j, 63:64], 0.0)

            def moments(src, done, rms=False, eps=EPS_LN):
                for t in range(NT):
                    last = dve.bn_stats(stats[:, t, :], src[:, t * P:(t + 1) * P])
                step.then(last)
                for t in range(NT):
                    last = dve.bn_aggr(mv[:, t, :], stats[:, t, :])
                step.then(last)
                mean, v, out_ = mv[:, :, 0:1], mv[:, :, 1:2], var[:, 0, 0:NT].unsqueeze(2)
                if rms:
                    step.then(dve.tensor_tensor(out_, mean, mean, ALU.mult))
                    step.then(dve.tensor_tensor(out_, out_, v, ALU.add))
                    v = out_
                dve.tensor_scalar(out_, v, eps, None, ALU.add).then_inc(done, 1)

            def scaled(dst, src, rms=False, done=None):
                for t in range(NT):
                    a = slice(t * P, (t + 1) * P)
                    if rms:
                        last = dve.tensor_scalar(dst[:, a], src[:, a], rstd[:, 0, t:t + 1], None, ALU.mult)
                    else:
                        last = dve.tensor_scalar(dst[:, a], src[:, a], mv[:, t, 0:1], rstd[:, 0, t:t + 1],
                                                 ALU.subtract, ALU.mult)
                    if done is not None and t % TB == TB - 1:
                        last.then_inc(done, 1)
                if done is None:
                    step.then(last)

            def wide(v, n=TB):
                return v.unsqueeze(1).broadcast_to([P, n, P])

            def tiles(v):
                return v.rearrange("p (t d) -> p t d", d=P)

            def by_head(v):
                return v.rearrange("p (h d) -> p h d", d=64)

            def centre_weights():
                held_in(dve, 3)
                for v in (by_head(w("x2_wq")), by_head(w("x2_wk"))):
                    step.then(dve.tensor_reduce(small[:, 1, 0:16], v, AX_X, ALU.add))
                    step.then(dve.tensor_scalar(small[:, 1, 16:32], small[:, 1, 0:16], 1.0 / 64, None, ALU.mult))
                    step.then(dve.tensor_tensor(v, v, small[:, 1, 16:32].unsqueeze(2).broadcast_to([P, 16, 64]),
                                                ALU.subtract))
                dve.memset(small[:, 1, 63:64], 0.0).then_inc(centred, 1)

            def heads_var(rows, j, squares, sm, done):
                step.then(dve.tensor_reduce(sm[0:rows, j, 32:48], squares, AX_X, ALU.add))
                dve.tensor_scalar(var[0:rows, j, :], sm[0:rows, j, 32:48], 1.0 / 64, EPS_LN, ALU.mult, ALU.add)\
                   .then_inc(done, 1)

            def key_variances():
                for b in range(B):
                    dve.wait_ge(ksq_ok, b + 1)
                    heads_var(KV, 1 + b, by_head(O[0:KV, b, :]), small, kvar_ok)

            def keys(l):
                L = XATTN[l]
                G, NH, dh = L["G"], L["H"], L["dh"]
                K = kbd[:, 0:B * NH * KV].rearrange("p (b h k) -> p b h k", b=B, k=KV)
                if L["qk_norm"]:
                    dve.wait_ge(kT_ps, 1)
                    for n in range(3):
                        cols = min(3, G - 3 * n) * 2 * KV
                        last = dve.tensor_scalar(kaff[:, n * 462:n * 462 + cols], bank(n, 0, cols),
                                                 w("kn_w"), w("kn_b"), ALU.mult, ALU.add)
                    step.then(last)
                else:
                    dve.wait_ge(kv_ps, l + 1)
                for h in range(NH):
                    g = h * dh // P
                    src = kaff[:, g * 154:g * 154 + 154] if L["qk_norm"] else bank(g // 3, g % 3 * 154, g % 3 * 154 + 154)
                    own = w("headmask", h, h + 1) if dh == DS else w("halfmask", h % 2, h % 2 + 1)
                    last = dve.tensor_scalar(K[:, :, h, :], src.rearrange("p (b k) -> p b k", b=B), own, None, ALU.mult)
                if l:
                    V = vx[:, 0:B * NH * (dh + 1)].rearrange("p (n d) -> p n d", d=dh + 1)
                    last = dve.memset(V[:, :, dh:dh + 1], 1.0)
                last.then_inc(k_ok, 1)

            def xattn(l):
                L = XATTN[l]
                G, NH, dh = L["G"], L["H"], L["dh"]
                nb = NH // 4
                block_done(dve, 2 * l)
                held_in(dve, [0, 2, 3, 4][l])
                moments(x_res, x_stat)
                if l == 2:
                    for b in range(B):
                        dve.wait_ge(krstd_ok, b + 1)
                        dve.tensor_tensor(by_head(kn[0:KV, b, :]), by_head(psum[0:KV, 2 * b * BANK:(2 * b + 2) * BANK]),
                                          rstd[0:KV, 1 + b, :].unsqueeze(2).broadcast_to([KV, 16, 64]), ALU.mult)\
                           .then_inc(kn_ok, 1)
                dve.wait_ge(x_rstd, l + 1)
                scaled(xn_all, x_res, done=x_xn)
                if l != 1:
                    keys(l)
                if l == 0:
                    mask_term()
                if L["qk_norm"]:
                    def variance(n):
                        dve.wait_ge(qsq_ok, n + 1)
                        heads_var(P, n % 4, by_head(qsq4[:, n % 4, :]), small, qvar_ok)

                    dve.wait_ge(x_xTp, 2 * l + 2)
                    variance(0)
                    for n in range(NT):
                        if n + 1 < NT:
                            variance(n + 1)
                        dve.wait_ge(qrstd_ok, n + 1)
                        first = 2 * (n % 3)
                        dve.tensor_tensor(by_head(qn4[:, n % 4, :]), by_head(psum[:, first * BANK:(first + 2) * BANK]),
                                          rstd[:, n % 4, :].unsqueeze(2).broadcast_to([P, 16, 64]), ALU.mult)\
                           .then_inc(qn_ok, 1)
                else:
                    for n in range(1, B * G, 2):
                        dve.wait_ge(q_ps, QB[l] + n + 1)
                        dve.tensor_copy(qT_all[:, n * S:(n + 1) * S], bank((6 + n) % 8, 0, BANK)).then_inc(q_dve, 1)
                nh, nbp = NH // PARTS[l], nb // PARTS[l]
                with dve.Fori(0, TB) as i:
                    step.loop(i, [18, 10, 10, 10][l])
                    for c, j, part in chains(l):
                        dve.wait_ge(sc_ps, unit(l, i, c) + 8)
                        first = 4 * j + part * nbp
                        raw = psum[:, first * BANK:(first + nbp) * BANK].rearrange("p (c n) -> p c n", n=BANK)[:, :, 0:4 * KV]
                        e = E[:, j, part * nh * KV:(part + 1) * nh * KV]
                        top = small[:, c, 0:nh]
                        if L["mask"]:
                            step.then(dve.scalar_tensor_tensor(
                                e.rearrange("p (c n) -> p c n", c=nbp), raw, dh ** -0.5,
                                ext[:, j, :].unsqueeze(1).broadcast_to([P, nbp, 4 * KV]), ALU.mult, ALU.add))
                            eh = e.rearrange("p (h k) -> p h k", k=KV)
                            step.then(dve.tensor_reduce(top, eh, AX_X, ALU.max))
                            dve.tensor_tensor(eh, eh, top.unsqueeze(2).broadcast_to([P, nh, KV]), ALU.subtract)\
                               .then_inc(e_ok, 1)
                        else:
                            rawh = raw.rearrange("p c (h k) -> p c h k", k=KV)
                            toph = top.rearrange("p (c h) -> p c h", c=nbp)
                            step.then(dve.tensor_reduce(toph, rawh, AX_X, ALU.max))
                            dve.tensor_tensor(e.rearrange("p (c h k) -> p c h k", c=nbp, k=KV), rawh,
                                              toph.unsqueeze(3).broadcast_to([P, nbp, 4, KV]), ALU.subtract)\
                               .then_inc(e_ok, 1)
                    for c, j, part in chains(l):
                        if l != 1 or part == 1:
                            dve.wait_ge(pT_ps, unit(l, i, c))
                            n = max(1, nbp // 2)
                            lo = (part + 1) * nbp - n
                            dve.tensor_copy(PT[0:KV, j, lo * BANK:(lo + n) * BANK],
                                            psum[0:KV, (4 * j + lo) * BANK:(4 * j + lo + n) * BANK]).then_inc(pT_dve, 1)
                    if l == 0:
                        for c, j, part in chains(l):
                            dve.wait_ge(p_ok, unit(l, i, c))
                            e = E[:, j, part * nh * KV:(part + 1) * nh * KV].rearrange("p (h k) -> p h k", k=KV)
                            step.then(dve.tensor_reduce(small[:, c, 16:16 + nh], e, AX_X, ALU.add))
                            step.then(dve.reciprocal(small[:, c, 32:32 + nh], small[:, c, 16:16 + nh]))
                            dve.tensor_copy(O[:, j, part * 64:(part + 1) * 64].rearrange("p (h d) -> p h d", d=dh),
                                            small[:, c, 32:32 + nh].unsqueeze(2).broadcast_to([P, nh, dh])).then_inc(o_ok, 1)
                        for at, j, part in out_chains(l):
                            dve.wait_ge(oT_ps, at(i))
                            step.then(dve.tensor_copy(O[:, j, P:2 * P], bank(4 * j + 1, 0, P)))
                            dve.wait_ge(o_ps, unit(l, i, j * PARTS[l] + part))
                            dve.tensor_tensor(OT[:, j, 0:P], bank(4 * j, 0, P), O[:, j, P:2 * P], ALU.mult).then_inc(oT_ok, 1)
                    for c, j, part in chains(l) if l else ():
                        dve.wait_ge(o_ps, unit(l, i, c))
                        first = 4 * j + part * nbp
                        raw = psum[:, first * BANK:(first + nbp) * BANK].rearrange("p (c n) -> p c n", n=BANK)
                        raw = raw[:, :, 0:4 * (dh + 1)].rearrange("p c (h d) -> p c h d", d=dh + 1)
                        inv = small[:, c, 16:16 + nh].rearrange("p (c h) -> p c h", c=nbp)
                        step.then(dve.reciprocal(inv.unsqueeze(3), raw[:, :, :, dh:dh + 1]))
                        n = G * P // PARTS[l]
                        dve.tensor_tensor(O[:, j, part * n:(part + 1) * n].rearrange("p (c h d) -> p c h d", c=nbp, d=dh),
                                          raw[:, :, :, 0:dh], inv.unsqueeze(3).broadcast_to([P, nbp, 4, dh]), ALU.mult)\
                           .then_inc(o_ok, 1)
                    for j in range(B):
                        dve.wait_ge(y_ps, count(8 * l, i, j))
                        t = x_res[:, tile(i, j)]
                        last = dve.tensor_tensor(t, t, bank(4 * j + YBANK[l], 0, P), ALU.add)
                        if L["bias"]:
                            step.then(last)
                            last = dve.tensor_tensor(t, t, w(f"x{l}_bo"), ALU.add)
                        last.then_inc(x_done, 1)
                    if l == 3:
                        for side in range(2):
                            dve.wait_ge(n_ps, i * 2 + (side + 3))
                            raw = bank(4 * side + 3, 0, 5)
                            dve.tensor_scalar(s1_all[:, bass.ds(i * 8 + side * 4, 4)], raw[:, 0:4], 1e-24, None, ALU.max)
                            dve.tensor_scalar(s2_col[:, bass.ds(i * 2 + side, 1)], raw[:, 4:5], 1e-24, None, ALU.max)\
                               .then_inc(n_max, 1)
                step.end(TB)
                dve.wait_ge(x_done, 2 + NT * (l + 1))

            def selfattn(u):
                l = 2 * u
                held_in(dve, [1, 3][u])
                if u == 0:
                    dve.wait_ge(zeros_out, 16 * (SLOTS // 1024))
                moments(x_res, a_stat)
                dve.wait_ge(a_rstd, l + 1)
                scaled(r_res, x_res)
                moments(r_res, b_stat, rms=(u == 1), eps=[EPS_LN, 1e-6][u])
                dve.wait_ge(b_rstd, u + 1)
                scaled(xn_self, r_res, rms=(u == 1), done=b_xn)
                for b in range(B):
                    dve.wait_ge(qkv_ps, QKV[l] + b + 1)
                    a = slice(b * S, (b + 1) * S)
                    qp, kp, vp = (bank(2 + 3 * b + n, 0, BANK) for n in range(3))
                    if u == 0:
                        dve.tensor_scalar(q_all[:, a], qp, w("s0_q_b"), DS ** -0.5, ALU.add, ALU.mult)
                        dve.tensor_scalar(k_all[:, a], kp, w("s0_k_b"), None, ALU.add)
                        last = dve.tensor_tensor(tiles(v_all[:, a]), tiles(vp), wide(w("s0_v_b")), ALU.add)
                    else:
                        dve.tensor_scalar(q_all[:, a], qp, DS ** -0.5, None, ALU.mult)
                        dve.tensor_copy(k_all[:, a], kp)
                        last = dve.tensor_copy(v_all[:, a], vp)
                step.then(last)
                for b in range(B):
                    pair = [(x[:, b * S:(b + 1) * S], parts[:, :, b * S:(b + 1) * S])
                            for x, parts in ((k_all, k_parts), (q_all, q_parts))]
                    for n in range(3):
                        for x_, parts in pair:
                            last = dve.tensor_copy(parts[:, n, :], x_)
                        if n == 2:
                            last.then_inc(split_ok, 1)
                            continue
                        step.then(last)
                        for x_, parts in pair:
                            last = dve.tensor_tensor(x_, x_, parts[:, n, :], ALU.subtract)
                        step.then(last)
                    with dve.Fori(0, HS // 4) as i:
                        for k in range(4):
                            dve.wait_ge(rk_ps, i * 4 + ((u * B + b) * HS + k + 1))
                            dve.tensor_scalar(k_rep[:, bass.ds(i * (4 * B * S) + (k * B * S + b * S), S)],
                                              bank(2 * k, 0, BANK, ROWS), 1.0, None, ALU.mult).then_inc(rk_ok, 1)
                dve.wait_ge(split_ok, B * (u + 1))
                step.then(dve.memset(v_wide, 0.0))

                def widen(b):
                    wide = v_wide.rearrange("p (n r c) -> p n r c", r=4, c=32)
                    now = v_all[:, bass.ds(b * S, S)].rearrange("p (n r d) -> p n r d", r=4, d=DS)
                    for n in range(4):
                        last = dve.tensor_copy(wide[:, :, n, DS * n:DS * n + DS], now[:, :, n, :])
                    last.then_inc(v_wide_ok, 1)

                def invert(o, par):
                    dve.wait_ge(up_ok, o * HS + (LEAD + u * UNITS + HS))
                    dve.reciprocal(small[:, 3, 0:HS], small[:, 1 + par, 0:HS]).then_inc(inv_ok, 1)
                    dve.wait_ge(inv_ok, o * 2 + (2 * NT * u + 1))
                    dve.tensor_copy(inv_wide.rearrange("p (h d) -> p h d", d=DS),
                                    small[:, 3, 0:HS].unsqueeze(2).broadcast_to([P, HS, DS])).then_inc(inv_ok, 1)

                def normalise(o, par):
                    dve.wait_ge(r_ps, o + (NT * u + 1))
                    carry(3)
                    dve.tensor_copy(inv_turned, bank(6 + par, P, 2 * P)).then_inc(invT_ok, 1)
                    dve.wait_ge(invT_ok, o + (NT * u + 1))
                    dve.tensor_tensor(ctxT_all[:, bass.ds(o * P, P)], bank(6 + par, 0, P), inv_turned,
                                      ALU.mult).then_inc(ctx_ok, 1)

                with dve.Fori(0, B) as b:
                    widen(b)
                    for n in range(BU + 2):
                        qt, h = divmod(n, HS)
                        first = b * BU + (u * UNITS + n)
                        if n < BU:
                            dve.wait_ge(us_ps, first + (LEAD + 1))
                            dve.tensor_reduce(small[:, 0, h:h + 1], bank(h % 4, 0, keys_seen(u, qt)), AX_X, ALU.max,
                                              negate=True).then_inc(um_ok, 1)
                        g = n - 2
                        if g > 0 and g % 2:
                            W = keys_seen(u, g // HS)
                            dve.wait_ge(upT_ps, first + (LEAD - 1))
                            dve.wait_ge(uo_ps, first + (LEAD - 5))
                            dve.tensor_copy(ptself[:, (g % 4) * BANK:(g % 4) * BANK + W], bank(5, 0, W)).then_inc(upT_dve, 1)
                        if 0 < qt < TB:
                            if h == INVERT:
                                invert(b * TB + (qt - 1), (qt - 1) % 2)
                            if h == FINISH:
                                normalise(b * TB + (qt - 1), (qt - 1) % 2)
                    invert(b * TB + (TB - 1), (TB - 1) % 2)
                    normalise(b * TB + (TB - 1), (TB - 1) % 2)

            def experts_input(l, src, rms=False):
                dve.wait_ge(m_rstd, l + 1)
                if l == 1:
                    scaled(src, src)
                    step.then(dve.tensor_tensor(tiles(src[:, :]), tiles(src[:, :]), wide(w("h_g1"), NT), ALU.mult))
                    for b in range(B):
                        a = src[:, b * S:(b + 1) * S]
                        dve.tensor_tensor(tiles(a), tiles(a), wide(w("h_be1")), ALU.add).then_inc(m_xn, 1)
                else:
                    scaled(xn_moe, src, rms=rms, done=m_xn)
                E_ = MOE[l]["E"]
                dve.wait_ge(lg_ps, l + 1)
                src = bank(XT[l] + 2, 0, NT * E_)
                if l == 3:
                    dve.tensor_tensor(logits[:, 0:NT * E_].rearrange("p (t e) -> p t e", e=E_),
                                      src.rearrange("p (t e) -> p t e", e=E_),
                                      w("m3_gate_b").unsqueeze(1).broadcast_to([P, NT, E_]), ALU.add).then_inc(lg_ok, 1)
                else:
                    dve.tensor_copy(logits[:, 0:NT * E_], src).then_inc(lg_ok, 1)

            def moe_input(l):
                held_in(dve, [1, 2, 3, 4][l])
                if l == 3:
                    moments(x_res, m_stat)
                    norms3()
                    experts_input(l, x_res)
                    return
                for b in range(B):
                    r_, x_ = (v[:, b * S:(b + 1) * S] for v in (r_res, x_res))
                    dve.wait_ge(t_y, 2 * l + b + 1)
                    step.then(dve.tensor_tensor(r_, r_, bank(b, 0, BANK), ALU.add))
                    if l == 0:
                        step.then(dve.tensor_tensor(tiles(r_), tiles(r_), wide(w("s0_o_b")), ALU.add))
                    step.then(dve.tensor_tensor(x_, x_, r_, ALU.add))
                moments(r_res, m_stat, rms=(l == 2), eps=[EPS_LN, 0, 1e-6][l])
                experts_input(l, r_res, rms=(l == 2))

            def two_token():
                held_in(dve, 2)
                sc = H["sc"]
                heads = lambda v: v.rearrange("p (n d) -> p n d", d=32)
                qkv = H["qkv"].rearrange("p (b t n) -> p b t n", b=B, t=TB)
                prod = H["prod"].rearrange("p (q k n) -> p q k n", q=B, k=B)
                moments(x_res, a_stat)
                dve.wait_ge(a_rstd, 2)
                scaled(r_res, x_res, done=h0_ok)
                for b in range(B):
                    dve.wait_ge(qkv_ps, QKV[1] + (b + 1) * TB)
                    raw = psum[:, b * TB * BANK:(b + 1) * TB * BANK].rearrange("p (t n) -> p t n", n=BANK)[:, :, 0:384]
                    last = dve.tensor_tensor(qkv[:, b], raw, w("h_bqkv").unsqueeze(1).broadcast_to([P, TB, 384]), ALU.add)
                step.then(last)
                for j in range(B):
                    for k in range(B):
                        last = dve.tensor_tensor(tiles(prod[:, j, k]), qkv[:, j, :, 0:P], qkv[:, k, :, P:2 * P], ALU.mult)
                step.then(last)
                step.then(dve.tensor_reduce(sc[:, 0:64], heads(H["prod"]), AX_X, ALU.add))
                s4 = sc[:, 0:64].rearrange("p (q k n) -> p q k n", q=2, k=2)
                top = sc[:, 64:96].rearrange("p (q n) -> p q n", q=2)
                step.then(dve.tensor_tensor(top, s4[:, :, 0, :], s4[:, :, 1, :], ALU.max))
                dve.tensor_tensor(s4, s4, top.unsqueeze(2).broadcast_to([P, 2, 2, 16]), ALU.subtract).then_inc(t1_e, 1)
                dve.wait_ge(t1_p, 1)
                step.then(dve.tensor_tensor(top, s4[:, :, 0, :], s4[:, :, 1, :], ALU.add))
                step.then(dve.reciprocal(top, top))
                step.then(dve.tensor_tensor(s4, s4, top.unsqueeze(2).broadcast_to([P, 2, 2, 16]), ALU.mult))
                for j in range(B):
                    for k in range(B):
                        p4 = prod[:, j, k].rearrange("p (t h d) -> p t h d", t=TB, d=32)
                        last = dve.tensor_tensor(p4, qkv[:, k, :, 2 * P:3 * P].rearrange("p t (h d) -> p t h d", d=32),
                                                 s4[:, j, k, :].rearrange("p (t h) -> p t h", t=TB).unsqueeze(3)
                                                 .broadcast_to([P, TB, 4, 32]), ALU.mult)
                    step.then(last)
                    dve.tensor_tensor(H["cc"][:, j * S:(j + 1) * S], prod[:, j, 0], prod[:, j, 1], ALU.add).then_inc(t1_av, 1)
                for b in range(B):
                    r_ = r_res[:, b * S:(b + 1) * S]
                    dve.wait_ge(t_y, 2 + b + 1)
                    step.then(dve.tensor_tensor(r_, r_, bank(2 + b, 0, BANK), ALU.add))
                    step.then(dve.tensor_tensor(tiles(r_), tiles(r_), wide(w("h_bo")), ALU.add))
                moments(r_res, m_stat)
                experts_input(1, r_res)

            def norms3():
                dve.wait_ge(n_gv, 1)
                dve.tensor_scalar(small[0:8, 0, 33:34], small[0:8, 0, 32:33], 1e-24, None, ALU.max).then_inc(n_max, 1)
                dve.wait_ge(n_pow, 1)
                dve.tensor_scalar(M["gv"][0:8, :], w("m3_gate_v"), small[0:8, 0, 33:34], None, ALU.mult).then_inc(n_pow, 1)

            def norm_rows3():
                dve.wait_ge(n_ok, 1)
                for n in range(2):
                    for e in range(4 * n, 4 * n + 4):
                        last = dve.tensor_scalar(M["diag"][:, e * P:(e + 1) * P], w("ident"), s2_col[:, e:e + 1], None, ALU.mult)
                    last.then_inc(n_diag, 1)

            def top_mask(dst, src, n, shape):
                bc = lambda v: v.unsqueeze(2).broadcast_to(shape)
                best = small[:, 0, 0:NT] if n == 0 else small[:, 0, 8:16]
                first = small[:, 0, 16:24]
                step.then(dve.tensor_reduce(best, src, AX_X, ALU.max))
                step.then(dve.tensor_tensor(dst, src, bc(best), ALU.is_equal))
                step.then(dve.tensor_tensor(dst, dst, w("firstness", 0, shape[2]).unsqueeze(1).broadcast_to(shape), ALU.mult))
                step.then(dve.tensor_reduce(first, dst, AX_X, ALU.max))
                step.then(dve.tensor_tensor(dst, dst, bc(first), ALU.is_equal))

            def gating(l):
                E_ = MOE[l]["E"]
                shape = [P, NT, E_]
                n = NT * E_
                bc = lambda v: v.unsqueeze(2).broadcast_to(shape)
                t3 = lambda v: v[:, 0:n].rearrange("p (t e) -> p t e", e=E_)
                LG, ga, gb, gc = t3(logits), t3(M["ga"]), t3(M["gb"]), t3(M["gc"])
                G_ = gates[:, :, 0:E_]
                total = small[:, 0, 24:32]
                dve.wait_ge(lg_ok, l + 1)
                if l == 1:
                    top_mask(ga, LG, 0, shape)
                    dve.tensor_copy(G_, ga).then_inc(gate_ok, 1)
                elif l == 3:
                    top_mask(ga, LG, 0, shape)
                    step.then(dve.scalar_tensor_tensor(M["gc"][:, 0:n], M["ga"][:, 0:n], FMIN, logits[:, 0:n], ALU.mult, ALU.add))
                    top_mask(gb, gc, 1, shape)
                    dve.tensor_tensor(G_, ga, gb, ALU.add).then_inc(gate_ok, 1)
                else:
                    m1, m2 = (M["m12"][:, k * n:k * n + n] for k in range(2))
                    top_mask(t3(m1), LG, 0, shape)
                    step.then(dve.scalar_tensor_tensor(M["gc"][:, 0:n], m1, FMIN, logits[:, 0:n], ALU.mult, ALU.add))
                    top_mask(t3(m2), gc, 1, shape)
                    dve.tensor_tensor(gc, LG, bc(small[:, 0, 0:NT]), ALU.subtract).then_inc(g_sub, 1)
                    dve.wait_ge(g_exp, [1, 0, 2][l])
                    step.then(dve.tensor_reduce(total, gc, AX_X, ALU.add))
                    step.then(dve.reciprocal(total, total))
                    step.then(dve.tensor_tensor(gc, gc, bc(total), ALU.mult))
                if l == 0:
                    m12 = M["m12"].rearrange("p (k t e) -> p k t e", k=2, t=NT)
                    pre = M["pre"].rearrange("p (k t e) -> p k t e", k=2, t=NT)
                    step.then(dve.memset(pre[:, :, 0, :], 0.0))
                    for t in range(1, NT):
                        step.then(dve.tensor_tensor(pre[:, :, t, :], pre[:, :, t - 1, :], m12[:, :, t - 1, :], ALU.add))
                    dve.tensor_tensor(M["tot"], pre[:, 0, NT - 1, :], m12[:, 0, NT - 1, :], ALU.add).then_inc(g_m, 1)
                    dve.wait_ge(g_loc, 1)
                    step.then(dve.scalar_tensor_tensor(M["mk"], bank(0, 0, 2 * n), float(CAPACITY), M["m12"], ALU.is_le, ALU.mult))
                    q3 = lambda v: v.rearrange("p (n e) -> p n e", e=E_)
                    place, kept, to = (D["slot"][:, a:a + 16] for a in (0, 16, 32))
                    step.then(dve.tensor_tensor(q3(D["loc"]), q3(bank(0, 0, 2 * n)),
                                                w("queue").unsqueeze(1).broadcast_to([P, 2 * NT, E_]), ALU.add))
                    step.then(dve.tensor_tensor(D["loc"], D["loc"], M["mk"], ALU.mult))
                    step.then(dve.tensor_reduce(place, q3(D["loc"]), AX_X, ALU.add))
                    step.then(dve.tensor_reduce(kept, q3(M["mk"]), AX_X, ALU.add))
                    step.then(dve.tensor_scalar(to, kept, -float(DROPPED), float(DROPPED), ALU.mult, ALU.add))
                    step.then(dve.tensor_tensor(to, to, place, ALU.add))
                    dve.tensor_copy(slot_i[:, 16:32], place)
                    dve.tensor_copy(slot_i[:, 0:16], to).then_inc(slots_ok, 1)
                    step.then(dve.tensor_tensor(M["ga"], M["mk"][:, 0:n], M["mk"][:, n:2 * n], ALU.add))
                    step.then(dve.tensor_tensor(M["ga"], M["ga"], M["gc"], ALU.mult))
                    step.then(dve.tensor_reduce(total, ga, AX_X, ALU.add))
                    step.then(dve.tensor_scalar(total, total, float(np.finfo(np.float32).eps), None, ALU.max))
                    step.then(dve.reciprocal(total, total))
                    step.then(dve.tensor_scalar(total, total, 0.8, None, ALU.mult))
                    dve.tensor_tensor(G_, ga, bc(total), ALU.mult).then_inc(gate_ok, 1)
                    dve.wait_ge(gate_ok, 1)
                    mk4 = M["mk"].rearrange("p (k t e) -> p k t e", k=2, t=NT)
                    for k in range(2):
                        step.then(dve.tensor_tensor(mk4[:, k], mk4[:, k], G_, ALU.mult))
                    step.then(dve.tensor_reduce(D["slot"][:, 48:64], q3(M["mk"]), AX_X, ALU.add))
                if l == 2:
                    step.then(dve.tensor_reduce(small[:, 0, 0:NT], gc, AX_X, ALU.max))
                    dve.tensor_tensor(gc, gc, bc(small[:, 0, 0:NT]), ALU.subtract).then_inc(g_sub, 1)
                    dve.wait_ge(g_exp, 3)
                    step.then(dve.tensor_tensor(M["ga"][:, 0:n], m1, m2, ALU.add))
                    step.then(dve.tensor_tensor(ga, ga, gc, ALU.mult))
                    step.then(dve.tensor_reduce(total, ga, AX_X, ALU.add))
                    step.then(dve.reciprocal(total, total))
                    step.then(dve.tensor_tensor(G_, ga, bc(total), ALU.mult))
                    step.then(dve.memset(gates[:, :, E_:E_ + 1], 1.0))
                if l != 2:
                    acc = r_res if l == 1 else x_res
                    dve.wait_ge(b2_ps, [1, 2, 0, 3][l])
                    dve.wait_ge(gate_ok, [1, 2, 0, 3][l])
                    dve.tensor_tensor(acc[:, :], acc[:, :], psum[:, BB[l] * BANK:(BB[l] + 2) * BANK], ALU.add).then_inc(b2_ok, 1)
                    dve.wait_ge(b2_ok, [1, 2, 0, 3][l])

            def experts(l):
                acc = r_res if l == 1 else x_res
                gflat = M["gates"]

                def product(e, side, b):
                    if l != 2:
                        return
                    for c in range(2):
                        dve.wait_ge(sg_ok, e * 4 + (2 + 2 * b + c + 1))
                        dve.wait_ge(h_ps, e * 8 + (HPB[l] + 4 * b + 2 + c + 1))
                        if c == 0:
                            dve.wait_ge(ye_ps, e * 2 + (2 + KB[l] + b - 1))
                        dve.tensor_tensor(hT[:, b, c * BANK:(c + 1) * BANK], sg[:, b, c * BANK:(c + 1) * BANK],
                                          bank(2 + c, 0, BANK), ALU.mult).then_inc(h2_ok, 1)

                def gather(e, side, b):
                    dve.wait_ge(ye_ps, e * 2 + (2 + KB[l] + b + 1))
                    dve.wait_ge(acc_ok, e * 2 + (2 + KB[l] + b - 1))
                    for t in range(TB):
                        a = acc[:, b * S + t * P:b * S + t * P + P]
                        last = dve.scalar_tensor_tensor(a, bank(4 + b, t * P, t * P + P),
                                                        gflat[:, bass.ds(e + (b * TB + t) * 16, 1)], a, ALU.mult, ALU.add)
                    last.then_inc(acc_ok, 1)

                def gates_ready(late):
                    if not late:
                        gating(l)
                        if l == 1:
                            centre_weights()

                expert_order(dve, l, product, gather, gates_ready)
                dve.wait_ge(acc_ok, 2 + KB[l + 1])

            def experts0():
                def features(e, side, i):
                    dve.wait_ge(d_T, e + 1)
                    dve.tensor_scalar(D["xe"][:, side % 2 * P:(side % 2 + 1) * P], bank(side % 2, 0, P),
                                      w("s0_ln2_w"), w("s0_ln2_b"), ALU.mult, ALU.add).then_inc(d_xe, 1)

                def answer(e, side, i):
                    dve.wait_ge(d_O, e + 1)
                    dve.wait_ge(d_stored[side], i * 16 + 16)
                    dve.tensor_copy(D["y"][:, side * P:(side + 1) * P], bank(4 + side % 2, 0, P)).then_inc(d_y, 1)

                run_queues(dve, (features, 2), (answer, 0))
                keys(1)
                for n in range(2 * NT):
                    if n % 4 == 0:
                        dve.wait_ge(d_back[n // 4], 16 * 4)
                    a = x_res[:, n % NT * P:(n % NT + 1) * P]
                    last = dve.scalar_tensor_tensor(a, D["back"][:, n * P:(n + 1) * P], D["slot"][:, 48 + n:49 + n], a,
                                                    ALU.mult, ALU.add)
                    if n == NT - 1:
                        step.then(last)
                last.then_inc(d_done, 1)
                dve.wait_ge(d_done, 1)

            def last_norm():
                moments(r_res, f_stat)
                key_variances()
                dve.wait_ge(f_rstd, 1)
                scaled(r_res, r_res)
                step.then(dve.tensor_tensor(tiles(r_res[:, :]), tiles(r_res[:, :]), wide(w("h_g2"), NT), ALU.mult))
                step.then(dve.tensor_tensor(tiles(r_res[:, :]), tiles(r_res[:, :]), wide(w("h_be2"), NT), ALU.add))
                dve.tensor_tensor(x_res[:, :], x_res[:, :], r_res[:, :], ALU.add).then_inc(f_done, 1)
                dve.wait_ge(f_done, 1)

            for l in range(4):
                xattn(l)
                if l == 1:
                    two_token()
                elif l == 3:
                    moe_input(l)
                    norm_rows3()
                else:
                    selfattn(l // 2)
                    moe_input(l)
                if l:
                    experts(l)
                else:
                    gating(l)
                    experts0()
                if l == 1:
                    last_norm()

        @block.tensor
        def _(pe):
            pe.sem_inc(us_ps, LEAD)
            pe.sem_inc(sc_ps, 8)
            pe.sem_inc(upT_ps, LEAD)
            pe.sem_inc(uo_ps, LEAD)
            pe.sem_inc(ye_ps, 2)
            pe.sem_inc(n_ps, 2)
            ident = w("ident")
            mm, turn = pe.matmul, pe.transpose

            def keys_values(l):
                L = XATTN[l]
                G, NH, dh = L["G"], L["H"], L["dh"]
                wk, wv, cT = (w(n) for n in (f"x{l}_wk", f"x{l}_wv", "ctxT"))
                held_in(pe, [0, 2, 3, 4][l])
                if l == 1:
                    pe.wait_ge(d_h, 2 + E0)
                    pe.wait_ge(d_y, 2 + E0)
                elif l:
                    pe.wait_ge(acc_ok, 2 + KB[l])
                if l == 2:
                    pe.wait_ge(centred, 1)
                for b in range(B):
                    for n in range(max(1, NH * dh // BANK)):
                        cols = min(BANK, NH * dh)
                        mm(bank(4 + 2 * b + n, 0, cols, KV), cT[:, b * KV:(b + 1) * KV],
                           wv[:, n * BANK:n * BANK + cols], start=True, stop=True)
                if L["qk_norm"]:
                    for b in range(B):
                        for n in range(2):
                            last = mm(bank(2 * b + n, 0, BANK, KV), cT[:, b * KV:(b + 1) * KV],
                                      wk[:, n * BANK:(n + 1) * BANK], start=True, stop=True)
                else:
                    for g in range(G):
                        last = mm(bank(g // 3, g % 3 * 154, g % 3 * 154 + 154), wk[:, g * P:(g + 1) * P], cT,
                                  start=True, stop=True)
                last.then_inc(kv_ps, 1)

            def xattn(l):
                L = XATTN[l]
                G, NH, dh = L["G"], L["H"], L["dh"]
                wq, wo = w(f"x{l}_wq"), w(f"x{l}_wo")
                keys_values(l)
                if L["qk_norm"]:
                    pe.wait_ge(kn_ok, B)
                    for g in range(G):
                        for b in range(B):
                            a = g % 3 * 154 + b * KV
                            last = turn(bank(g // 3, a, a + KV), kn[0:KV, b, g * P:(g + 1) * P], ident[0:KV, 0:KV])
                    last.then_inc(kT_ps, 1)
                pe.wait_ge(v_ok, l + 1)
                K = kbd[:, 0:B * NH * KV].rearrange("p (b n) -> p b n", b=B)
                V = vx[:, 0:B * NH * (dh + 1)].rearrange("p (b h d) -> p b h d", b=B, d=dh + 1)
                for b in range(B):
                    pe.wait_ge(x_xn, 2 * l + b + 1)
                    for t in range(TB):
                        last = turn(bank(4 + b, t * P, (t + 1) * P), xn_all[:, b * S + t * P:b * S + (t + 1) * P], ident)
                    last.then_inc(x_xTp, 1)
                if L["qk_norm"]:
                    pe.wait_ge(x_xT, 2 * l + 2)
                    pe.wait_ge(k_ok, l + 1)

                    def queries(n):
                        if n >= 3:
                            pe.wait_ge(qn_ok, n - 2)
                        for k in range(2):
                            last = mm(bank(2 * (n % 3) + k, 0, BANK), xT_all[:, n * P:(n + 1) * P],
                                      wq[:, k * BANK:(k + 1) * BANK], start=True, stop=True)
                        last.then_inc(q_nat, 1)

                    for n in range(3):
                        queries(n)
                    for n in range(NT):
                        pe.wait_ge(qn_ok, n + 1)
                        if n:
                            pe.wait_ge(qT_ok, n)
                        for g in range(G):
                            last = turn(psum[:, 6 * BANK + g * P:6 * BANK + (g + 1) * P], qn4[:, n % 4, g * P:(g + 1) * P], ident)
                        last.then_inc(qnT_ps, 1)
                        if n + 3 < NT:
                            queries(n + 3)
                    pe.wait_ge(qT_ok, NT)
                else:
                    for n in range(B * G):
                        b, g = n // G, n % G
                        pe.wait_ge(x_xT, 2 * l + (1 if n < min(G, 6) else 2))
                        if n == 2:
                            pe.wait_ge(k_ok, l + 1)
                        if n >= 8:
                            pe.wait_ge(q_dve if n % 2 else q_act, QB[l] // 2 + (n - 8) // 2 + 1)
                        mm(bank((6 + n) % 8, 0, BANK), wq[:, g * P:(g + 1) * P], xT_all[:, b * S:(b + 1) * S],
                           start=True, stop=True).then_inc(q_ps, 1)
                    pe.wait_ge(q_act, QB[l] // 2 + G)
                    pe.wait_ge(q_dve, QB[l] // 2 + G)
                pe.wait_ge(k_ok, l + 1)
                nh, nbp, gp = NH // PARTS[l], NH // 4 // PARTS[l], max(1, G // PARTS[l])
                with pe.Fori(0, TB) as i:
                    for c, j, part in chains(l):
                        if part == 0:
                            pe.wait_ge(xq_ok, count(8 * l, i, j))
                            pe.wait_ge(x_done, count(8 * l, i, j))
                            if l == 3:
                                pe.wait_ge(n_max, count(0, i, j))
                        if G == 1:
                            for n in range(part * nbp, (part + 1) * nbp):
                                last = mm(bank(4 * j + n, 0, 4 * KV), qcur2[:, j, 0:P], K[:, j, n * 4 * KV:(n + 1) * 4 * KV],
                                          start=True, stop=True)
                        else:
                            for g in range(part * gp, (part + 1) * gp):
                                last = mm(bank(4 * j + g // 2, g % 2 * 154, g % 2 * 154 + 154), qcur2[:, j, g * P:(g + 1) * P],
                                          K[:, j, g * 154:(g + 1) * 154], start=True, stop=True)
                        last.then_inc(sc_ps, 1)
                    for c, j, part in chains(l):
                        pe.wait_ge(p_ok, unit(l, i, c))
                        for h in range(part * nh, (part + 1) * nh):
                            a = 4 * j * BANK + h * P
                            last = turn(psum[0:KV, a:a + P], E[:, j, h * KV:(h + 1) * KV], ident)
                        last.then_inc(pT_ps, 1)
                    for c, j, part in chains(l):
                        by_act, by_dve = turned_by(l, i, j, part)
                        if by_act is not None:
                            pe.wait_ge(pT_act, by_act)
                        if by_dve is not None:
                            pe.wait_ge(pT_dve, by_dve)
                        for h in range(part * nh, (part + 1) * nh):
                            if l == 0:
                                a = h // 4 * 32
                                last = mm(psum[a:a + 32, 4 * j * BANK:4 * j * BANK + P],
                                          vx[:, (j * NH + h) * 32:(j * NH + h + 1) * 32], PT[0:KV, j, h * P:(h + 1) * P],
                                          start=(h % 4 == 0), stop=(h % 4 == 3), skip_group_check=True)
                                continue
                            a = h % 4 * (dh + 1)
                            last = mm(bank(4 * j + h // 4, a, a + dh + 1), PT[0:KV, j, h * P:(h + 1) * P], V[:, j, h, :],
                                      start=True, stop=True)
                        last.then_inc(o_ps, 1)
                    for _, j, part in out_chains(l):
                        pe.wait_ge(o_ok, unit(l, i, j * PARTS[l] + part))
                        if G == 1:
                            turn(bank(4 * j + 1, 0, P), O[:, j, 0:P], ident).then_inc(oT_ps, 1)
                            continue
                        for g in range(gp):
                            a = (4 * j + part * nbp) * BANK + g * P
                            n = part * gp + g
                            last = turn(psum[:, a:a + P], O[:, j, n * P:(n + 1) * P], ident)
                        last.then_inc(oT_ps, 1)
                    for at, j, part in out_chains(l):
                        pe.wait_ge(oT_ok, at(i))
                        for g in range(G) if G == 1 else range(part * gp, (part + 1) * gp):
                            last = mm(bank(4 * j + YBANK[l], 0, P), OT[:, j, g * P:(g + 1) * P], wo[:, g * P:(g + 1) * P],
                                      start=(g == 0), stop=(g == G - 1))
                        if part == PARTS[l] - 1:
                            last.then_inc(y_ps, 1)
                    if l == 3:
                        for side in range(2):
                            pe.wait_ge(n_sq, i * 2 + (side + 1))
                            for c in range(8):
                                at_ = min(c, 4)
                                last = mm(bank(4 * side + 3, at_, at_ + 1), sq[:, side, c * P:(c + 1) * P],
                                          w("ones", 0, 1), start=(c <= 4), stop=(c < 4 or c == 7))
                            last.then_inc(n_ps, 1)

            def turn_tiles(bank_, src, b, done):
                for t in range(TB):
                    last = turn(bank(bank_, t * P, (t + 1) * P), src[:, b * S + t * P:b * S + (t + 1) * P], ident)
                last.then_inc(done, 1)

            def selfattn(u):
                l = 2 * u
                held_in(pe, [1, 3][u])
                wq, wk, wv = (w(f"s{l}_{n}_w") for n in "qkv")
                for b in range(B):
                    pe.wait_ge(b_xn, B * u + b + 1)
                    turn_tiles(b, xn_self, b, s_xTp)
                for b in range(B):
                    pe.wait_ge(s_xT, 2 * l + b + 1)
                    mine = xT_self[:, b * S:(b + 1) * S]
                    for n, wn in enumerate((wq, wk)):
                        mm(bank(2 + 3 * b + n, 0, BANK), wn, mine, start=True, stop=True)
                    for t in range(TB):
                        last = mm(bank(4 + 3 * b, t * P, (t + 1) * P), mine[:, t * P:(t + 1) * P], wv, start=True, stop=True)
                    last.then_inc(qkv_ps, 1)
                pe.wait_ge(const_ok, 1)
                flat_q, flat_k = (v[:, :, :].rearrange("p h n -> p (h n)") for v in (spread_q, spread_k))
                for b in range(B):
                    pe.wait_ge(split_ok, B * u + b + 1)
                    with pe.Fori(0, HS // 4) as i:
                        for k in range(4):
                            pe.wait_ge(rk_ok, i * 4 + ((u * B + b) * HS + k + 1))
                            for n in range(3):
                                onto = flat_k[:, bass.ds(i * 448 + (k * 112 + 16 - 8 * n), ROWS)]
                                last = mm(bank(2 * k, 0, BANK, ROWS), onto,
                                          k_parts[:, n, b * S:(b + 1) * S], start=(n == 0), stop=(n == 2))
                            last.then_inc(rk_ps, 1)
                            pe.wait_ge(rq_ok, i * 4 + ((u * B + b) * HS + k + 1))
                            for n in range(3):
                                onto = flat_q[:, bass.ds(i * 640 + (k * 160 + 64 - 32 * n), ROWS)]
                                last = mm(bank(2 * k + 1, 0, BANK, ROWS), onto,
                                          q_parts[:, n, b * S:(b + 1) * S], start=(n == 0), stop=(n == 2))
                            last.then_inc(rq_ps, 1)
                pe.wait_ge(rk_ok, LEAD + B * HS * (u + 1))
                pe.wait_ge(rq_ok, LEAD + B * HS * (u + 1))
                base = u * UNITS
                def turn_inverse(o, par):
                    pe.wait_ge(inv_ok, o * 2 + (2 * NT * u + 2))
                    turn(bank(6 + par, P, 2 * P), inv_wide, ident).then_inc(r_ps, 1)

                with pe.Fori(0, B) as b:
                    for n in range(BU + 4):
                        first = b * BU + (base + n)
                        pairs = b * (BU // 2) + base // 2
                        if n < BU:
                            qt, h = divmod(n, HS)
                            W = keys_seen(u, qt)
                            pe.wait_ge(up_ok, first + (LEAD - 3))
                            last = mm(bank(h % 4, 0, W), q_rep[:, bass.ds(b * S + (qt * P + h * B * S), P)],
                                      k_rep[:, bass.ds(b * S + h * B * S, W)], start=True, stop=True)
                            if u == 0:
                                last = mm(bank(h % 4, W - P, W), ident_bf[:, :], later_bf[:, :], start=False, stop=True,
                                          skip_group_check=True)
                            last.then_inc(us_ps, 1)
                        g = n - 2
                        if 0 <= g < BU:
                            pe.wait_ge(up_ok, first + (LEAD - 1))
                            pe.wait_ge(upT_dve if g % 2 else upT_act, pairs + (LEAD + g // 2))
                            for k in range(keys_seen(u, g // HS) // P):
                                last = turn(bank(4 + g % 2, k * P, k * P + P),
                                            pself[:, (g % 4) * BANK + k * P:(g % 4) * BANK + k * P + P], ident)
                            last.then_inc(upT_ps, 1)
                        g = n - 4
                        if g >= 0:
                            qt, h = divmod(g, HS)
                            chunks = keys_seen(u, qt) // P
                            pe.wait_ge(upT_dve if g % 2 else upT_act, pairs + (LEAD + g // 2 + 1))
                            if h == 0:
                                pe.wait_ge(v_wide_ok, b + (B * u + 1))
                                pe.wait_ge(ctx_ok, b * TB + (qt + NT * u + 1))
                            for k in range(chunks):
                                a = h // 4 * 32
                                last = mm(psum[a:a + 32, (6 + qt % 2) * BANK:(6 + qt % 2) * BANK + P],
                                          v_wide[:, k * BANK + h * 32:k * BANK + h * 32 + 32],
                                          ptself[:, (h % 4) * BANK + k * P:(h % 4) * BANK + k * P + P],
                                          start=(h % 4 == 0 and k == 0), stop=(h % 4 == 3 and k == chunks - 1),
                                          skip_group_check=True)
                            last.then_inc(uo_ps, 1)
                        qt, h = divmod(n, HS)
                        if 0 < qt < TB and h == TURN:
                            turn_inverse(b * TB + (qt - 1), (qt - 1) % 2)
                    turn_inverse(b * TB + (TB - 1), (TB - 1) % 2)

            def project(l, first, src, weights):
                for t in range(NT):
                    last = mm(bank(first + t // TB, t % TB * P, (t % TB + 1) * P), src[:, t * P:(t + 1) * P], weights,
                              start=True, stop=True)
                    if t % TB == TB - 1:
                        last.then_inc(t_y, 1)

            def experts_input(l, src):
                for b in range(B):
                    pe.wait_ge(m_xn, 2 * l + b + 1)
                    turn_tiles(XT[l] + b, src, b, m_xTp)
                E_ = MOE[l]["E"]
                router_w = M["gwT"] if l == 3 else w(f"m{l}_router")
                for t in range(NT):
                    pe.wait_ge(m_xT, 2 * l + t // TB + 1)
                    last = mm(bank(XT[l] + 2, t * E_, (t + 1) * E_), xT_all[:, t * P:(t + 1) * P], router_w,
                              start=True, stop=True)
                last.then_inc(lg_ps, 1)

            def moe_input(l):
                held_in(pe, [1, 2, 3, 4][l])
                if l != 3:
                    pe.wait_ge(ctx_ok, 2 + NT * (l // 2 + 1))
                    project(l, 0, ctxT_all, w(f"s{l}_o_w"))
                experts_input(l, xn_moe)

            def two_token():
                held_in(pe, 2)
                for b in range(B):
                    pe.wait_ge(h0_ok, b + 1)
                    turn_tiles(b, r_res, b, s_xTp)
                pe.wait_ge(s_xT, 2 + B)
                for t in range(NT):
                    mm(bank(t, 0, 384), xT_all[:, t * P:(t + 1) * P], w("h_wqkv"), start=True, stop=True).then_inc(qkv_ps, 1)
                for b in range(B):
                    pe.wait_ge(t1_av, b + 1)
                    turn_tiles(b, H["cc"], b, t_ccT)
                pe.wait_ge(t_ccS, B)
                project(1, 2, xT_all, w("h_wo"))
                experts_input(1, r_res)

            def norms3():
                held_in(pe, 4)
                pe.wait_ge(n_pow, 2)
                turn(bank(7, 0, 8), M["gv"][0:8, :], ident[0:8, 0:8]).then_inc(n_gvT, 1)
                pe.wait_ge(n_gv, 2)

            def norm_rows3():
                for n in range(2):
                    pe.wait_ge(n_diag, n + 1)
                    mm(bank(4 + n, 0, BANK), w("ones"), M["diag"][:, n * BANK:(n + 1) * BANK],
                       start=True, stop=True).then_inc(n_row, 1)

            def gating(l):
                E_ = MOE[l]["E"]
                if l == 0:
                    pe.wait_ge(g_m, 1)
                    mm(bank(0, 0, 256), w("before"), M["m12"], start=True, stop=True)
                    mm(bank(0, 0, 256), w("ones"), M["pre"], start=False, stop=True, skip_group_check=True)
                    mm(bank(0, P, 256), w("ones"), M["tot"].unsqueeze(1).broadcast_to([P, NT, E_]),
                       start=False, stop=True, skip_group_check=True).then_inc(g_loc, 1)
                if l != 2:
                    n = [1, 2, 0, 3][l]
                    pe.wait_ge(gate_ok, n)
                    for t in range(NT):
                        last = turn(psum[0:E_, GB[l] * BANK + t * P:GB[l] * BANK + (t + 1) * P], gates[:, t, 0:E_], ident)
                    last.then_inc(gT_ps, 1)
                    pe.wait_ge(gT_ok, n)
                    for t in range(NT):
                        last = mm(psum[:, BB[l] * BANK + t * P:BB[l] * BANK + (t + 1) * P], gatesT[0:E_, t * P:(t + 1) * P],
                                  w(f"m{l}_b2"), start=True, stop=True)
                    last.then_inc(b2_ps, 1)
                    if l == 0:
                        pe.wait_ge(b2_ok, n)

            def experts(l):
                m = MOE[l]
                C = m["C"]

                def hidden(e, side, b):
                    if b == 0:
                        pe.wait_ge(w_in[side], load_count(l, e, side))
                    for c in range(4):
                        if l != 2:
                            pe.wait_ge(h_ok, e * 8 + (HB[l] + 4 * b + c + 1))
                        elif c < 2:
                            pe.wait_ge(sg_ok, e * 4 + (2 * b + c + 1))
                        else:
                            pe.wait_ge(h2_ok, e * 4 + (2 * b + c - 2 + 3))
                        mm(bank(c, 0, BANK), wexp[:, side, c * P:(c + 1) * P], xT_all[:, b * S:(b + 1) * S],
                           start=True, stop=True).then_inc(h_ps, 1)

                def output(e, side, b):
                    if l == 2:
                        pe.wait_ge(h2_ok, e * 4 + (4 + 2 * b + 2))
                    else:
                        pe.wait_ge(h_ok, e * 8 + (4 + HB[l] + 4 * b + 4))
                    pe.wait_ge(acc_ok, e * 2 + (KB[l] + b + 1))
                    if l == 3:
                        pe.wait_ge(w2n_ok, e + 1)
                    for t in range(TB):
                        for c in range(C):
                            down = w2n[:, side, c * P:(c + 1) * P] if l == 3 else wexp[:, side, BANK + c * P:BANK + (c + 1) * P]
                            last = mm(bank(4 + b, t * P, (t + 1) * P), hT[:, b, c * BANK + t * P:c * BANK + (t + 1) * P], down,
                                      start=(c == 0), stop=(c == C - 1))
                    last.then_inc(ye_ps, 1)

                pe.wait_ge(m_xT, 2 * (l + 1))
                pe.wait_ge(lg_ok, l + 1)
                expert_order(pe, l, hidden, output, lambda late: gating(l) if late else None)

            def experts0():
                def turned(e, side, i):
                    pe.wait_ge(d_in[side], i * 16 + 16)
                    pe.wait_ge(d_xe, e + 1)
                    turn(bank(side % 2, 0, P), D["xin"][:, side * P:(side + 1) * P], ident).then_inc(d_T, 1)

                def hidden(e, side, i):
                    pe.wait_ge(w0_in[side], i * 16 + 16)
                    pe.wait_ge(d_xe, e + 3)
                    pe.wait_ge(d_h, e + 1)
                    for c in range(4):
                        last = mm(bank(2 + side % 2, c * P, (c + 1) * P), W0[side][:, c * P:(c + 1) * P],
                                  D["xe"][:, side % 2 * P:(side % 2 + 1) * P], start=True, stop=True)
                    last.then_inc(d_H, 1)

                def output(e, side, i):
                    pe.wait_ge(d_h, e + 3)
                    pe.wait_ge(d_y, e + 1)
                    for c in range(4):
                        last = mm(bank(4 + side % 2, 0, P), D["h"][:, side % 2 * BANK + c * P:side % 2 * BANK + (c + 1) * P],
                                  W0[side][:, BANK + c * P:BANK + (c + 1) * P], start=(c == 0), stop=(c == 3))
                    last.then_inc(d_O, 1)

                run_queues(pe, (turned, 2), (hidden, 1), (output, 0))

            for l in range(4):
                xattn(l)
                if l == 1:
                    two_token()
                elif l == 3:
                    norms3()
                    moe_input(l)
                    norm_rows3()
                else:
                    selfattn(l // 2)
                    moe_input(l)
                if l:
                    experts(l)
                else:
                    gating(l)
                    experts0()


def kernel(**inputs):
    import concourse.bacc as bacc
    from concourse.bass_utils import run_bass_kernel_spmd

    inp = {k: np.asarray(v) for k, v in inputs.items()}
    blocks = layout(inp)
    at, first = {}, 0
    for name, block in blocks.items():
        at[name] = (first, block.shape[0], block.shape[1])
        first += block.shape[1]
    packed = np.zeros((P, first), np.float32)
    for name, block in blocks.items():
        a, rows, cols = at[name]
        packed[0:rows, a:a + cols] = block
    mask = np.ascontiguousarray(np.broadcast_to(np.tile(inp["mask_BxS2_ik0"], (1, 4)), (P, B, 4 * KV)))
    arrays = {"x": np.ascontiguousarray(inp["x"].reshape(B * S, P)), "mask": mask, "packed": packed}
    for l, e in enumerate(expert_layout(inp)):
        arrays[f"experts{l}"] = np.ascontiguousarray(e)

    nc = bacc.Bacc("TRN2", target_bir_lowering=False, num_devices=1)
    ap = {n: nc.dram_tensor(n, a.shape, mybir.dt.from_np(a.dtype), kind="ExternalInput").ap() for n, a in arrays.items()}
    out = nc.dram_tensor("out", (B * S, P), F32, kind="ExternalOutput").ap()
    queued, answers = (nc.dram_tensor(n, (SLOTS, P), F32, kind="Internal").ap() for n in ("queued", "answers"))
    program(nc, ap["x"], ap["mask"], ap["packed"], [ap[f"experts{l}"] for l in range(4)], out, queued, answers, at)
    r = run_bass_kernel_spmd(nc, [arrays], core_ids=[0])
    return r.results[0]["out"].reshape(B, S, P)
```
